# Optimizing a Trainium2 kernel written in Bass

```python
import numpy as np
import jax
import jax.numpy as jnp

def _softmax(x, axis=-1):
    return jax.nn.softmax(x, axis=axis)

def _gelu(x):
    return jax.nn.gelu(x, approximate=True)

def _silu(x):
    return jax.nn.silu(x)

def _sigmoid(x):
    return jax.nn.sigmoid(x)

def _layernorm(x, axis=-1, eps=1e-05):
    m = jnp.mean(x, axis=axis, keepdims=True)
    v = jnp.var(x, axis=axis, keepdims=True)
    return (x - m) / jnp.sqrt(v + eps)

def _scatter_add(tgt, idx, src, axis=0):
    return tgt.at[idx].add(src)

def _segment_sum(src, seg, n):
    return jax.ops.segment_sum(src, seg, n)
kernel_name = 'mk_prb_d1_jaxref_r4_3f738c'

def setup_inputs(seed: int=0):
    np.random.seed(seed)
    _w = jnp.asarray

    def _L0_attn_setup():
        import jax, jax.numpy as jnp
        import numpy as np
        HIDDEN = 1024
        N_HEADS = 32
        N_KV_HEADS = 8
        HEAD_DIM = HIDDEN // N_HEADS
        N_REP = N_HEADS // N_KV_HEADS
        KV_DIM = N_KV_HEADS * HEAD_DIM

        def _kaiming_uniform(key, out_f, in_f):
            bound = 1.0 / np.sqrt(in_f)
            return jax.random.uniform(key, (out_f, in_f), jnp.float32, -bound, bound)

        def bitnet_linear(x, weight, scale_param):
            s = jnp.maximum(jnp.mean(jnp.abs(weight), axis=1), 1e-08)
            binary_w = jnp.sign(weight / s[:, None])
            y = jnp.einsum('bsi,oi->bso', x, binary_w)
            y = y * (s * scale_param)[None, None, :]
            return jnp.nan_to_num(y, nan=0.0, posinf=1000000.0, neginf=-1000000.0)
        key = jax.random.key(seed)
        ks = jax.random.split(key, 5)
        return {'hidden_states': jax.random.normal(ks[0], (1, 512, HIDDEN), jnp.float32), 'q_weight': _kaiming_uniform(ks[1], HIDDEN, HIDDEN), 'q_scale': jnp.ones((HIDDEN,), jnp.float32), 'k_weight': _kaiming_uniform(ks[2], KV_DIM, HIDDEN), 'k_scale': jnp.ones((KV_DIM,), jnp.float32), 'v_weight': _kaiming_uniform(ks[3], KV_DIM, HIDDEN), 'v_scale': jnp.ones((KV_DIM,), jnp.float32), 'o_weight': _kaiming_uniform(ks[4], HIDDEN, HIDDEN), 'o_scale': jnp.ones((HIDDEN,), jnp.float32)}
    _L0_attn_in = _L0_attn_setup()

    def _L0_ffn_setup():
        import jax, jax.numpy as jnp
        import numpy as np
        GROUP_SIZE = 128

        def dequantize(imatrix, scales, zeros, group_size, out_dtype):
            rs = jnp.repeat(scales, group_size, axis=0)
            rz = jnp.repeat(zeros, group_size, axis=0)
            return ((imatrix.astype(rs.dtype) - rz.astype(rs.dtype)) * rs).astype(out_dtype)
        key = jax.random.key(seed)
        ks = jax.random.split(key, 10)
        H, I, G = (1024, 3584, GROUP_SIZE)
        B, S = (4, 512)
        x = jax.random.normal(ks[0], (B, S, H), dtype=jnp.float32)
        gate_w = jax.random.randint(ks[1], (H, I), 0, 16, dtype=jnp.int32)
        gate_z = jax.random.randint(ks[2], (H // G, I), 0, 16, dtype=jnp.int32)
        gate_s = jax.random.uniform(ks[3], (H // G, I), dtype=jnp.float32) * 0.01
        up_w = jax.random.randint(ks[4], (H, I), 0, 16, dtype=jnp.int32)
        up_z = jax.random.randint(ks[5], (H // G, I), 0, 16, dtype=jnp.int32)
        up_s = jax.random.uniform(ks[6], (H // G, I), dtype=jnp.float32) * 0.01
        down_w = jax.random.randint(ks[7], (I, H), 0, 16, dtype=jnp.int32)
        down_z = jax.random.randint(ks[8], (I // G, H), 0, 16, dtype=jnp.int32)
        down_s = jax.random.uniform(ks[9], (I // G, H), dtype=jnp.float32) * 0.01
        return {'x': x, 'gate_w': gate_w, 'gate_z': gate_z, 'gate_s': gate_s, 'up_w': up_w, 'up_z': up_z, 'up_s': up_s, 'down_w': down_w, 'down_z': down_z, 'down_s': down_s}
    _L0_ffn_in = _L0_ffn_setup()
    _d = {'L0_attn_hidden_states': _L0_attn_in['hidden_states'], 'L0_attn_q_weight': _L0_attn_in['q_weight'], 'L0_attn_q_scale': _L0_attn_in['q_scale'], 'L0_attn_k_weight': _L0_attn_in['k_weight'], 'L0_attn_k_scale': _L0_attn_in['k_scale'], 'L0_attn_v_weight': _L0_attn_in['v_weight'], 'L0_attn_v_scale': _L0_attn_in['v_scale'], 'L0_attn_o_weight': _L0_attn_in['o_weight'], 'L0_attn_o_scale': _L0_attn_in['o_scale'], 'L0_ffn_gate_w': _L0_ffn_in['gate_w'], 'L0_ffn_gate_z': _L0_ffn_in['gate_z'], 'L0_ffn_gate_s': _L0_ffn_in['gate_s'], 'L0_ffn_up_w': _L0_ffn_in['up_w'], 'L0_ffn_up_z': _L0_ffn_in['up_z'], 'L0_ffn_up_s': _L0_ffn_in['up_s'], 'L0_ffn_down_w': _L0_ffn_in['down_w'], 'L0_ffn_down_z': _L0_ffn_in['down_z'], 'L0_ffn_down_s': _L0_ffn_in['down_s']}
    _x0 = _d['L0_attn_hidden_states']
    _d['L0_attn_hidden_states'] = jax.random.normal(jax.random.fold_in(jax.random.key(seed), 1), (2, 1024, 1024), dtype=_x0.dtype)
    del _x0
    return _d

def reference(L0_attn_hidden_states, L0_attn_q_weight, L0_attn_q_scale, L0_attn_k_weight, L0_attn_k_scale, L0_attn_v_weight, L0_attn_v_scale, L0_attn_o_weight, L0_attn_o_scale, L0_ffn_gate_w, L0_ffn_gate_z, L0_ffn_gate_s, L0_ffn_up_w, L0_ffn_up_z, L0_ffn_up_s, L0_ffn_down_w, L0_ffn_down_z, L0_ffn_down_s):

    def _L0_attn_ref(hidden_states, q_weight, q_scale, k_weight, k_scale, v_weight, v_scale, o_weight, o_scale):
        import jax, jax.numpy as jnp
        import numpy as np
        HIDDEN = 1024
        N_HEADS = 32
        N_KV_HEADS = 8
        HEAD_DIM = HIDDEN // N_HEADS
        N_REP = N_HEADS // N_KV_HEADS
        KV_DIM = N_KV_HEADS * HEAD_DIM

        def _kaiming_uniform(key, out_f, in_f):
            bound = 1.0 / np.sqrt(in_f)
            return jax.random.uniform(key, (out_f, in_f), jnp.float32, -bound, bound)

        def bitnet_linear(x, weight, scale_param):
            s = jnp.maximum(jnp.mean(jnp.abs(weight), axis=1), 1e-08)
            binary_w = jnp.sign(weight / s[:, None])
            y = jnp.einsum('bsi,oi->bso', x, binary_w)
            y = y * (s * scale_param)[None, None, :]
            return jnp.nan_to_num(y, nan=0.0, posinf=1000000.0, neginf=-1000000.0)
        b, s, _ = hidden_states.shape
        q = bitnet_linear(hidden_states, q_weight, q_scale)
        k = bitnet_linear(hidden_states, k_weight, k_scale)
        v = bitnet_linear(hidden_states, v_weight, v_scale)
        q = q.reshape(b, s, N_HEADS, HEAD_DIM).transpose(0, 2, 1, 3)
        k = k.reshape(b, s, N_KV_HEADS, HEAD_DIM).transpose(0, 2, 1, 3)
        v = v.reshape(b, s, N_KV_HEADS, HEAD_DIM).transpose(0, 2, 1, 3)
        k = jnp.repeat(k, N_REP, axis=1)
        v = jnp.repeat(v, N_REP, axis=1)
        scores = jnp.einsum('bhqd,bhkd->bhqk', q, k) / np.sqrt(HEAD_DIM)
        attn = jax.nn.softmax(scores, axis=-1)
        out = jnp.einsum('bhqk,bhkd->bhqd', attn, v)
        out = out.transpose(0, 2, 1, 3).reshape(b, s, HIDDEN)
        return bitnet_linear(out, o_weight, o_scale)

    def _L0_ffn_ref(x, gate_w, gate_z, gate_s, up_w, up_z, up_s, down_w, down_z, down_s):
        import jax, jax.numpy as jnp
        import numpy as np
        GROUP_SIZE = 128

        def dequantize(imatrix, scales, zeros, group_size, out_dtype):
            rs = jnp.repeat(scales, group_size, axis=0)
            rz = jnp.repeat(zeros, group_size, axis=0)
            return ((imatrix.astype(rs.dtype) - rz.astype(rs.dtype)) * rs).astype(out_dtype)
        dt = x.dtype
        gate_proj = dequantize(gate_w, gate_s, gate_z, GROUP_SIZE, dt)
        up_proj = dequantize(up_w, up_s, up_z, GROUP_SIZE, dt)
        down_proj = dequantize(down_w, down_s, down_z, GROUP_SIZE, dt)
        gate = jax.nn.silu(jnp.dot(x, gate_proj))
        up = jnp.dot(x, up_proj)
        return jnp.dot(gate * up, down_proj)
    x = L0_attn_hidden_states
    xn = _layernorm(x, axis=-1)
    x = x + _L0_attn_ref(xn, L0_attn_q_weight, L0_attn_q_scale, L0_attn_k_weight, L0_attn_k_scale, L0_attn_v_weight, L0_attn_v_scale, L0_attn_o_weight, L0_attn_o_scale) + _L0_ffn_ref(xn, L0_ffn_gate_w, L0_ffn_gate_z, L0_ffn_gate_s, L0_ffn_up_w, L0_ffn_up_z, L0_ffn_up_s, L0_ffn_down_w, L0_ffn_down_z, L0_ffn_down_s)
    return x

_drawn_inputs = setup_inputs


def setup_inputs(seed=0):
    import zlib

    import numpy as np

    out = dict(_drawn_inputs(seed))
    spreads = {'L0_attn_q_scale': (1.0, 0.6),
     'L0_attn_k_scale': (1.0, 0.6),
     'L0_attn_v_scale': (1.0, 0.6),
     'L0_attn_o_scale': (1.0, 0.6)}
    factors = {'L0_attn_q_weight': 8.0,
     'L0_attn_k_weight': 8.0,
     'L0_attn_v_weight': 8.0,
     'L0_attn_o_weight': 8.0}
    for name, (base, spread) in spreads.items():
        noise = np.random.default_rng([zlib.crc32(name.encode()), seed]).standard_normal(out[name].shape)
        drawn = base * np.exp(spread * noise) if base else spread * noise
        out[name] = jnp.asarray(drawn.astype(out[name].dtype))
    for name, factor in factors.items():
        out[name] = (out[name] * factor).astype(out[name].dtype)
    return out
```

```python
import concourse.bass as bass
from concourse import mybir
from contextlib import ExitStack


P = 128
T, H = 2048, 1024
S = 1024
KT = H // P
I = 3584
IT = I // P
PAIRS = IT // 2
D = 32
FQ, FK = 8, 2
NC = T // 512
NX = T // P
EPS = 1e-5
FMAX = 3.4028234663852886e38
XS = 256.0
QB = 4096.0
MU = 16384.0
HEADS_BODY, STEPS_BODY = 16, 128
LEAD_S = 14


RMAX = bass.bass_isa.ReduceOp.max


class Tally:

    def __init__(self, sem):
        self.sem, self.base, self.n = sem, 0, 0

    def inc(self, ins):
        self.n += 1
        return ins.then_inc(self.sem, 1)

    def value(self):
        return self.base + self.n

    def enter(self, start, i, per):
        self.base, self.n = start + i * per, 0

    def leave(self, total):
        self.base, self.n = 0, total


def layer_kernel(nc, x, wq, sq, wk, sk, wv, sv, wo, so, gw, gz, gs, uw, uz, us, dw, dz, ds, out, zscr):
    f32, f16, i32 = mybir.dt.float32, mybir.dt.float16, mybir.dt.int32
    ALU = mybir.AluOpType
    ACT = mybir.ActivationFunctionType
    AX = mybir.AxisListType.X
    add, sub, mult, amin, amax, iseq = ALU.add, ALU.subtract, ALU.mult, ALU.min, ALU.max, ALU.is_equal

    ctx = ExitStack()
    with ctx:
        def sb(name, shape, dt=f32):
            return ctx.enter_context(nc.sbuf_tensor(name, shape, dt))

        def sem(name):
            return ctx.enter_context(nc.semaphore(name))

        xT = sb("xT", [P, 2, KT, T], f16)
        zone_a = sb("zone_a", [P, 64 * 256])
        zone_b = sb("zone_b", [P, 75 * 256])

        def view(zone, kb, words, dt=f32):
            v = zone[:, kb * 256:kb * 256 + words]
            return v if dt == f32 else v.bitcast(dt)

        xs = view(zone_a, 0, 16384).rearrange("p (n c) -> p n c", n=NX)
        snat_g = view(zone_b, 0, 1024)[0:IT, :].rearrange("t (g c) -> t g c", g=KT)
        snat_u = view(zone_b, 4, 1024)[0:IT, :].rearrange("t (g c) -> t g c", g=KT)
        snat_d = view(zone_b, 8, 1024)[0:IT, :]
        znat = view(zone_b, 12, 3072, i32)[0:IT, :]
        zf16 = view(zone_b, 24, 1536, f16)[0:IT, :]
        bn = view(zone_b, 30, NX * 12).rearrange("p (n c) -> p n c", n=NX)
        wT = view(zone_b, 32, 6144, f16).rearrange("p (k c) -> p k c", k=KT)
        hst = view(zone_b, 56, 1024, f16).rearrange("p (n c) -> p n c", n=2)
        lst = view(zone_b, 60, 1024, f16).rearrange("p (n c) -> p n c", n=2)
        wraw = view(zone_b, 64, 2048).rearrange("p (n c) -> p n c", n=2)
        wsg = view(zone_b, 72, 512, f16)
        y2 = view(zone_b, 56, 1024).rearrange("p (n c) -> p n c", n=2)
        r2 = view(zone_b, 60, 1024).rearrange("p (n c) -> p n c", n=2)
        rv2 = view(zone_b, 64, 1024).rearrange("p (n c) -> p n c", n=2)
        fin = view(zone_b, 68, 512, i32)
        qz = view(zone_a, 0, 16384, f16).rearrange("p (g h c) -> p g h c", g=16, h=2)
        vz = view(zone_b, 0, 4096).rearrange("p (g k d) -> p g k d", g=16, k=8)
        kz = view(zone_b, 16, 4096, f16).rearrange("p (n h c) -> p n h c", n=4, h=2)
        qst = view(zone_b, 32, 2048, f16).rearrange("p (n c) -> p n c", n=4)
        kst = view(zone_b, 40, 1024, f16).rearrange("p (n c) -> p n c", n=2)
        vst = view(zone_b, 44, 1024).rearrange("p (n k d) -> p n k d", n=2, k=8)
        prob = view(zone_b, 48, 4096).rearrange("p (n c) -> p n c", n=4)
        ost = view(zone_b, 64, 1024, f16).rearrange("p (h c) -> p h c", h=2)
        rsum = view(zone_b, 68, 512)
        o32 = view(zone_b, 70, 512)
        mrow = view(zone_b, 72, 128, f16).rearrange("p (n c) -> p n c", n=2)
        acc = [view(zone_b, 0, 8192).rearrange("p (o c) -> p o c", o=FQ),
               view(zone_a, 0, 8192).rearrange("p (o c) -> p o c", o=FQ)]
        woT = view(zone_b, 32, 4096, f16).rearrange("p (k c) -> p k c", k=KT)
        yo2 = view(zone_b, 48, 1024).rearrange("p (n c) -> p n c", n=2)
        ro = view(zone_b, 52, 512)
        fino = view(zone_b, 54, 512, i32)
        woraw = view(zone_b, 56, 2048).rearrange("p (n c) -> p n c", n=2)
        wosg = view(zone_b, 64, 1024, f16).rearrange("p (n c) -> p n c", n=2)
        gu = view(zone_a, 32, 8192).rearrange("p (u m c) -> p u m c", u=2, m=2)
        tmp = view(zone_b, 32, 2048).rearrange("p (n c) -> p n c", n=4)
        hT = view(zone_b, 40, 4096, f16).rearrange("p (u h c) -> p u h c", u=2, h=2)
        wf = view(zone_b, 56, 3072, f16).rearrange("p (u m c) -> p u m c", u=2, m=3)
        wst = view(zone_b, 68, 1024, i32).rearrange("p (n c) -> p n c", n=2)
        zst = view(zone_b, 72, 512, f16).rearrange("p (n c) -> p n c", n=2)
        xin = view(zone_a, 32, 4096).rearrange("p (n c) -> p n c", n=4)
        fo = view(zone_a, 48, 4096).rearrange("p (n c) -> p n c", n=4)
        id32 = sb("id32", [P, P])
        id16 = sb("id16", [P, P], f16)
        tab = sb("tab", [P, IT, 17])
        dtab = sb("dtab", [P, IT, FQ])
        sm = sb("sm", [P, 286])

        def cols(a, n):
            return sm[:, a:a + n]

        ssum, spar, cc = cols(0, 20), cols(20, 20), cols(40, 20)
        mv = cols(60, 32).rearrange("p (n c) -> p n c", n=NX)
        ve, sd_, rs, t4 = cols(92, 4), cols(96, 4), cols(100, 4), cols(104, 4)
        fl, mark = cols(108, NX), cols(124, NX)
        cm, cmr, fac, gam = cols(140, 3), cols(143, 3), cols(146, 3), cols(149, 1)
        mxs = cols(150, 16).rearrange("p (n c) -> p n c", n=2)
        mhl = cols(166, 8).bitcast(f16)
        pmx, pmx2, pmr, pmr2 = (cols(174 + 28 * j, 28) for j in range(4))
        scl = sb("scl", [P, 2, 17])
        dscl = sb("dscl", [P, 2, FQ])

        ps = ctx.enter_context(nc.psum_tensor("ps", [P, 8, 512], f32))

        def bank16(b):
            return ps[:, b, :].bitcast(f16)

        names = """x_in w_in0 w_in1 par_in snat_in znat_in z_out ident sgn_done abs_done wT_pe wT_out
            stat_ok std_ok norm_ok xc_ok h_ok l_ok xh_pe xl_pe xh_out xl_out snat_pe tab_ok pmx_ok pmr_ok
            cm_ok cmr_ok fac_ok chain
            qkv_pe y_ok r_ok h2_ok lq_ok vr_ok v_pe v_out
            q_in0 q_in1 q_in2 q_in3 m_in0 m_in1 m_in2 m_in3 k_in0 k_in1 v_in0 v_in1 const_ok
            s_pe max_ok mhl_ok m_pe mrow_ok st_pe exp_ok pv_pe o_ok oh_ok ol_ok ost_out
            wo_in0 wo_in1 wosgn_ok woabs_ok woT_pe woT_out co_ok o_pe yo_ok ro_ok acc_ok
            p_in0 p_in1 sub_ok even_pe odd_pe act_ok pool_ok dve_ok sil_ok hp_ok hh_ok hl_ok scl0_in scl1_in dscl_in
            t_pe f_ok xr_in0 xr_in1 xr_in2 xr_in3 out_ok0 out_ok1 out_ok2 out_ok3""".split()
        s = {n: sem(n) for n in names}

        WSRC = [(wq, i * P) for i in range(FQ)] + [(wk, i * P) for i in range(FK)] + [(wv, i * P) for i in range(FK)]
        NW = len(WSRC)
        QKV = [10, 11] + list(range(10))
        GATE_UP = [(u, m, gp) for u in range(2) for m in range(2) for gp in range(4)]
        ROUNDS = [("gu",) + t for t in GATE_UP[:8]] + [("dn", ot, 0, 0) for ot in range(FQ)] \
            + [("gu",) + t for t in GATE_UP[8:]]

        def rounds(down, gateup):
            return [(r, t) for r, t in enumerate(ROUNDS) if (t[0] == "gu" and gateup) or (t[0] == "dn" and down)]

        def first_of(t):
            return t[0] == "gu" and t[3] == 0

        def on_pool(t, c):
            return not first_of(t) and not (t[0] == "gu" and c == 3)

        NPOOL_GU = sum(on_pool(t, c) for t in ROUNDS if t[0] == "gu" for c in range(NC))
        NPOOL_DN = sum(on_pool(t, c) for t in ROUNDS if t[0] == "dn" for c in range(NC))

        def target(t, c):
            if t[0] == "gu":
                return gu[:, t[1], t[2], c * 512:(c + 1) * 512]
            return acc[c // 2][:, t[1], (c % 2) * 512:(c % 2) * 512 + 512]

        def scale_col(t, odd):
            if t[0] == "gu":
                k = t[2] * KT + 2 * t[3] + odd
                return scl[:, t[1], k:k + 1]
            return dscl[:, odd, t[1]:t[1] + 1]

        block = ctx.enter_context(nc.Block())

        @block.sync
        def _(sp):
            w_sem = [s["w_in0"], s["w_in1"]]
            for i in range(NX):
                b, r0 = i // 8, (i % 8) * P
                sp.dma_start(xs[:, i, :], x[b, r0:r0 + P, :]).then_inc(s["x_in"], 16)
                if i < 2:
                    src, w0 = WSRC[i]
                    sp.dma_start(wraw[:, i, :], src[w0:w0 + P, :]).then_inc(w_sem[i], 16)
                if i % 4 == 3:
                    if i == 3:
                        for k, (v, n, c0) in enumerate(((sq, FQ, 0), (sk, FK, 8), (sv, FK, 10), (so, FQ, 12))):
                            sp.dma_start(spar[:, c0:c0 + n], v.rearrange("(t p) -> p t", p=P), allow_slow_non_contiguous=True).then_inc(s["par_in"], 16)
                        sp.dma_start(snat_g, gs.rearrange("g (t c) -> t g c", c=P)).then_inc(s["snat_in"], 16)
                        sp.dma_start(snat_u, us.rearrange("g (t c) -> t g c", c=P)).then_inc(s["snat_in"], 16)
                        sp.dma_start(snat_d, ds).then_inc(s["snat_in"], 16)
                        for m, zsrc in enumerate((gz, uz)):
                            sp.dma_start(znat[:, m * 1024:(m + 1) * 1024].rearrange("t (g c) -> t g c", g=KT),
                                         zsrc.rearrange("g (t c) -> t g c", c=P)).then_inc(s["znat_in"], 16)
                        sp.dma_start(znat[:, 2048:3072], dz).then_inc(s["znat_in"], 16)
                    sp.wait_ge(s["x_in"], 16 * (i + 1))
                    for j in range(3):
                        k = 2 + (i // 4) * 3 + j
                        if k < NW:
                            sp.wait_ge(s["sgn_done"], k - 1)
                            sp.wait_ge(s["abs_done"], k - 1)
                            src, w0 = WSRC[k]
                            sp.dma_start(wraw[:, k % 2, :], src[w0:w0 + P, :]).then_inc(w_sem[k % 2], 16)
            sp.wait_ge(s["tab_ok"], 1)
            sp.dma_start(zscr.rearrange("t m c -> t (m c)"), zf16).then_inc(s["z_out"], 16)

            def load_q(hd, g, buf):
                rows = slice(32 * (hd % 4), 32 * (hd % 4) + 32)
                for part, to in ((0, 0), (1, 32), (0, 64)):
                    sp.dma_start(qst[to:to + 32, buf, :], qz[rows, g, part, :]).then_inc(s[f"q_in{buf}"], 16)

            def load_kv(gi, it, g, buf):
                rows = slice(32 * gi, 32 * gi + 32)
                for part, to in ((0, 0), (0, 32), (1, 64)):
                    sp.dma_start(kst[to:to + 32, buf, :], kz[rows, it, part, :]).then_inc(s[f"k_in{buf}"], 16)
                sp.dma_start(vst[:, buf, :, 0:32], vz[:, g, :, :]).then_inc(s[f"v_in{buf}"], 16)

            def load_m(hd_n, buf, par):
                for part in range(2):
                    sp.dma_start(qst[96 + part:97 + part, buf, :].rearrange("a (q c) -> a q c", q=8),
                                 mrow[8 * part:8 * part + 8, par, :]).then_inc(s[f"m_in{buf}"], 16)

            sp.wait_ge(s["lq_ok"], 10 * NC + 1)
            sp.wait_ge(s["h2_ok"], 10 * NC)
            sp.wait_ge(s["v_out"], 2 * NC)
            sp.wait_ge(s["const_ok"], 2)
            load_kv(0, 0, 0, 0)
            for hd in range(4):
                load_q(hd, 0, hd)
            sp.wait_ge(s["mrow_ok"], 1)
            load_m(0, 0, 0)

            def sp_attention(it, last):
                for n in range(HEADS_BODY):
                    gi = n // 4
                    if not (last and n == 15):
                        sp.wait_ge(s["mrow_ok"], 16 * it + n + 2)
                        load_m(n + 1, (n + 1) % 4, (n + 1) % 2)
                    if n + 4 < 16 or not last:
                        sp.wait_ge(s["st_pe"], 128 * it + 8 * n + 8)
                        nx = n + 4
                        load_q(nx, (4 * it + nx // 4), nx % 4)
                    if n % 4 == 0 and not (last and gi == 3):
                        sp.wait_ge(s["pv_pe"], 128 * it + 32 * gi + 4)
                        ng = gi + 1
                        load_kv(ng % 4, it + ng // 4, 4 * it + ng, ng % 2)
                    if n % 4 == 3:
                        sp.wait_ge(s["ol_ok"], 32 * it + 2 * n + 2)
                        sp.dma_start(qz[:, 4 * it + gi, :, :], ost[:, :, :]).then_inc(s["ost_out"], 16)

            with sp.Fori(0, 3) as it:
                sp_attention(it, False)
            sp_attention(3, True)

            wo_sem = [s["wo_in0"], s["wo_in1"]]
            for i in range(FQ):
                if i >= 2:
                    sp.wait_ge(s["wosgn_ok"], i - 1)
                    sp.wait_ge(s["woabs_ok"], i - 1)
                else:
                    sp.wait_ge(s["pv_pe"], 512 + 4)
                    sp.wait_ge(s["ost_out"], 16 * 17)
                sp.dma_start(woraw[:, i % 2, :], wo[i * P:(i + 1) * P, :]).then_inc(wo_sem[i % 2], 16)

            def piece(k, t, m, j):
                sp_ring = k % 2
                if m < 2:
                    src = (gw, uw)[m].rearrange("(g p) i -> p g i", p=P)
                    src = src[:, 4 * j:4 * j + 4, bass.ts(t, P)]
                    dst = wst[:, sp_ring, :].rearrange("p (g c) -> p g c", g=4)
                else:
                    src = dw[bass.ts(t, P), j * 512:(j + 1) * 512]
                    dst = wst[:, sp_ring, :]
                sp.dma_start(dst, src).then_inc(s[f"p_in{sp_ring}"], 16)
                z = zscr[bass.ds(t, 1), m, j * 512:(j + 1) * 512]
                sp.dma_start(zst[:, sp_ring, :], z.rearrange("a c -> (a c)").partition_broadcast(P)
                             ).then_inc(s[f"p_in{sp_ring}"], 16)

            def scales(u, t):
                sp.dma_start(scl[:, u, :], tab[:, bass.ds(t, 1), :].rearrange("p a c -> p (a c)")
                             ).then_inc(s[f"scl{u}_in"], 16)

            def sp_ffn(k, first, last):
                base = 4 + 12 * k
                plan = [(2 * k + 1, m, j) for m in range(2) for j in range(2)]
                if not last:
                    plan += [(2 * k + 2, m, j) for m in range(2) for j in range(2)]
                plan += [(2 * k + u, 2, j) for u in range(2) for j in range(2)]
                for i, (t, m, j) in enumerate(plan):
                    if i == 2:
                        if not first:
                            sp.wait_ge(s["hl_ok"], 8 * k)
                        scales(1, 2 * k + 1)
                        if not first:
                            sp.dma_start(dscl[:, :, :], dtab[:, bass.ds(2 * k - 2, 2), :]).then_inc(s["dscl_in"], 16)
                    if i == len(plan) - 2 and not last:
                        sp.wait_ge(s["hl_ok"], 8 * k + 4)
                        scales(0, 2 * k + 2)
                    sp.wait_ge(s["sub_ok"], base + i - 1)
                    piece(i, t, m, j)

            sp.wait_ge(s["acc_ok"], 32 + 2)
            sp.wait_ge(s["z_out"], 16)
            for i, (m, j) in enumerate([(m, j) for m in range(2) for j in range(2)]):
                if i >= 2:
                    sp.wait_ge(s["sub_ok"], i - 1)
                piece(i, 0, m, j)
            scales(0, 0)
            sp_ffn(0, True, False)
            with sp.Fori(1, PAIRS - 1) as k:
                sp_ffn(k, False, False)
            sp_ffn(PAIRS - 1, False, True)
            sp.wait_ge(s["hl_ok"], 8 * PAIRS)
            sp.dma_start(dscl[:, :, :], dtab[:, IT - 2:IT, :]).then_inc(s["dscl_in"], 16)

            def rows_out(j):
                sp.wait_ge(s["f_ok"], j + 1)
                sp.dma_start(out[j // 8, (j % 8) * P:(j % 8) * P + P, :], fo[:, j % 4, :]).then_inc(s[f"out_ok{j % 4}"], 16)

            for i in range(NX):
                if i >= 4:
                    rows_out(i - 4)
                sp.dma_start(xin[:, i % 4, :], x[i // 8, (i % 8) * P:(i % 8) * P + P, :]).then_inc(s[f"xr_in{i % 4}"], 16)
            for j in range(NX - 4, NX):
                rows_out(j)
            for j in range(4):
                sp.wait_ge(s[f"out_ok{j}"], 16 * NX // 4)

        @block.gpsimd
        def _(pool):
            nc.gpsimd.memset(id32[:], 0.0).then_inc(s["ident"], 1)
            nc.gpsimd.memset(id16[:], 0.0).then_inc(s["ident"], 1)
            pool.wait_ge(s["ident"], 2)
            for m in (id32, id16):
                nc.gpsimd.affine_select(out=m[:], in_=m[:], compare_op=ALU.not_equal, fill=1.0, base=0,
                                        pattern=[[-1, P]], channel_multiplier=1).then_inc(s["ident"], 1)
            for i in range(NX):
                pool.wait_ge(s["norm_ok"], i + 1)
                nc.gpsimd.tensor_scalar(xs[:, i, :], xs[:, i, :], 64.0, -64.0, amin, amax).then_inc(s["xc_ok"], 1)
            pool.wait_ge(s["pmx_ok"], 1)
            nc.gpsimd.partition_all_reduce(pmr, pmx, P, RMAX).then_inc(s["pmr_ok"], 1)
            pool.wait_ge(s["pmx_ok"], 2)
            nc.gpsimd.partition_all_reduce(pmr2, pmx2, P, RMAX).then_inc(s["pmr_ok"], 1)
            pool.wait_ge(s["cm_ok"], 1)
            nc.gpsimd.partition_all_reduce(cmr, cm, P, RMAX).then_inc(s["cmr_ok"], 1)
            pool.wait_ge(s["qkv_pe"], 12 * NC)
            pool.wait_ge(s["lq_ok"], 10 * NC + 1)
            nc.gpsimd.memset(kst[96:98, :, :], MU).then_inc(s["const_ok"], 1)
            pool.wait_ge(s["const_ok"], 1)
            nc.gpsimd.memset(vst[:, :, :, 32:64], 1.0).then_inc(s["const_ok"], 1)

            def pool_ffn(n0, p0, down, gateup):
                n, k = 0, 0
                for _, t in rounds(down, gateup):
                    for c in range(NC):
                        if on_pool(t, c):
                            pool.wait_ge(s["act_ok"], n0 + n + 5)
                            pool.wait_ge(s["dve_ok"], n0 + n + 1)
                            nc.gpsimd.tensor_tensor(tmp[:, c, :], tmp[:, c, :], target(t, c), add).then_inc(s["pool_ok"], 1)
                        n += 1

            pool_ffn(0, 0, False, True)
            with pool.Fori(1, PAIRS) as k:
                pool_ffn((k - 1) * 96 + 64, 0, True, True)
            pool_ffn(64 + 96 * (PAIRS - 1), 0, True, False)

        @block.scalar
        def _(act):
            A = nc.scalar.activation
            w_sem = [s["w_in0"], s["w_in1"]]

            def evac_x(i):
                act.wait_ge(s["xh_pe"], i + 1)
                A(xT[:, 0, :, i * P:(i + 1) * P], bank16(2 + 2 * (i % 2)).rearrange("p (k c) -> p k c", k=KT),
                  ACT.Copy).then_inc(s["xh_out"], 1)
                act.wait_ge(s["xl_pe"], i + 1)
                A(xT[:, 1, :, i * P:(i + 1) * P], bank16(3 + 2 * (i % 2)).rearrange("p (k c) -> p k c", k=KT),
                  ACT.Copy).then_inc(s["xl_out"], 1)

            for bt in range(4):
                for k in range(3 * bt, 3 * bt + 3):
                    act.wait_ge(w_sem[k % 2], 16 * (k // 2 + 1))
                    if k >= 1:
                        act.wait_ge(s["wT_pe"], k)
                    A(wsg, wraw[:, k % 2, :], ACT.Sign).then_inc(s["sgn_done"], 1)
                act.wait_ge(s["stat_ok"], bt + 1)
                A(sd_, ve, ACT.Sqrt).then_inc(s["std_ok"], 1)
                for i in range(4 * bt, 4 * bt + 4):
                    act.wait_ge(s["xc_ok"], i + 1)
                    if i >= 2:
                        act.wait_ge(s["xh_pe"], i - 1)
                        act.wait_ge(s["l_ok"], i - 1)
                    A(hst[:, i % 2, :], xs[:, i, :], ACT.Copy, scale=fl[:, i:i + 1]).then_inc(s["h_ok"], 1)
                    if i > 4 * bt:
                        evac_x(i - 1)
                evac_x(4 * bt + 3)

            act.sem_inc(s["y_ok"], 6)
            act.wait_ge(s["fac_ok"], 1)
            act.wait_ge(s["z_out"], 16)

            def act_qkv(b2, s2):
                c = 2 * b2 + s2
                for p in range(12):
                    f = QKV[p]
                    act.wait_ge(s["qkv_pe"], 12 * c + p + 1)
                    act.wait_ge(s["r_ok"], 12 * c + p + 1)
                    A(y2[:, p % 2, :], ps[:, p % 6, :], ACT.Copy, scale=cc[:, f:f + 1]).then_inc(s["y_ok"], 1)
                    if p >= 3:
                        head(c, b2, s2, p - 1)
                head(c, b2, s2, 11)

            def head(c, b2, s2, p):
                f = QKV[p]
                act.wait_ge(s["r_ok"], 12 * c + p + 3)
                src, k = (r2[:, p % 2, :], 0 if f < 8 else 1)
                if f < 8:
                    dst = qz[:, bass.ds(b2 * 8 + f, 1), 0, s2 * 512:(s2 + 1) * 512].rearrange("p a c -> p (a c)")
                else:
                    dst = kz[:, bass.ds(b2 * 2 + (f - 8), 1), 0, s2 * 512:(s2 + 1) * 512].rearrange("p a c -> p (a c)")
                act.nop(nofuse=True)
                A(dst, src, ACT.Copy, scale=fac[:, k:k + 1]).then_inc(s["h2_ok"], 1)

            with act.Fori(0, 2) as b2:
                act_qkv(b2, 0)
                act_qkv(b2, 1)

            act.sem_inc(s["exp_ok"], 2)
            act.sem_inc(s["ost_out"], 16)

            def exp_step(n0, e):
                act.wait_ge(s["st_pe"], n0 + e + 1)
                act.wait_ge(s["pv_pe"], n0 + e + 1)
                A(prob[:, e % 4, :].rearrange("p (a c) -> p a c", a=2), ps[:, 2 + 2 * (e % 2):4 + 2 * (e % 2), :],
                  ACT.Exp, scale=gam[:, 0:1]).then_inc(s["exp_ok"], 1)

            exp_step(0, 0)
            exp_step(0, 1)

            def act_attention(it, last):
                for n in range(HEADS_BODY):
                    rows = slice(32 * (n % 4), 32 * (n % 4) + 32)
                    for k in range(8):
                        e = 8 * n + k
                        if e + 2 < STEPS_BODY or not last:
                            exp_step(128 * it, e + 2)
                        if k % 4 == 3:
                            half = k // 4
                            if n % 4 == 0 and half == 0:
                                act.wait_ge(s["ost_out"], 64 * it + 16 * (n // 4) + 16)
                            act.wait_ge(s["o_ok"], 32 * it + 2 * n + half + 3)
                            A(ost[rows, 0, half * 512:(half + 1) * 512], o32[rows, :], ACT.Copy).then_inc(s["oh_ok"], 1)

            with act.Fori(0, 3) as it:
                act_attention(it, False)
            act_attention(3, True)

            wo_sem = [s["wo_in0"], s["wo_in1"]]
            for i in range(FQ):
                act.wait_ge(wo_sem[i % 2], 16 * (i // 2 + 1))
                if i >= 2:
                    act.wait_ge(s["woT_pe"], i - 1)
                A(wosg[:, i % 2, :], woraw[:, i % 2, :], ACT.Sign).then_inc(s["wosgn_ok"], 1)
            act.wait_ge(s["co_ok"], 1)
            act.sem_inc(s["yo_ok"], 2)

            def act_oproj(ot, m0):
                for s2 in range(2):
                    act.wait_ge(s["o_pe"], m0 + s2 + 1)
                    act.wait_ge(s["acc_ok"], m0 + s2 + 1)
                    act.nop(nofuse=True)
                    A(yo2[:, s2, :], ps[:, s2, :], ACT.Copy,
                      scale=cc[:, bass.ds(ot + 12, 1)]).then_inc(s["yo_ok"], 1)

            for b in range(2):
                with act.Fori(0, FQ) as ot:
                    act_oproj(ot, ot * 2 + 16 * b)

            act.sem_inc(s["act_ok"], 4)

            def act_ffn(n0, k, down, gateup, h1):
                n = 0
                for r, t in rounds(down, gateup):
                    if r == 0:
                        act.wait_ge(s["scl0_in"], 16 * k + 16)
                    if r == 8:
                        act.wait_ge(s["dscl_in"], 16 * k)
                    if r == 16:
                        act.wait_ge(s["scl1_in"], 16 * k + 16)
                    for c in range(NC):
                        act.wait_ge(s["even_pe"], n0 + n + 1)
                        act.wait_ge(s["dve_ok"], n0 + n + 1)
                        A(tmp[:, c, :], ps[:, c, :], ACT.Copy, scale=scale_col(t, 0)).then_inc(s["act_ok"], 1)
                        if (r in (0, 2) and h1) or r in (16, 18):
                            act_h(0 if r < 8 else 1, r % 4, k, c)
                        n += 1

            def act_h(w, step, k, c):
                u = 1 - w
                cs = slice(c * 512, (c + 1) * 512)
                hc = 8 * k - 4 + 4 * w + c
                if step == 0:
                    A(gu[:, u, 0, cs], gu[:, u, 0, cs], ACT.Silu).then_inc(s["sil_ok"], 1)
                else:
                    act.wait_ge(s["hp_ok"], hc + 1)
                    A(hT[:, u, 0, cs], gu[:, u, 0, cs], ACT.Copy).then_inc(s["hh_ok"], 1)

            def act_last():
                act.wait_ge(s["dve_ok"], 64 + 96 * (PAIRS - 1) + 4)
                for step in (0, 2):
                    for c in range(NC):
                        act_h(0, step, PAIRS, c)

            act_ffn(0, 0, False, True, False)
            with act.Fori(1, PAIRS) as k:
                act_ffn((k - 1) * 96 + 64, k, True, True, True)
            act_last()
            act_ffn(64 + 96 * (PAIRS - 1), PAIRS, True, False, False)

        @block.vector
        def _(dve):
            V = nc.vector
            ch = Tally(s["chain"])

            def settle():
                dve.wait_ge(s["chain"], ch.value())

            w_sem = [s["w_in0"], s["w_in1"]]
            for bt in range(4):
                dve.wait_ge(s["x_in"], 64 * (bt + 1))
                for k in range(3 * bt, 3 * bt + 3):
                    dve.wait_ge(w_sem[k % 2], 16 * (k // 2 + 1))
                    V.tensor_reduce(ssum[:, k:k + 1], wraw[:, k % 2, :], AX, add,
                                    apply_absolute_value=True).then_inc(s["abs_done"], 1)
                    dve.wait_ge(s["wT_pe"], k + 1)
                    V.tensor_copy(wT[:, :, k * P:(k + 1) * P],
                                  bank16(k % 2).rearrange("p (k c) -> p k c", k=KT)).then_inc(s["wT_out"], 1)
                for i in range(4 * bt, 4 * bt + 4):
                    ch.inc(V.bn_stats(bn[:, i, 0:6], xs[:, i, 0:512]))
                    ch.inc(V.bn_stats(bn[:, i, 6:12], xs[:, i, 512:1024]))
                settle()
                for i in range(4 * bt, 4 * bt + 4):
                    ch.inc(V.bn_aggr(mv[:, i, :], bn[:, i, :]))
                settle()
                b4 = slice(4 * bt, 4 * bt + 4)
                V.tensor_scalar(ve, mv[:, b4, 1], EPS, None, add).then_inc(s["stat_ok"], 1)
                ch.inc(V.tensor_scalar(fl[:, b4], mv[:, b4, 1], 0.0, 0.0, mult, iseq))
                ch.inc(V.tensor_scalar(mark[:, b4], mv[:, b4, 0], 0.0, None, mult))
                settle()
                ch.inc(V.tensor_scalar(fl[:, b4], fl[:, b4], XS, None, mult))
                dve.wait_ge(s["std_ok"], bt + 1)
                ch.inc(V.reciprocal(rs, sd_))
                settle()
                ch.inc(V.tensor_tensor(t4, rs, rs, mult))
                settle()
                ch.inc(V.tensor_tensor(t4, t4, ve, mult))
                settle()
                ch.inc(V.tensor_scalar(t4, t4, -0.5, 1.5, mult, add))
                settle()
                ch.inc(V.tensor_tensor(rs, rs, t4, mult))
                settle()
                for i in range(4 * bt, 4 * bt + 4):
                    V.tensor_scalar(xs[:, i, :], xs[:, i, :], mv[:, i, 0:1], rs[:, i % 4:i % 4 + 1], sub, mult
                                    ).then_inc(s["norm_ok"], 1)
                for i in range(4 * bt, 4 * bt + 4):
                    dve.wait_ge(s["h_ok"], i + 1)
                    if i >= 2:
                        dve.wait_ge(s["xl_pe"], i - 1)
                    V.scalar_tensor_tensor(lst[:, i % 2, :], xs[:, i, :], fl[:, i:i + 1], hst[:, i % 2, :],
                                           mult, sub).then_inc(s["l_ok"], 1)

            dve.wait_ge(s["znat_in"], 48)
            dve.wait_ge(s["snat_pe"], 1)
            for m in range(2):
                ch.inc(V.tensor_scalar(tab[:, :, m * KT:(m + 1) * KT].rearrange("p t g -> p g t"),
                                       ps[:, 6 + m // 2, m * 224:(m + 1) * 224].rearrange("p (g t) -> p g t", g=KT),
                                       1.0 / XS, None, mult))
            ch.inc(V.tensor_copy(dtab[:, :, :].rearrange("p t o -> p o t"),
                                 ps[:, 7, 0:224].rearrange("p (o t) -> p o t", o=FQ)))
            V.tensor_copy(zf16, znat).then_inc(s["tab_ok"], 1)
            settle()
            V.tensor_reduce(pmx, tab[:, :, 0:KT], AX, amax, apply_absolute_value=True).then_inc(s["pmx_ok"], 1)
            V.tensor_reduce(pmx2, tab[:, :, KT:2 * KT], AX, amax, apply_absolute_value=True).then_inc(s["pmx_ok"], 1)
            dve.wait_ge(s["par_in"], 64)
            dve.wait_ge(s["abs_done"], NW)

            def channel_scales(a, b):
                ch.inc(V.tensor_scalar(cc[:, a:b], ssum[:, a:b], 1.0 / H, 1e-8, mult, amax))
                settle()
                ch.inc(V.tensor_tensor(cc[:, a:b], cc[:, a:b], spar[:, a:b], mult))
                settle()
                ch.inc(V.tensor_scalar(cc[:, a:b], cc[:, a:b], FMAX, -FMAX, amin, amax))
                settle()

            channel_scales(0, 12)
            ch.inc(V.tensor_scalar(cc[:, 0:12], cc[:, 0:12], 1.0 / XS, None, mult))
            settle()
            for j, (a, b) in enumerate(((0, 8), (8, 10), (10, 12))):
                ins = V.tensor_reduce(cm[:, j:j + 1], cc[:, a:b], AX, amax, apply_absolute_value=True)
                if j < 2:
                    ch.inc(ins)
                else:
                    ins.then_inc(s["cm_ok"], 1)
            dve.wait_ge(s["cmr_ok"], 1)
            ch.inc(V.tensor_scalar(cmr, cmr, 1e-30, None, amax))
            settle()
            ch.inc(V.reciprocal(fac, cmr))
            ch.inc(V.tensor_tensor(gam, cmr[:, 0:1], cmr[:, 1:2], mult))
            settle()
            ch.inc(V.tensor_scalar(gam, gam, (256.0 * 1024.0 / QB) ** 2 / float(D) ** 0.5, None, mult))
            V.tensor_scalar(fac, fac, QB / (256.0 * 1024.0), None, mult).then_inc(s["fac_ok"], 1)
            dve.wait_ge(s["pmr_ok"], 2)
            ch.inc(V.tensor_tensor(pmr, pmr, pmr2, mult))
            settle()
            ch.inc(V.tensor_scalar(pmr, pmr, XS * XS, 1e-30, mult, amax))
            settle()
            ch.inc(V.reciprocal(pmx, pmr))
            settle()
            ch.inc(V.tensor_scalar(tab[:, :, 16], pmx, 2.0 ** -12, None, mult))
            ch.inc(V.tensor_scalar(pmr, pmr, 2.0 ** 12, None, mult))
            settle()
            for o in range(FQ):
                ch.inc(V.tensor_tensor(dtab[:, :, o], dtab[:, :, o], pmr, mult))
            settle()

            def guard(y, r, f):
                ch.inc(V.tensor_scalar(r, y, 1e6, -1e6, amin, amax))
                ch.inc(V.tensor_scalar(f, y, 0.0, 0.0, mult, iseq))
                settle()
                dve.nop(nofuse=True)
                return V.copy_predicated(r, f, y)

            dve.sem_inc(s["lq_ok"], 1)
            dve.sem_inc(s["r_ok"], 2)
            ch0 = ch.value()

            def dve_qkv(b2, s2):
                c = 2 * b2 + s2
                for p in range(12):
                    dve.wait_ge(s["y_ok"], 12 * c + p + 7)
                    dve.wait_ge(s["r_ok"], 12 * c + p + 2)
                    if p >= 2:
                        dve.wait_ge(s["lq_ok"], 10 * c + max(p - 3, 0) + 1)
                    dst = rv2[:, p, :] if p < 2 else r2[:, p % 2, :]
                    guard(y2[:, p % 2, :], dst, fin).then_inc(s["r_ok"], 1)
                    if p < 2:
                        dve.wait_ge(s["r_ok"], 12 * c + p + 3)
                        V.tensor_scalar(dst, dst, fac[:, 2:3], None, mult).then_inc(s["vr_ok"], 1)
                    if p >= 3:
                        tail(c, b2, s2, p - 1)
                    if p == 7:
                        for fv in range(2):
                            dve.wait_ge(s["v_pe"], 2 * c + fv + 1)
                            src = ps[:, 6 + fv, :].rearrange("p (t g d) -> p g t d", t=4, g=4)
                            to = vz[:, bass.ds(b2 * 8 + fv * 4, 4), 4 * s2:4 * s2 + 4, :]
                            dve.nop(nofuse=True)
                            V.tensor_copy(to, src).then_inc(s["v_out"], 1)
                tail(c, b2, s2, 11)

            def tail(c, b2, s2, p):
                f = QKV[p]
                dve.wait_ge(s["h2_ok"], 10 * c + p - 1)
                k = 0 if f < 8 else 1
                z, f0 = (qz, b2 * 8 + f) if f < 8 else (kz, b2 * 2 + (f - 8))
                hd = z[:, bass.ds(f0, 1), 0, s2 * 512:(s2 + 1) * 512].rearrange("p a c -> p (a c)")
                to = z[:, bass.ds(f0, 1), 1, s2 * 512:(s2 + 1) * 512].rearrange("p a c -> p (a c)")
                V.scalar_tensor_tensor(to, r2[:, p % 2, :], fac[:, k:k + 1], hd, mult, sub).then_inc(s["lq_ok"], 1)

            with dve.Fori(0, 2) as b2:
                ch.enter(ch0, b2, 48)
                dve_qkv(b2, 0)
                dve_qkv(b2, 1)
                assert ch.n == 48
            ch.leave(ch0 + 24 * NC)

            dve.sem_inc(s["o_ok"], 2)

            def row_max(i0, i, par, qt):
                dve.wait_ge(s["s_pe"], i0 + i + 1)
                V.tensor_reduce(mxs[:, par, qt:qt + 1], ps[:, 0:2, :].rearrange("p a c -> p (a c)"), AX, amax
                                ).then_inc(s["max_ok"], 1)

            def split_max(i0, i, par):
                dve.wait_ge(s["max_ok"], i0 + i + 1)
                ch.inc(V.tensor_scalar(mhl[:, 0:8], mxs[:, par, :], -1.0 / MU, None, mult))
                settle()
                V.scalar_tensor_tensor(mhl[:, 8:16], mxs[:, par, :], -1.0 / MU, mhl[:, 0:8], mult, sub
                                       ).then_inc(s["mhl_ok"], 1)

            def copy_rows(hd, par):
                dve.wait_ge(s["m_pe"], hd)
                V.tensor_copy(mrow[0:16, par, :], ps[0:16, 7, 0:64].bitcast(f16)).then_inc(s["mrow_ok"], 1)

            for i in range(8):
                row_max(0, i, 0, i)
            split_max(0, 7, 0)
            copy_rows(1, 0)
            for i in range(6):
                row_max(0, 8 + i, 1, i)
            cha = ch.value()

            def dve_attention(it, last):
                for n in range(HEADS_BODY):
                    rows = slice(32 * (n % 4), 32 * (n % 4) + 32)
                    for k in range(8):
                        e = 8 * n + k
                        hd, qt = (n + 1, 6 + k) if k < 2 else (n + 2, k - 2)
                        if not (last and hd > 15):
                            row_max(128 * it, LEAD_S + e, hd % 2, qt)
                            if k == 1:
                                split_max(128 * it, LEAD_S + e, hd % 2)
                        if k == 3 and not (last and n == 15):
                            copy_rows(16 * it + n + 2, (n + 1) % 2)
                        if k % 4 == 3:
                            half = k // 4
                            pv = ps[:, 6 + half, :]
                            dve.wait_ge(s["pv_pe"], 128 * it + e + 5)
                            ch.inc(V.reciprocal(rsum[rows, :], pv[32:64, :]))
                            settle()
                            ins = V.tensor_tensor(o32[rows, :], pv[0:32, :], rsum[rows, :], mult)
                            ins.then_inc(s["o_ok"], 1)
                            dve.wait_ge(s["oh_ok"], 32 * it + 2 * n + half + 1)
                            V.tensor_tensor(ost[rows, 1, half * 512:(half + 1) * 512], o32[rows, :],
                                            ost[rows, 0, half * 512:(half + 1) * 512], sub).then_inc(s["ol_ok"], 1)

            CHA = 48
            with dve.Fori(0, 3) as it:
                ch.enter(cha, it, CHA)
                dve_attention(it, False)
                assert ch.n == CHA, ch.n
            ch.leave(cha + 3 * CHA)
            dve_attention(3, True)

            wo_sem = [s["wo_in0"], s["wo_in1"]]
            for i in range(FQ):
                dve.wait_ge(wo_sem[i % 2], 16 * (i // 2 + 1))
                V.tensor_reduce(ssum[:, 12 + i:13 + i], woraw[:, i % 2, :], AX, add,
                                apply_absolute_value=True).then_inc(s["woabs_ok"], 1)
                dve.wait_ge(s["woT_pe"], i + 1)
                V.tensor_copy(woT[:, :, i * P:(i + 1) * P],
                              bank16(2 + i % 2).rearrange("p (k c) -> p k c", k=KT)).then_inc(s["woT_out"], 1)
            dve.wait_ge(s["woabs_ok"], FQ)
            channel_scales(12, 20)
            ch.inc(V.tensor_scalar(fac[:, 2:3], cmr[:, 2:3], 256.0 * 1024.0 / QB, None, mult))
            settle()
            V.tensor_scalar(cc[:, 12:20], cc[:, 12:20], fac[:, 2:3], None, mult).then_inc(s["co_ok"], 1)
            dve.sem_inc(s["acc_ok"], 2)
            cho = ch.value()

            def dve_oproj(ot, m0, b):
                for s2 in range(2):
                    dve.wait_ge(s["yo_ok"], m0 + s2 + 3)
                    dve.wait_ge(s["acc_ok"], m0 + s2 + 2)
                    ch.inc(guard(yo2[:, s2, :], ro, fino))
                    settle()
                    dve.nop(nofuse=True)
                    V.tensor_copy(acc[b][:, bass.ds(ot, 1), s2 * 512:(s2 + 1) * 512].rearrange("p a c -> p (a c)"), ro
                                  ).then_inc(s["acc_ok"], 1)

            for b in range(2):
                with dve.Fori(0, FQ) as ot:
                    ch.enter(cho + 48 * b, ot, 6)
                    dve_oproj(ot, ot * 2 + 16 * b, b)
                    assert ch.n == 6
            ch.leave(cho + 96)

            def subtract(k0, k, u, m, j):
                ring = k % 2
                dve.wait_ge(s[f"p_in{ring}"], piece_value(k0, k))
                w = wst[:, ring, :]
                V.tensor_tensor(wf[:, u, m, j * 512:(j + 1) * 512], w, zst[:, ring, :], sub).then_inc(s["sub_ok"], 1)

            def piece_value(k0, k):
                if isinstance(k0, int):
                    return 32 * (k0 // 2 + k // 2 + 1)
                return k0 * 16 + 32 * (k // 2 + 1)

            dve.sem_inc(s["dve_ok"], 4)
            for i, (m, j) in enumerate([(m, j) for m in range(2) for j in range(2)]):
                subtract(0, i, 0, m, j)
            chf = ch.value()

            def dve_ffn(n0, k, down, gateup, h1, last):
                n, np_ = 0, 0
                p0 = pool_base(k, gateup)
                i = 0
                for r, t in rounds(down, gateup):
                    if r == 0:
                        dve.wait_ge(s["scl0_in"], 16 * k + 16)
                    if r == 8:
                        dve.wait_ge(s["dscl_in"], 16 * k)
                    if r == 16:
                        dve.wait_ge(s["scl1_in"], 16 * k + 16)
                    for c in range(NC):
                        if on_pool(t, c):
                            np_ += 1
                            dve.wait_ge(s["pool_ok"], p0 + np_)
                        else:
                            dve.wait_ge(s["act_ok"], n0 + n + 5)
                            if not first_of(t):
                                ch.inc(V.tensor_tensor(tmp[:, c, :], tmp[:, c, :], target(t, c), add))
                                settle()
                        dve.wait_ge(s["odd_pe"], n0 + n + 1)
                        V.scalar_tensor_tensor(target(t, c), ps[:, 4 + c, :], scale_col(t, 1), tmp[:, c, :],
                                               mult, add).then_inc(s["dve_ok"], 1)
                        if (r in (1, 3) and h1) or r in (17, 19):
                            dve_h(0 if r < 8 else 1, r % 4, k, c)
                        n += 1
                    if gateup and r in (4, 5, 6, 7):
                        subtract(4 + 12 * k, i, 1, (r - 4) // 2, (r - 4) % 2)
                        i += 1
                        if r == 7 and not down:
                            for m, j in ((0, 0), (0, 1), (1, 0), (1, 1)):
                                subtract(4 + 12 * k, i, 0, m, j)
                                i += 1
                    if gateup and down and not last and r in (10, 11, 12, 13):
                        subtract(4 + 12 * k, i, 0, (r - 10) // 2, (r - 10) % 2)
                        i += 1
                    if gateup and r >= 20:
                        subtract(4 + 12 * k, i, (r - 20) // 2, 2, (r - 20) % 2)
                        i += 1

            def dve_h(w, step, k, c):
                u = 1 - w
                cs = slice(c * 512, (c + 1) * 512)
                hc = 8 * k - 4 + 4 * w + c
                if step == 1:
                    dve.wait_ge(s["sil_ok"], hc + 1)
                    V.scalar_tensor_tensor(gu[:, u, 0, cs], gu[:, u, 0, cs], scl[:, u, 16:17], gu[:, u, 1, cs],
                                           mult, mult).then_inc(s["hp_ok"], 1)
                else:
                    dve.wait_ge(s["hh_ok"], hc + 1)
                    V.tensor_tensor(hT[:, u, 1, cs], gu[:, u, 0, cs], hT[:, u, 0, cs], sub).then_inc(s["hl_ok"], 1)

            def pool_base(k, gateup):
                if isinstance(k, int) and k == 0:
                    return 0
                return (k - 1) * (NPOOL_GU + NPOOL_DN) + NPOOL_GU

            dve_ffn(0, 0, False, True, False, False)
            ch1 = ch.value()
            with dve.Fori(1, PAIRS - 1) as k:
                ch.enter(ch1 - 12, k, 12)
                dve_ffn((k - 1) * 96 + 64, k, True, True, True, False)
                assert ch.n == 12, ch.n
            ch.leave(ch1 + 12 * (PAIRS - 2))
            dve_ffn(64 + 96 * (PAIRS - 2), PAIRS - 1, True, True, True, True)
            for step in (1, 3):
                for c in range(NC):
                    dve_h(0, step, PAIRS, c)
            dve_ffn(64 + 96 * (PAIRS - 1), PAIRS, True, False, False, True)

            for i in range(NX):
                dve.wait_ge(s["t_pe"], i + 1)
                dve.wait_ge(s[f"xr_in{i % 4}"], 16 * (i // 4 + 1))
                if i >= 4:
                    dve.wait_ge(s[f"out_ok{i % 4}"], 16 * (i // 4))
                V.scalar_tensor_tensor(fo[:, i % 4, :].rearrange("p (a c) -> p a c", a=2),
                                       ps[:, 2 * (i % 4):2 * (i % 4) + 2, :], mark[:, i:i + 1],
                                       xin[:, i % 4, :].rearrange("p (a c) -> p a c", a=2), add, add
                                       ).then_inc(s["f_ok"], 1)

        @block.tensor
        def _(pe):
            MM = nc.tensor.matmul
            TR = nc.tensor.transpose
            pe.wait_ge(s["ident"], 4)
            for bt in range(4):
                for k in range(3 * bt, 3 * bt + 3):
                    pe.wait_ge(s["sgn_done"], k + 1)
                    if k >= 2:
                        pe.wait_ge(s["wT_out"], k - 1)
                    for t in range(KT):
                        last = TR(bank16(k % 2)[:, t * P:(t + 1) * P], wsg[:, t * P:(t + 1) * P], id16[:])
                    last.then_inc(s["wT_pe"], 1)
                for i in range(4 * bt, 4 * bt + 4):
                    for part, st_, ok, done, free in ((0, hst, "h_ok", "xh_pe", "xh_out"),
                                                      (1, lst, "l_ok", "xl_pe", "xl_out")):
                        pe.wait_ge(s[ok], i + 1)
                        if i >= 2:
                            pe.wait_ge(s[free], i - 1)
                        for t in range(KT):
                            last = TR(bank16(2 + 2 * (i % 2) + part)[:, t * P:(t + 1) * P],
                                      st_[:, i % 2, t * P:(t + 1) * P], id16[:])
                        last.then_inc(s[done], 1)
            pe.wait_ge(s["snat_in"], 48)
            for m, nat in enumerate((snat_g, snat_u)):
                for g in range(KT):
                    TR(ps[:, 6, m * 224 + g * IT:m * 224 + (g + 1) * IT], nat[:, g, :], id32[0:IT, 0:IT])
            for o in range(FQ):
                last = TR(ps[:, 7, o * IT:(o + 1) * IT], snat_d[:, o * P:(o + 1) * P], id32[0:IT, 0:IT])
            last.then_inc(s["snat_pe"], 1)

            pe.wait_ge(s["wT_out"], NW)
            pe.wait_ge(s["xh_out"], NX)
            pe.wait_ge(s["xl_out"], NX)
            pe.wait_ge(s["tab_ok"], 1)

            def pe_qkv(c):
                for p in range(12):
                    f = QKV[p]
                    pe.wait_ge(s["y_ok"], 12 * c + p + 1)
                    for kt in range(KT):
                        for part in range(2):
                            last = MM(ps[:, p % 6, :], wT[:, kt, f * P:(f + 1) * P],
                                      xT[:, part, kt, bass.ds(c * 512, 512)],
                                      start=(kt == 0 and part == 0), stop=(kt == KT - 1 and part == 1))
                    last.then_inc(s["qkv_pe"], 1)
                    if p == 5:
                        for fv in range(2):
                            pe.wait_ge(s["vr_ok"], 2 * c + fv + 1)
                            for t in range(4):
                                last = TR(ps[:, 6 + fv, t * P:(t + 1) * P], rv2[:, fv, t * P:(t + 1) * P], id32[:])
                            last.then_inc(s["v_pe"], 1)

            with pe.Fori(0, NC) as c:
                pe_qkv(c)

            pe.sem_inc(s["pv_pe"], 4)

            def row_scores(i0, i, qbuf, kbuf, qt):
                if not (isinstance(i0, int) and i0 + i == 0):
                    pe.wait_ge(s["max_ok"], i0 + i)
                for h2 in range(2):
                    last = MM(ps[:, h2, :], qst[0:96, qbuf, qt * P:(qt + 1) * P],
                              kst[0:96, kbuf, h2 * 512:(h2 + 1) * 512], start=True, stop=True)
                last.then_inc(s["s_pe"], 1)

            def maxima_rows(hd_count):
                pe.wait_ge(s["mhl_ok"], hd_count)
                TR(ps[0:16, 7, 0:64].bitcast(f16), mhl[:, 0:16], id16[:]).then_inc(s["m_pe"], 1)

            def key_scores(n0, e, qbuf, kbuf):
                half, j = (e // 4) % 2, e % 4
                pe.wait_ge(s["exp_ok"], n0 + e + 1)
                for a in range(2):
                    kt = 2 * j + a
                    last = MM(ps[:, 2 + 2 * (e % 2) + a, :], kst[0:98, kbuf, kt * P:(kt + 1) * P],
                              qst[0:98, qbuf, half * 512:(half + 1) * 512], start=True, stop=True)
                last.then_inc(s["st_pe"], 1)

            pe.wait_ge(s["y_ok"], 12 * NC + 6)
            pe.wait_ge(s["v_out"], 2 * NC)
            pe.wait_ge(s["k_in0"], 48)
            pe.wait_ge(s["q_in0"], 48)
            for i in range(8):
                row_scores(0, i, 0, 0, i)
            maxima_rows(1)
            pe.wait_ge(s["q_in1"], 48)
            for i in range(6):
                row_scores(0, 8 + i, 1, 0, i)
            pe.wait_ge(s["m_in0"], 32)
            for e in range(2):
                key_scores(0, e, 0, 0)

            def pe_attention(it, last_body):
                for n in range(HEADS_BODY):
                    gi = n // 4
                    for k in range(8):
                        e = 8 * n + k
                        half = k // 4
                        if n % 4 == 0 and k == 0:
                            pe.wait_ge(s[f"v_in{gi % 2}"], 32 * it + 16 * (gi // 2) + 16)
                        if k % 4 == 0:
                            pe.wait_ge(s["o_ok"], 32 * it + 2 * n + half + 1)
                            if half == 1 and not (last_body and n == 15):
                                pe.wait_ge(s["mrow_ok"], 16 * it + n + 2)
                        pe.wait_ge(s["exp_ok"], 128 * it + e + 3)
                        for a in range(2):
                            last = MM(ps[0:64, 6 + half, :], vst[:, gi % 2, 2 * (k % 4) + a, :],
                                      prob[:, e % 4, a * 512:(a + 1) * 512],
                                      start=(k % 4 == 0 and a == 0), stop=(k % 4 == 3 and a == 1))
                        last.then_inc(s["pv_pe"], 1)
                        e2 = e + 2
                        if e2 < STEPS_BODY or not last_body:
                            n2 = e2 // 8
                            if e2 % 8 == 0:
                                pe.wait_ge(s[f"m_in{n2 % 4}"], 128 * it + 32 * (n2 // 4) + 32)
                            key_scores(128 * it, e2, n2 % 4, (n2 // 4) % 2)
                        hd, qt = (n + 1, 6 + k) if k < 2 else (n + 2, k - 2)
                        if not (last_body and hd > 15):
                            if qt == 0:
                                pe.wait_ge(s[f"q_in{hd % 4}"], 192 * it + 48 * (hd // 4) + 48)
                                if hd % 4 == 0:
                                    gb = (hd // 4) % 2
                                    pe.wait_ge(s[f"k_in{gb}"], 96 * it + 48 * (hd // 8) + 48)
                            row_scores(128 * it, LEAD_S + e, hd % 4, (hd // 4) % 2, qt)
                        if k == 2 and not (last_body and n == 15):
                            pe.wait_ge(s["o_ok"], 32 * it + 2 * n + 2)
                            maxima_rows(16 * it + n + 2)

            with pe.Fori(0, 3) as it:
                pe_attention(it, False)
            pe_attention(3, True)

            for i in range(FQ):
                pe.wait_ge(s["wosgn_ok"], i + 1)
                if i >= 2:
                    pe.wait_ge(s["woT_out"], i - 1)
                for t in range(KT):
                    last = TR(bank16(2 + i % 2)[:, t * P:(t + 1) * P], wosg[:, i % 2, t * P:(t + 1) * P], id16[:])
                last.then_inc(s["woT_pe"], 1)
            pe.wait_ge(s["woT_out"], FQ)
            pe.wait_ge(s["ost_out"], 16 * 17)

            def pe_oproj(ot, m0, b):
                for s2 in range(2):
                    pe.wait_ge(s["yo_ok"], m0 + s2 + 1)
                    pe.nop(nofuse=True)
                    for kt in range(KT):
                        for part in range(2):
                            last = MM(ps[:, s2, :], woT[:, kt, bass.ts(ot, P)],
                                      qz[:, 8 * b + kt, part, s2 * 512:(s2 + 1) * 512],
                                      start=(kt == 0 and part == 0), stop=(kt == KT - 1 and part == 1))
                    last.then_inc(s["o_pe"], 1)

            for b in range(2):
                with pe.Fori(0, FQ) as ot:
                    pe_oproj(ot, ot * 2 + 16 * b, b)

            def pe_ffn(n0, k, down, gateup):
                n = 0
                for r, t in rounds(down, gateup):
                    if r == 0:
                        pe.wait_ge(s["sub_ok"], 12 * k if down else 4)
                    if r == 8:
                        pe.wait_ge(s["sub_ok"], 12 * k + 4 if gateup else 12 * k)
                        pe.wait_ge(s["hl_ok"], 8 * k)
                    if r == 16:
                        pe.wait_ge(s["sub_ok"], 12 * k + 8)
                    for odd in range(2):
                        for c in range(NC):
                            bank = 4 * odd + c
                            pe.wait_ge(s["dve_ok" if odd else "act_ok"], n0 + n + c + 1)
                            for part in range(2):
                                if t[0] == "gu":
                                    g = 2 * t[3] + odd
                                    lhsT = wf[:, t[1], t[2], g * P:(g + 1) * P]
                                    rhs = xT[:, part, g, c * 512:(c + 1) * 512]
                                else:
                                    lhsT = wf[:, odd, 2, t[1] * P:(t[1] + 1) * P]
                                    rhs = hT[:, odd, part, c * 512:(c + 1) * 512]
                                last = MM(ps[:, bank, :], lhsT, rhs, start=(part == 0), stop=(part == 1))
                            last.then_inc(s["odd_pe" if odd else "even_pe"], 1)
                    n += NC

            pe.wait_ge(s["yo_ok"], 2 + 32)
            pe_ffn(0, 0, False, True)
            with pe.Fori(1, PAIRS) as k:
                pe_ffn((k - 1) * 96 + 64, k, True, True)
            pe_ffn(64 + 96 * (PAIRS - 1), PAIRS, True, False)

            NQ = 64 + 96 * (PAIRS - 1) + 32
            pe.wait_ge(s["dve_ok"], NQ + 4)
            for i in range(NX):
                b, c0 = i // 8, (i % 8) * P
                if i >= 4:
                    pe.wait_ge(s["f_ok"], i - 3)
                for o in range(FQ):
                    last = TR(ps[:, 2 * (i % 4) + o // 4, (o % 4) * P:(o % 4 + 1) * P], acc[b][:, o, c0:c0 + P], id32[:])
                last.then_inc(s["t_pe"], 1)


_INS = ['L0_attn_hidden_states', 'L0_attn_q_weight', 'L0_attn_q_scale', 'L0_attn_k_weight', 'L0_attn_k_scale',
        'L0_attn_v_weight', 'L0_attn_v_scale', 'L0_attn_o_weight', 'L0_attn_o_scale',
        'L0_ffn_gate_w', 'L0_ffn_gate_z', 'L0_ffn_gate_s', 'L0_ffn_up_w', 'L0_ffn_up_z', 'L0_ffn_up_s',
        'L0_ffn_down_w', 'L0_ffn_down_z', 'L0_ffn_down_s']


def kernel(**inputs):
    import numpy as _np
    import concourse.bacc as _bacc
    from concourse import mybir as _mybir
    from concourse.bass_utils import run_bass_kernel_spmd as _run

    nc = _bacc.Bacc("TRN2", target_bir_lowering=False, num_devices=1)
    arrays, args = {}, []
    for name in _INS:
        a = _np.ascontiguousarray(inputs[name])
        arrays[f"in_{name}_dram"] = a
        args.append(nc.dram_tensor(f"in_{name}_dram", a.shape, _mybir.dt.from_np(a.dtype), kind="ExternalInput").ap())
    args.append(nc.dram_tensor("out_0_dram", (2, 1024, 1024), _mybir.dt.float32, kind="ExternalOutput").ap())
    args.append(nc.dram_tensor("zero_points", (28, 3, 1024), _mybir.dt.float16, kind="Internal").ap())
    layer_kernel(nc, *args)
    r = _run(nc, [arrays], core_ids=[0])
    return r.results[0]["out_0_dram"]
```

```python
import concourse.bass as bass
from concourse import mybir
from contextlib import ExitStack


P = 128
T, H = 2048, 1024
S = 1024
KT = H // P
I = 3584
IT = I // P
PAIRS = IT // 2
D = 32
FQ, FK = 8, 2
NC = T // 512
NX = T // P
EPS = 1e-5
FMAX = 3.4028234663852886e38
XS = 256.0
QB = 4096.0
MU = 16384.0
HEADS_BODY, STEPS_BODY = 16, 128
LEAD_S = 20


RMAX = bass.bass_isa.ReduceOp.max


class Tally:

    def __init__(self, sem):
        self.sem, self.base, self.n = sem, 0, 0

    def inc(self, ins):
        self.n += 1
        return ins.then_inc(self.sem, 1)

    def value(self):
        return self.base + self.n

    def enter(self, start, i, per):
        self.base, self.n = start + i * per, 0

    def leave(self, total):
        self.base, self.n = 0, total


def layer_kernel(nc, x, wq, sq, wk, sk, wv, sv, wo, so, gw, gz, gs, uw, uz, us, dw, dz, ds, out, zscr, wscr):
    f32, f16, i32 = mybir.dt.float32, mybir.dt.float16, mybir.dt.int32
    ALU = mybir.AluOpType
    ACT = mybir.ActivationFunctionType
    AX = mybir.AxisListType.X
    add, sub, mult, amin, amax, iseq = ALU.add, ALU.subtract, ALU.mult, ALU.min, ALU.max, ALU.is_equal

    ctx = ExitStack()
    with ctx:
        def sb(name, shape, dt=f32):
            return ctx.enter_context(nc.sbuf_tensor(name, shape, dt))

        def sem(name):
            return ctx.enter_context(nc.semaphore(name))

        xT = sb("xT", [P, 2, KT, T], f16)
        zone_a = sb("zone_a", [P, 64 * 256])
        zone_b = sb("zone_b", [P, 75 * 256])

        def view(zone, kb, words, dt=f32):
            v = zone[:, kb * 256:kb * 256 + words]
            return v if dt == f32 else v.bitcast(dt)

        xs = view(zone_a, 0, 16384).rearrange("p (n c) -> p n c", n=NX)
        znat = view(zone_b, 12, 3072, i32)[0:IT, :]
        zf16 = view(zone_b, 24, 1536, f16)[0:IT, :]
        bn = view(zone_b, 30, NX * 12).rearrange("p (n c) -> p n c", n=NX)
        wT = view(zone_b, 32, 6144, f16).rearrange("p (k c) -> p k c", k=KT)
        hst = view(zone_b, 56, 1024, f16).rearrange("p (n c) -> p n c", n=2)
        lst = view(zone_b, 60, 1024, f16).rearrange("p (n c) -> p n c", n=2)
        wraw = view(zone_b, 64, 2048).rearrange("p (n c) -> p n c", n=2)
        wsg = view(zone_b, 72, 512, f16)
        y2 = view(zone_b, 56, 1024).rearrange("p (n c) -> p n c", n=2)
        r2 = view(zone_b, 60, 1024).rearrange("p (n c) -> p n c", n=2)
        rv2 = view(zone_b, 64, 1024).rearrange("p (n c) -> p n c", n=2)
        fin = view(zone_b, 68, 512, i32)
        qz = view(zone_a, 0, 16384, f16).rearrange("p (g h c) -> p g h c", g=16, h=2)
        vz = view(zone_b, 0, 4096).rearrange("p (g k d) -> p g k d", g=16, k=8)
        kz = view(zone_b, 16, 4096, f16).rearrange("p (n h c) -> p n h c", n=4, h=2)
        qst = view(zone_b, 32, 2048, f16).rearrange("p (n c) -> p n c", n=4)
        kst = view(zone_b, 40, 1024, f16).rearrange("p (n c) -> p n c", n=2)
        vst = view(zone_b, 44, 1024).rearrange("p (n k d) -> p n k d", n=2, k=8)
        prob = view(zone_b, 48, 2048).rearrange("p (n c) -> p n c", n=2)
        num = view(zone_b, 56, 2048).rearrange("p (n c) -> p n c", n=2)
        den = view(zone_b, 64, 2048).rearrange("p (n c) -> p n c", n=2)
        ost = view(zone_b, 64, 2048, f16).rearrange("p (n h c) -> p n h c", n=2, h=2)
        wst = view(zone_b, 72, 512, i32)
        acc = [view(zone_b, 0, 8192).rearrange("p (o c) -> p o c", o=FQ),
               view(zone_a, 0, 8192).rearrange("p (o c) -> p o c", o=FQ)]
        woT = view(zone_b, 32, 4096, f16).rearrange("p (k c) -> p k c", k=KT)
        yo2 = view(zone_b, 48, 1024).rearrange("p (n c) -> p n c", n=2)
        ro = view(zone_b, 52, 512)
        fino = view(zone_b, 54, 512, i32)
        woraw = view(zone_b, 56, 2048).rearrange("p (n c) -> p n c", n=2)
        wosg = view(zone_b, 64, 1024, f16).rearrange("p (n c) -> p n c", n=2)
        snat_g = view(zone_b, 0, 1024)[0:IT, :].rearrange("t (g c) -> t g c", g=KT)
        snat_u = view(zone_b, 4, 1024)[0:IT, :].rearrange("t (g c) -> t g c", g=KT)
        snat_d = view(zone_b, 8, 1024)[0:IT, :]
        gu = view(zone_a, 32, 8192).rearrange("p (u m c) -> p u m c", u=2, m=2)
        tmp = view(zone_b, 32, 4096).rearrange("p (n c) -> p n c", n=8)
        hT = [view(zone_b, 48, 2048, f16).rearrange("p (c h n) -> p c h n", c=NC, h=2),
              view(zone_a, 32 + 24, 2048, f16).rearrange("p (c h n) -> p c h n", c=NC, h=2)]
        wf = view(zone_b, 56, 3072, f16).rearrange("p (u m c) -> p u m c", u=2, m=3)
        xin = view(zone_a, 32, 4096).rearrange("p (n c) -> p n c", n=4)
        fo = view(zone_a, 48, 4096).rearrange("p (n c) -> p n c", n=4)
        id32 = sb("id32", [P, P])
        id16 = sb("id16", [P, P], f16)
        zone_c = sb("zone_c", [P, 750])
        zst = zone_c[:, 0:512].bitcast(f16).rearrange("p (n c) -> p n c", n=2)
        mrow = zone_c[:, 512:640].bitcast(f16).rearrange("p (n c) -> p n c", n=2)
        tab = zone_c[:, 0:IT * 17].rearrange("p (t c) -> p t c", t=IT)
        dtab = zone_c[:, IT * 17:IT * 25].rearrange("p (t c) -> p t c", t=IT)
        sm = sb("sm", [P, 286])

        def cols(a, n):
            return sm[:, a:a + n]

        ssum, spar, cc = cols(0, 20), cols(20, 20), cols(40, 20)
        mv = cols(60, 32).rearrange("p (n c) -> p n c", n=NX)
        ve, sd_, rs, t4 = cols(92, 4), cols(96, 4), cols(100, 4), cols(104, 4)
        fl, mark = cols(108, NX), cols(124, NX)
        cm, cmr, fac, gam = cols(140, 3), cols(143, 3), cols(146, 3), cols(149, 1)
        mxs = cols(150, 16).rearrange("p (n c) -> p n c", n=2)
        mhl = cols(166, 8).bitcast(f16)
        pmx, pmx2, pmr, pmr2 = (cols(174 + 28 * j, 28) for j in range(4))
        scl = zone_c[:, 700:734].rearrange("p (u c) -> p u c", u=2)
        dscl = zone_c[:, 734:750].rearrange("p (u c) -> p u c", u=2)

        ps = ctx.enter_context(nc.psum_tensor("ps", [P, 8, 512], f32))

        def bank16(b):
            return ps[:, b, :].bitcast(f16)

        names = """x_in w_in0 w_in1 par_in snat_in znat_in z_out ident sgn_done abs_done wT_pe wT_out
            stat_ok std_ok norm_ok xc_ok h_ok l_ok xh_pe xl_pe xh_out xl_out snat_pe z_ok pmx_ok pmr_ok
            cm_ok cmr_ok fac_ok chain
            qkv_pe y_ok r_ok h2_ok lq_ok vr_ok v_pe v_out
            q_in0 q_in1 q_in2 q_in3 m_in0 m_in1 m_in2 m_in3 k_in0 k_in1 v_in0 v_in1 const_ok
            s_pe max_ok mhl_ok m_pe mrow_ok st_pe exp_ok pv_pe ev_ok rc_ok mu_ok oh_ok ol_ok ost_out0 ost_out1
            piece_in sub_ok wz_out0 wz_out1 wgu_in0 wgu_in1 wd_in evb_ok
            wo_in0 wo_in1 wosgn_ok woabs_ok woT_pe woT_out co_ok o_pe yo_ok ro_ok acc_ok
            even_pe odd_pe act_ok pool_ok dve_ok sil_ok hp_ok hh_ok hl_ok scl0_in scl1_in dscl_in
            t_pe f_ok xr_in0 xr_in1 xr_in2 xr_in3 out_ok0 out_ok1 out_ok2 out_ok3""".split()
        s = {n: sem(n) for n in names}

        WSRC = [(wq, i * P) for i in range(FQ)] + [(wk, i * P) for i in range(FK)] + [(wv, i * P) for i in range(FK)]
        NW = len(WSRC)
        QKV = [10, 11] + list(range(10))
        GATE_UP = [(u, m, gp) for u in range(2) for m in range(2) for gp in range(4)]
        ROUNDS = [("gu",) + t for t in GATE_UP[:8]] + [("dn", ot, 0, 0) for ot in range(FQ)] \
            + [("gu",) + t for t in GATE_UP[8:]]

        def rounds(down, gateup):
            return [(r, t) for r, t in enumerate(ROUNDS) if (t[0] == "gu" and gateup) or (t[0] == "dn" and down)]

        def first_of(t):
            return t[0] == "gu" and t[3] == 0

        def by_vector(t, c):
            return not first_of(t) and c == 3 and (t[0] == "gu" or t[1] % 2 == 0)

        def chunks(down, gateup):
            out, n, a, b, g = [], 0, 0, 0, 0
            bank = {0: ("a", -3), 1: ("a", -2), 2: ("a", -1), 3: ("b", -1)}
            slots = {0: ("g", -6), 1: ("g", -5), 2: ("g", -4), 3: ("n", -13),
                     4: ("g", -3), 5: ("g", -2), 6: ("g", -1), 7: ("g", -19)}
            if gateup and not down:
                bank = {c: ("a", c - 4) for c in range(NC)}
                slots = {}
            for r, t in rounds(down, gateup):
                for c in range(NC):
                    kind, slot = "b" if by_vector(t, c) else "a", 4 * (r % 2) + c
                    pool = kind == "a" and not first_of(t)
                    out.append(dict(r=r, t=t, c=c, n=n, a=a, b=b, g=g, kind=kind, pool=pool, bank=bank[c],
                                    slot=slot, freed=slots.get(slot)))
                    bank[c] = (kind, a if kind == "a" else b)
                    if kind == "a":
                        slots[slot] = ("g", g) if pool else ("n", n)
                    n, a, b, g = n + 1, a + (kind == "a"), b + (kind == "b"), g + pool
            return out, (n, a, b, g)

        BODY = {"first": chunks(False, True), "full": chunks(True, True), "last": chunks(True, False)}

        def counts_before(k):
            return tuple(f + (k - 1) * g for f, g in zip(BODY["first"][1], BODY["full"][1]))

        ZERO = (0, 0, 0, 0)
        H_STEPS = {"first": {(1, c, j): 16 + c + j for c in range(NC) for j in range(4)},
                   "full": {**{(0, c, j): (0, 1, 3, 4)[j] + c for c in range(NC) for j in range(4)},
                            **{(1, c, j): (8, 9, 16, 17)[j] + c for c in range(NC) for j in range(4)}},
                   "last": {}}

        def h_steps(kind, ch, mine):
            if ch["c"] != 1:
                return []
            return sorted((j, w, c) for (w, c, j), r in H_STEPS[kind].items() if r == ch["r"] and j in mine)

        def wait_products(eng, w, m, c, n0, g0):
            if c == 3:
                eng.wait_ge(s["dve_ok"], n0 + (-16, 0, 16, 32)[2 * w + m] + 4)
            else:
                eng.wait_ge(s["pool_ok"], g0 + (-9, 0, 9, 18)[2 * w + m])

        def target(t, c):
            if t[0] == "gu":
                return gu[:, t[1], t[2], c * 512:(c + 1) * 512]
            return acc[c // 2][:, t[1], (c % 2) * 512:(c % 2) * 512 + 512]

        def scale_col(t, odd):
            if t[0] == "gu":
                k = t[2] * KT + 2 * t[3] + odd
                return scl[:, t[1], k:k + 1]
            return dscl[:, odd, t[1]:t[1] + 1]

        def wait_scales(eng, r, k):
            name, n = {0: ("scl0_in", 16 * k + 16), 8: ("dscl_in", 16 * k), 16: ("scl1_in", 16 * k + 16)}[r]
            eng.wait_ge(s[name], n)

        block = ctx.enter_context(nc.Block())

        @block.sync
        def _(sp):
            w_sem = [s["w_in0"], s["w_in1"]]
            for i in range(NX):
                b, r0 = i // 8, (i % 8) * P
                sp.dma_start(xs[:, i, :], x[b, r0:r0 + P, :]).then_inc(s["x_in"], 16)
                if i < 2:
                    src, w0 = WSRC[i]
                    sp.dma_start(wraw[:, i, :], src[w0:w0 + P, :]).then_inc(w_sem[i], 16)
                if i % 4 == 3:
                    if i == 3:
                        for k, (v, n, c0) in enumerate(((sq, FQ, 0), (sk, FK, 8), (sv, FK, 10), (so, FQ, 12))):
                            sp.dma_start(spar[:, c0:c0 + n], v.rearrange("(t p) -> p t", p=P), allow_slow_non_contiguous=True).then_inc(s["par_in"], 16)
                        for m, zsrc in enumerate((gz, uz)):
                            sp.dma_start(znat[:, m * 1024:(m + 1) * 1024].rearrange("t (g c) -> t g c", g=KT),
                                         zsrc.rearrange("g (t c) -> t g c", c=P)).then_inc(s["znat_in"], 16)
                        sp.dma_start(znat[:, 2048:3072], dz).then_inc(s["znat_in"], 16)
                    sp.wait_ge(s["x_in"], 16 * (i + 1))
                    for j in range(3):
                        k = 2 + (i // 4) * 3 + j
                        if k < NW:
                            sp.wait_ge(s["sgn_done"], k - 1)
                            sp.wait_ge(s["abs_done"], k - 1)
                            src, w0 = WSRC[k]
                            sp.dma_start(wraw[:, k % 2, :], src[w0:w0 + P, :]).then_inc(w_sem[k % 2], 16)
            sp.wait_ge(s["z_ok"], 1)
            sp.dma_start(zscr.rearrange("t m c -> t (m c)"), zf16).then_inc(s["z_out"], 16)

            def load_q(hd, g, buf):
                rows = slice(32 * (hd % 4), 32 * (hd % 4) + 32)
                for part, to in ((0, 0), (1, 32), (0, 64)):
                    sp.dma_start(qst[to:to + 32, buf, :], qz[rows, g, part, :]).then_inc(s[f"q_in{buf}"], 16)

            def load_kv(gi, it, g, buf):
                rows = slice(32 * gi, 32 * gi + 32)
                for part, to in ((0, 0), (0, 32), (1, 64)):
                    sp.dma_start(kst[to:to + 32, buf, :], kz[rows, it, part, :]).then_inc(s[f"k_in{buf}"], 16)
                sp.dma_start(vst[:, buf, :, 0:32], vz[:, g, :, :]).then_inc(s[f"v_in{buf}"], 16)

            def load_m(buf, par):
                for part in range(2):
                    sp.dma_start(qst[96 + part:97 + part, buf, :].rearrange("a (q c) -> a q c", q=8),
                                 mrow[8 * part:8 * part + 8, par, :]).then_inc(s[f"m_in{buf}"], 16)

            sp.wait_ge(s["lq_ok"], 10 * NC + 1)
            sp.wait_ge(s["h2_ok"], 10 * NC)
            sp.wait_ge(s["v_out"], 2 * NC)
            sp.wait_ge(s["const_ok"], 2)
            load_kv(0, 0, 0, 0)
            for hd in range(4):
                load_q(hd, 0, hd)
            for hd in range(2):
                sp.wait_ge(s["mrow_ok"], hd + 1)
                load_m(hd, hd)

            def load_piece(t, p):
                t, m, j = t + p // 6, p % 6 // 2, p % 2
                if m < 2:
                    src = (gw, uw)[m].rearrange("(g p) i -> p g i", p=P)[:, 4 * j:4 * j + 4, bass.ts(t, P)]
                    dst = wst.rearrange("p (g c) -> p g c", g=4)
                else:
                    src, dst = dw[bass.ts(t, P), j * 512:(j + 1) * 512], wst
                sp.dma_start(dst, src).then_inc(s["piece_in"], 16)
                z = zscr[bass.ds(t, 1), m, j * 512:(j + 1) * 512]
                sp.dma_start(zst[:, p % 2, :], z.rearrange("a c -> (a c)").partition_broadcast(P)
                             ).then_inc(s["piece_in"], 16)

            def store_piece(t, p):
                t, m, j = t + p // 6, p % 6 // 2, p % 2
                dst = wscr[bass.ds(t, 1), m, :, j * 512:(j + 1) * 512].rearrange("a p c -> p (a c)")
                sp.dma_start(dst, zst[:, p % 2, :]).then_inc(s[f"wz_out{p % 2}"], 16)

            def next_piece(it, p, last):
                sp.wait_ge(s["sub_ok"], 42 * it + p + 1)
                sp.nop(nofuse=True)
                if p + 1 < 42 or not last:
                    sp.wait_ge(s[f"wz_out{(p + 1) % 2}"], 16 * 21 * it + 16 * ((p + 1) // 2) + 16)
                    sp.nop(nofuse=True)
                    load_piece(7 * it, p + 1)
                store_piece(7 * it, p)

            def store_output(it, go):
                sp.wait_ge(s["ol_ok"], 4 * it + go + 1)
                sp.nop(nofuse=True)
                sp.dma_start(qz[:, 4 * it + go, :, :], ost[:, go % 2, :, :]).then_inc(s[f"ost_out{go % 2}"], 16)

            def sp_attention(it, last):
                for e in range(STEPS_BODY):
                    n, k, gi = e // 8, e % 8, e // 32
                    if e % 3 == 0 and e // 3 < 42:
                        next_piece(it, e // 3, last)
                    if e % 32 == 2 and not (last and gi == 3):
                        sp.wait_ge(s["pv_pe"], 128 * it + 32 * gi + 2)
                        ng = gi + 1
                        sp.nop(nofuse=True)
                        load_kv(ng % 4, it + ng // 4, 4 * it + ng, ng % 2)
                    if k == 6 and (n + 2 < 16 or not last):
                        sp.wait_ge(s["mrow_ok"], 16 * it + n + 3)
                        load_m((n + 2) % 4, n % 2)
                    if k == 7 and (n + 4 < 16 or not last):
                        sp.wait_ge(s["st_pe"], 128 * it + 8 * n + 8)
                        nx = n + 4
                        sp.nop(nofuse=True)
                        load_q(nx, (4 * it + nx // 4), nx % 4)
                    if e % 32 == 31 and gi > 0:
                        store_output(it, gi - 1)
                store_output(it, 3)

            for j in range(2):
                sp.sem_inc(s[f"wz_out{j}"], 16)
            sp.wait_ge(s["z_out"], 16)
            load_piece(0, 0)
            with sp.Fori(0, 3) as it:
                sp_attention(it, False)
            sp_attention(3, True)

            sp.dma_start(snat_g, gs.rearrange("g (t c) -> t g c", c=P)).then_inc(s["snat_in"], 16)
            sp.dma_start(snat_u, us.rearrange("g (t c) -> t g c", c=P)).then_inc(s["snat_in"], 16)
            sp.dma_start(snat_d, ds).then_inc(s["snat_in"], 16)
            wo_sem = [s["wo_in0"], s["wo_in1"]]
            for i in range(FQ):
                if i >= 2:
                    sp.wait_ge(s["wosgn_ok"], i - 1)
                    sp.wait_ge(s["woabs_ok"], i - 1)
                sp.dma_start(woraw[:, i % 2, :], wo[i * P:(i + 1) * P, :]).then_inc(wo_sem[i % 2], 16)

            def load_gate_up(u, t):
                sp.dma_start(wf[:, u, 0:2, :], wscr[bass.ds(t, 1), 0:2, :, :].rearrange("a m p c -> p (a m) c")
                             ).then_inc(s[f"wgu_in{u}"], 16)

            def load_down(t):
                sp.dma_start(wf[:, :, 2, :], wscr[bass.ds(t, 2), 2, :, :].rearrange("u p c -> p u c")
                             ).then_inc(s["wd_in"], 16)

            def scales(u, t):
                sp.dma_start(scl[:, u, :], tab[:, bass.ds(t, 1), :].rearrange("p a c -> p (a c)")
                             ).then_inc(s[f"scl{u}_in"], 16)

            def sp_ffn(k, n0, first, last):
                if not first:
                    sp.wait_ge(s["odd_pe"], n0)
                load_gate_up(1, 2 * k + 1)
                if not first:
                    sp.wait_ge(s["dve_ok"], n0 - 32 + 4)
                    sp.dma_start(dscl[:, :, :], dtab[:, bass.ds(2 * k - 2, 2), :]).then_inc(s["dscl_in"], 16)
                    sp.wait_ge(s["hp_ok"], 8 * k)
                scales(1, 2 * k + 1)
                if not last:
                    sp.wait_ge(s["odd_pe"], n0 + 32)
                    load_gate_up(0, 2 * k + 2)
                if not first:
                    sp.wait_ge(s["odd_pe"], n0 + 64)
                load_down(2 * k)
                if not last:
                    sp.wait_ge(s["hp_ok"], 8 * k + 4)
                    scales(0, 2 * k + 2)

            sp.wait_ge(s["acc_ok"], 32 + 2)
            for j in range(2):
                sp.wait_ge(s[f"wz_out{j}"], 16 * 84 + 16)
            load_gate_up(0, 0)
            scales(0, 0)
            sp_ffn(0, 0, True, False)
            with sp.Fori(1, PAIRS - 1) as k:
                sp_ffn(k, counts_before(k)[0], False, False)
            sp_ffn(PAIRS - 1, counts_before(PAIRS - 1)[0], False, True)
            sp.wait_ge(s["dve_ok"], counts_before(PAIRS)[0] - 32 + 4)
            sp.dma_start(dscl[:, :, :], dtab[:, IT - 2:IT, :]).then_inc(s["dscl_in"], 16)

            def rows_out(j):
                sp.wait_ge(s["f_ok"], j + 1)
                sp.dma_start(out[j // 8, (j % 8) * P:(j % 8) * P + P, :], fo[:, j % 4, :]).then_inc(s[f"out_ok{j % 4}"], 16)

            sp.wait_ge(s["hl_ok"], 8 * PAIRS)
            for i in range(NX):
                if i >= 4:
                    rows_out(i - 4)
                sp.dma_start(xin[:, i % 4, :], x[i // 8, (i % 8) * P:(i % 8) * P + P, :]).then_inc(s[f"xr_in{i % 4}"], 16)
            for j in range(NX - 4, NX):
                rows_out(j)
            for j in range(4):
                sp.wait_ge(s[f"out_ok{j}"], 16 * NX // 4)

        @block.gpsimd
        def _(pool):
            nc.gpsimd.memset(id32[:], 0.0).then_inc(s["ident"], 1)
            nc.gpsimd.memset(id16[:], 0.0).then_inc(s["ident"], 1)
            pool.wait_ge(s["ident"], 2)
            for m in (id32, id16):
                nc.gpsimd.affine_select(out=m[:], in_=m[:], compare_op=ALU.not_equal, fill=1.0, base=0,
                                        pattern=[[-1, P]], channel_multiplier=1).then_inc(s["ident"], 1)
            for i in range(NX):
                pool.wait_ge(s["norm_ok"], i + 1)
                nc.gpsimd.tensor_scalar(xs[:, i, :], xs[:, i, :], 64.0, -64.0, amin, amax).then_inc(s["xc_ok"], 1)
            pool.wait_ge(s["cm_ok"], 1)
            nc.gpsimd.partition_all_reduce(cmr, cm, P, RMAX).then_inc(s["cmr_ok"], 1)
            pool.wait_ge(s["qkv_pe"], 12 * NC)
            pool.wait_ge(s["lq_ok"], 10 * NC + 1)
            nc.gpsimd.memset(kst[96:98, :, :], MU).then_inc(s["const_ok"], 1)
            pool.wait_ge(s["const_ok"], 1)
            nc.gpsimd.memset(vst[:, :, :, 32:64], 1.0).then_inc(s["const_ok"], 1)

            def divide(it, gi):
                pool.wait_ge(s["rc_ok"], 64 * it + 16 * gi + 16)
                nc.gpsimd.tensor_tensor(num[:, gi % 2, :], num[:, gi % 2, :], den[:, gi % 2, :], mult
                                        ).then_inc(s["mu_ok"], 1)

            def tail_of(it, gi):
                pool.wait_ge(s["oh_ok"], 4 * it + gi + 1)
                nc.gpsimd.tensor_tensor(ost[:, gi % 2, 1, :], num[:, gi % 2, :], ost[:, gi % 2, 0, :], sub
                                        ).then_inc(s["ol_ok"], 1)

            def pool_attention(it):
                for gi in range(4):
                    divide(it, gi)
                    tail_of(it, gi)

            with pool.Fori(0, 4) as it:
                pool_attention(it)

            pool.wait_ge(s["pmx_ok"], 1)
            nc.gpsimd.partition_all_reduce(pmr, pmx, P, RMAX).then_inc(s["pmr_ok"], 1)
            pool.wait_ge(s["pmx_ok"], 2)
            nc.gpsimd.partition_all_reduce(pmr2, pmx2, P, RMAX).then_inc(s["pmr_ok"], 1)

            def pool_ffn(kind, before):
                n0, _, _, g0 = before
                for q in BODY[kind][0]:
                    if q["pool"]:
                        if not (kind == "first" and q["g"] < 3):
                            pool.wait_ge(s["pool_ok"], g0 + q["g"] - 2)
                        pool.wait_ge(s["dve_ok"], n0 + q["n"] + 5)
                        to = target(q["t"], q["c"])
                        nc.gpsimd.tensor_tensor(to, to, tmp[:, q["slot"], :], add).then_inc(s["pool_ok"], 1)

            pool_ffn("first", ZERO)
            with pool.Fori(1, PAIRS) as k:
                pool_ffn("full", counts_before(k))
            pool_ffn("last", counts_before(PAIRS))

        @block.scalar
        def _(act):
            A = nc.scalar.activation
            w_sem = [s["w_in0"], s["w_in1"]]

            def evac_x(i):
                act.wait_ge(s["xh_pe"], i + 1)
                A(xT[:, 0, :, i * P:(i + 1) * P], bank16(2 + 2 * (i % 2)).rearrange("p (k c) -> p k c", k=KT),
                  ACT.Copy).then_inc(s["xh_out"], 1)
                act.wait_ge(s["xl_pe"], i + 1)
                A(xT[:, 1, :, i * P:(i + 1) * P], bank16(3 + 2 * (i % 2)).rearrange("p (k c) -> p k c", k=KT),
                  ACT.Copy).then_inc(s["xl_out"], 1)

            for bt in range(4):
                for k in range(3 * bt, 3 * bt + 3):
                    act.wait_ge(w_sem[k % 2], 16 * (k // 2 + 1))
                    if k >= 1:
                        act.wait_ge(s["wT_pe"], k)
                    A(wsg, wraw[:, k % 2, :], ACT.Sign).then_inc(s["sgn_done"], 1)
                act.wait_ge(s["stat_ok"], bt + 1)
                A(sd_, ve, ACT.Sqrt).then_inc(s["std_ok"], 1)
                for i in range(4 * bt, 4 * bt + 4):
                    act.wait_ge(s["xc_ok"], i + 1)
                    if i >= 2:
                        act.wait_ge(s["xh_pe"], i - 1)
                        act.wait_ge(s["l_ok"], i - 1)
                    A(hst[:, i % 2, :], xs[:, i, :], ACT.Copy, scale=fl[:, i:i + 1]).then_inc(s["h_ok"], 1)
                    if i > 4 * bt:
                        evac_x(i - 1)
                evac_x(4 * bt + 3)

            act.sem_inc(s["y_ok"], 6)
            act.wait_ge(s["fac_ok"], 1)
            act.wait_ge(s["z_out"], 16)

            def act_qkv(b2, s2):
                c = 2 * b2 + s2
                for p in range(12):
                    f = QKV[p]
                    act.wait_ge(s["qkv_pe"], 12 * c + p + 1)
                    act.wait_ge(s["r_ok"], 12 * c + p + 1)
                    A(y2[:, p % 2, :], ps[:, p % 6, :], ACT.Copy, scale=cc[:, f:f + 1]).then_inc(s["y_ok"], 1)
                    if p >= 3:
                        head(c, b2, s2, p - 1)
                head(c, b2, s2, 11)

            def head(c, b2, s2, p):
                f = QKV[p]
                act.wait_ge(s["r_ok"], 12 * c + p + 3)
                src, k = (r2[:, p % 2, :], 0 if f < 8 else 1)
                if f < 8:
                    dst = qz[:, bass.ds(b2 * 8 + f, 1), 0, s2 * 512:(s2 + 1) * 512].rearrange("p a c -> p (a c)")
                else:
                    dst = kz[:, bass.ds(b2 * 2 + (f - 8), 1), 0, s2 * 512:(s2 + 1) * 512].rearrange("p a c -> p (a c)")
                act.nop(nofuse=True)
                A(dst, src, ACT.Copy, scale=fac[:, k:k + 1]).then_inc(s["h2_ok"], 1)

            with act.Fori(0, 2) as b2:
                act_qkv(b2, 0)
                act_qkv(b2, 1)

            act.sem_inc(s["exp_ok"], 2)
            act.sem_inc(s["ev_ok"], 8)
            for j in range(2):
                act.sem_inc(s[f"ost_out{j}"], 16)

            def exp_step(n0, e):
                act.wait_ge(s["st_pe"], n0 + e + 1)
                act.wait_ge(s["pv_pe"], n0 + e + 1)
                A(prob[:, e % 2, :].rearrange("p (a c) -> p a c", a=2), ps[:, 2 + 2 * (e % 2):4 + 2 * (e % 2), :],
                  ACT.Exp, scale=gam[:, 0:1]).then_inc(s["exp_ok"], 1)

            exp_step(0, 0)
            exp_step(0, 1)

            def evacuate(it, n, j):
                half, gi = j // 2, n // 4
                rows = slice(32 * (n % 4), 32 * (n % 4) + 32)
                if j == 0:
                    act.wait_ge(s["pv_pe"], 128 * it + 8 * n + 10)
                    if n % 4 == 0:
                        act.wait_ge(s[f"ost_out{gi % 2}"], 32 * it + 16 * (gi // 2) + 16)
                dst = (den if j % 2 else num)[rows, gi % 2, half * 512:(half + 1) * 512]
                r0 = 64 * half + 32 * (j % 2)
                A(dst, ps[r0:r0 + 32, 6 + n % 2, :], ACT.Copy).then_inc(s["ev_ok"], 1)

            def head_of(it, gi):
                act.wait_ge(s["mu_ok"], 4 * it + gi + 1)
                A(ost[:, gi % 2, 0, :], num[:, gi % 2, :], ACT.Copy).then_inc(s["oh_ok"], 1)

            def act_attention(it, last):
                for e in range(STEPS_BODY):
                    n, k = e // 8, e % 8
                    if e + 2 < STEPS_BODY or not last:
                        exp_step(128 * it, e + 2)
                    if n >= 1 and k < 4:
                        evacuate(it, n - 1, k)
                    if e >= 32 and e % 32 == 30:
                        head_of(it, e // 32 - 1)
                for j in range(4):
                    evacuate(it, 15, j)
                head_of(it, 3)

            with act.Fori(0, 3) as it:
                act_attention(it, False)
            act_attention(3, True)

            wo_sem = [s["wo_in0"], s["wo_in1"]]
            for i in range(FQ):
                act.wait_ge(wo_sem[i % 2], 16 * (i // 2 + 1))
                if i >= 2:
                    act.wait_ge(s["woT_pe"], i - 1)
                A(wosg[:, i % 2, :], woraw[:, i % 2, :], ACT.Sign).then_inc(s["wosgn_ok"], 1)
            act.wait_ge(s["co_ok"], 1)
            act.sem_inc(s["yo_ok"], 2)

            def act_oproj(ot, m0):
                for s2 in range(2):
                    act.wait_ge(s["o_pe"], m0 + s2 + 1)
                    act.wait_ge(s["acc_ok"], m0 + s2 + 1)
                    act.nop(nofuse=True)
                    A(yo2[:, s2, :], ps[:, s2, :], ACT.Copy,
                      scale=cc[:, bass.ds(ot + 12, 1)]).then_inc(s["yo_ok"], 1)

            for b in range(2):
                with act.Fori(0, FQ) as ot:
                    act_oproj(ot, ot * 2 + 16 * b)

            act.sem_inc(s["act_ok"], 4)

            def act_ffn(kind, k, before):
                n0, a0, _, g0 = before
                seen = -1
                for ch in BODY[kind][0]:
                    r, c = ch["r"], ch["c"]
                    if r != seen and r in (0, 8, 16):
                        wait_scales(act, r, k)
                    seen = r
                    if ch["kind"] == "a":
                        act.wait_ge(s["even_pe"], n0 + ch["n"] + 1)
                        if ch["freed"]:
                            who, place = ch["freed"]
                            if who == "g":
                                act.wait_ge(s["pool_ok"], g0 + place + 1)
                            else:
                                act.wait_ge(s["dve_ok"], n0 + place + 5)
                        A(tmp[:, ch["slot"], :], ps[:, c, :], ACT.Copy, scale=scale_col(ch["t"], 0)
                          ).then_inc(s["act_ok"], 1)
                    for j, w, hc in h_steps(kind, ch, (0, 2)):
                        act_h(w, j, k, hc, n0, g0)

            def act_h(w, step, k, c, n0, g0):
                u = 1 - w
                g = gu[:, u, 0, c * 512:(c + 1) * 512]
                if step == 0:
                    wait_products(act, w, 0, c, n0, g0)
                    A(g, g, ACT.Silu).then_inc(s["sil_ok"], 1)
                else:
                    act.wait_ge(s["hp_ok"], 8 * k - 4 + 4 * w + c + 1)
                    A(hT[u][:, c, 0, :], g, ACT.Copy).then_inc(s["hh_ok"], 1)

            act_ffn("first", 0, ZERO)
            with act.Fori(1, PAIRS) as k:
                act_ffn("full", k, counts_before(k))
            n_end, _, _, g_end = counts_before(PAIRS)
            for step in (0, 2):
                for c in range(NC):
                    act_h(0, step, PAIRS, c, n_end, g_end)
            act_ffn("last", PAIRS, counts_before(PAIRS))

        @block.vector
        def _(dve):
            V = nc.vector
            ch = Tally(s["chain"])

            def settle():
                dve.wait_ge(s["chain"], ch.value())

            w_sem = [s["w_in0"], s["w_in1"]]
            for bt in range(4):
                dve.wait_ge(s["x_in"], 64 * (bt + 1))
                for k in range(3 * bt, 3 * bt + 3):
                    dve.wait_ge(w_sem[k % 2], 16 * (k // 2 + 1))
                    V.tensor_reduce(ssum[:, k:k + 1], wraw[:, k % 2, :], AX, add,
                                    apply_absolute_value=True).then_inc(s["abs_done"], 1)
                    dve.wait_ge(s["wT_pe"], k + 1)
                    V.tensor_copy(wT[:, :, k * P:(k + 1) * P],
                                  bank16(k % 2).rearrange("p (k c) -> p k c", k=KT)).then_inc(s["wT_out"], 1)
                for i in range(4 * bt, 4 * bt + 4):
                    ch.inc(V.bn_stats(bn[:, i, 0:6], xs[:, i, 0:512]))
                    ch.inc(V.bn_stats(bn[:, i, 6:12], xs[:, i, 512:1024]))
                settle()
                for i in range(4 * bt, 4 * bt + 4):
                    ch.inc(V.bn_aggr(mv[:, i, :], bn[:, i, :]))
                settle()
                b4 = slice(4 * bt, 4 * bt + 4)
                V.tensor_scalar(ve, mv[:, b4, 1], EPS, None, add).then_inc(s["stat_ok"], 1)
                ch.inc(V.tensor_scalar(fl[:, b4], mv[:, b4, 1], 0.0, 0.0, mult, iseq))
                ch.inc(V.tensor_scalar(mark[:, b4], mv[:, b4, 0], 0.0, None, mult))
                settle()
                ch.inc(V.tensor_scalar(fl[:, b4], fl[:, b4], XS, None, mult))
                dve.wait_ge(s["std_ok"], bt + 1)
                ch.inc(V.reciprocal(rs, sd_))
                settle()
                ch.inc(V.tensor_tensor(t4, rs, rs, mult))
                settle()
                ch.inc(V.tensor_tensor(t4, t4, ve, mult))
                settle()
                ch.inc(V.tensor_scalar(t4, t4, -0.5, 1.5, mult, add))
                settle()
                ch.inc(V.tensor_tensor(rs, rs, t4, mult))
                settle()
                for i in range(4 * bt, 4 * bt + 4):
                    V.tensor_scalar(xs[:, i, :], xs[:, i, :], mv[:, i, 0:1], rs[:, i % 4:i % 4 + 1], sub, mult
                                    ).then_inc(s["norm_ok"], 1)
                for i in range(4 * bt, 4 * bt + 4):
                    dve.wait_ge(s["h_ok"], i + 1)
                    if i >= 2:
                        dve.wait_ge(s["xl_pe"], i - 1)
                    V.scalar_tensor_tensor(lst[:, i % 2, :], xs[:, i, :], fl[:, i:i + 1], hst[:, i % 2, :],
                                           mult, sub).then_inc(s["l_ok"], 1)

            dve.wait_ge(s["znat_in"], 48)
            V.tensor_copy(zf16, znat).then_inc(s["z_ok"], 1)
            dve.wait_ge(s["par_in"], 64)
            dve.wait_ge(s["abs_done"], NW)

            def channel_scales(a, b):
                ch.inc(V.tensor_scalar(cc[:, a:b], ssum[:, a:b], 1.0 / H, 1e-8, mult, amax))
                settle()
                ch.inc(V.tensor_tensor(cc[:, a:b], cc[:, a:b], spar[:, a:b], mult))
                settle()
                ch.inc(V.tensor_scalar(cc[:, a:b], cc[:, a:b], FMAX, -FMAX, amin, amax))
                settle()

            channel_scales(0, 12)
            ch.inc(V.tensor_scalar(cc[:, 0:12], cc[:, 0:12], 1.0 / XS, None, mult))
            settle()
            for j, (a, b) in enumerate(((0, 8), (8, 10), (10, 12))):
                ins = V.tensor_reduce(cm[:, j:j + 1], cc[:, a:b], AX, amax, apply_absolute_value=True)
                if j < 2:
                    ch.inc(ins)
                else:
                    ins.then_inc(s["cm_ok"], 1)
            dve.wait_ge(s["cmr_ok"], 1)
            ch.inc(V.tensor_scalar(cmr, cmr, 1e-30, None, amax))
            settle()
            ch.inc(V.reciprocal(fac, cmr))
            ch.inc(V.tensor_tensor(gam, cmr[:, 0:1], cmr[:, 1:2], mult))
            settle()
            ch.inc(V.tensor_scalar(gam, gam, (256.0 * 1024.0 / QB) ** 2 / float(D) ** 0.5, None, mult))
            V.tensor_scalar(fac, fac, QB / (256.0 * 1024.0), None, mult).then_inc(s["fac_ok"], 1)
            def guard(y, r, f):
                ch.inc(V.tensor_scalar(r, y, 1e6, -1e6, amin, amax))
                ch.inc(V.tensor_scalar(f, y, 0.0, 0.0, mult, iseq))
                settle()
                dve.nop(nofuse=True)
                return V.copy_predicated(r, f, y)

            dve.sem_inc(s["lq_ok"], 1)
            dve.sem_inc(s["r_ok"], 2)
            ch0 = ch.value()

            def dve_qkv(b2, s2):
                c = 2 * b2 + s2
                for p in range(12):
                    dve.wait_ge(s["y_ok"], 12 * c + p + 7)
                    dve.wait_ge(s["r_ok"], 12 * c + p + 2)
                    if p >= 2:
                        dve.wait_ge(s["lq_ok"], 10 * c + max(p - 3, 0) + 1)
                    dst = rv2[:, p, :] if p < 2 else r2[:, p % 2, :]
                    guard(y2[:, p % 2, :], dst, fin).then_inc(s["r_ok"], 1)
                    if p < 2:
                        dve.wait_ge(s["r_ok"], 12 * c + p + 3)
                        V.tensor_scalar(dst, dst, fac[:, 2:3], None, mult).then_inc(s["vr_ok"], 1)
                    if p >= 3:
                        tail(c, b2, s2, p - 1)
                    if p == 7:
                        for fv in range(2):
                            dve.wait_ge(s["v_pe"], 2 * c + fv + 1)
                            src = ps[:, 6 + fv, :].rearrange("p (t g d) -> p g t d", t=4, g=4)
                            to = vz[:, bass.ds(b2 * 8 + fv * 4, 4), 4 * s2:4 * s2 + 4, :]
                            dve.nop(nofuse=True)
                            V.tensor_copy(to, src).then_inc(s["v_out"], 1)
                tail(c, b2, s2, 11)

            def tail(c, b2, s2, p):
                f = QKV[p]
                dve.wait_ge(s["h2_ok"], 10 * c + p - 1)
                k = 0 if f < 8 else 1
                z, f0 = (qz, b2 * 8 + f) if f < 8 else (kz, b2 * 2 + (f - 8))
                hd = z[:, bass.ds(f0, 1), 0, s2 * 512:(s2 + 1) * 512].rearrange("p a c -> p (a c)")
                to = z[:, bass.ds(f0, 1), 1, s2 * 512:(s2 + 1) * 512].rearrange("p a c -> p (a c)")
                V.scalar_tensor_tensor(to, r2[:, p % 2, :], fac[:, k:k + 1], hd, mult, sub).then_inc(s["lq_ok"], 1)

            with dve.Fori(0, 2) as b2:
                ch.enter(ch0, b2, 48)
                dve_qkv(b2, 0)
                dve_qkv(b2, 1)
                assert ch.n == 48
            ch.leave(ch0 + 24 * NC)


            def row_max(i0, i, par, qt):
                dve.wait_ge(s["s_pe"], i0 + i + 1)
                V.tensor_reduce(mxs[:, par, qt:qt + 1], ps[:, 0:2, :].rearrange("p a c -> p (a c)"), AX, amax
                                ).then_inc(s["max_ok"], 1)

            def split_max(i0, i, par):
                dve.wait_ge(s["max_ok"], i0 + i + 1)
                ch.inc(V.tensor_scalar(mhl[:, 0:8], mxs[:, par, :], -1.0 / MU, None, mult))
                settle()
                V.scalar_tensor_tensor(mhl[:, 8:16], mxs[:, par, :], -1.0 / MU, mhl[:, 0:8], mult, sub
                                       ).then_inc(s["mhl_ok"], 1)

            def copy_rows(count, par, bank):
                dve.wait_ge(s["m_pe"], count)
                V.tensor_copy(mrow[0:16, par, :], ps[0:16, bank, 0:64].bitcast(f16)).then_inc(s["mrow_ok"], 1)

            for hd in range(2):
                for i in range(8):
                    row_max(0, 8 * hd + i, hd, i)
                split_max(0, 8 * hd + 7, hd)
                copy_rows(hd + 1, hd, 6 + hd)
            for i in range(4):
                row_max(0, 16 + i, 0, i)
            cha = ch.value()

            def dequantise(it, p):
                dve.wait_ge(s["piece_in"], 32 * (42 * it + p + 1))
                V.tensor_tensor(zst[:, p % 2, :], wst, zst[:, p % 2, :], sub).then_inc(s["sub_ok"], 1)

            def invert(it, gi, i):
                if i == 0:
                    dve.wait_ge(s["ev_ok"], 64 * it + 16 * gi + 24)
                d = den[:, gi % 2, 64 * i:64 * i + 64]
                V.reciprocal(d, d).then_inc(s["rc_ok"], 1)

            def dve_attention(it, last):
                left = []
                for e in range(STEPS_BODY):
                    n, k = e // 8, e % 8
                    hd, qt = (n + 2, 4 + k) if k < 4 else (n + 3, k - 4)
                    if not (last and hd > 15):
                        row_max(128 * it, LEAD_S + e, hd % 2, qt)
                        if k == 3:
                            split_max(128 * it, LEAD_S + e, hd % 2)
                    if k == 5 and not (last and n + 2 > 15):
                        copy_rows(16 * it + n + 3, n % 2, 6 + (n + 1) % 2)
                    if e % 32 == 4 and e >= 32:
                        left = [(e // 32 - 1, i) for i in range(16)]
                    if e % 3 == 0 and e // 3 < 42:
                        dequantise(it, e // 3)
                    elif left:
                        invert(it, *left.pop(0))
                assert not left
                for i in range(16):
                    invert(it, 3, i)

            CHA = 16
            with dve.Fori(0, 3) as it:
                ch.enter(cha, it, CHA)
                dve_attention(it, False)
                assert ch.n == CHA, ch.n
            ch.leave(cha + 3 * CHA)
            dve_attention(3, True)

            wo_sem = [s["wo_in0"], s["wo_in1"]]
            for i in range(FQ):
                dve.wait_ge(wo_sem[i % 2], 16 * (i // 2 + 1))
                V.tensor_reduce(ssum[:, 12 + i:13 + i], woraw[:, i % 2, :], AX, add,
                                apply_absolute_value=True).then_inc(s["woabs_ok"], 1)
                dve.wait_ge(s["woT_pe"], i + 1)
                V.tensor_copy(woT[:, :, i * P:(i + 1) * P],
                              bank16(2 + i % 2).rearrange("p (k c) -> p k c", k=KT)).then_inc(s["woT_out"], 1)
            dve.wait_ge(s["woabs_ok"], FQ)
            channel_scales(12, 20)
            ch.inc(V.tensor_scalar(fac[:, 2:3], cmr[:, 2:3], 256.0 * 1024.0 / QB, None, mult))
            settle()
            V.tensor_scalar(cc[:, 12:20], cc[:, 12:20], fac[:, 2:3], None, mult).then_inc(s["co_ok"], 1)
            dve.wait_ge(s["snat_pe"], 1)
            for j in range(2):
                dve.wait_ge(s[f"wz_out{j}"], 16 * 84 + 16)
            for m in range(2):
                ch.inc(V.tensor_scalar(tab[:, :, m * KT:(m + 1) * KT].rearrange("p t g -> p g t"),
                                       ps[:, 6, m * 224:(m + 1) * 224].rearrange("p (g t) -> p g t", g=KT),
                                       1.0 / XS, None, mult))
            ch.inc(V.tensor_copy(dtab[:, :, :].rearrange("p t o -> p o t"),
                                 ps[:, 7, 0:224].rearrange("p (o t) -> p o t", o=FQ)))
            settle()
            V.tensor_reduce(pmx, tab[:, :, 0:KT], AX, amax, apply_absolute_value=True).then_inc(s["pmx_ok"], 1)
            V.tensor_reduce(pmx2, tab[:, :, KT:2 * KT], AX, amax, apply_absolute_value=True).then_inc(s["pmx_ok"], 1)
            dve.wait_ge(s["pmr_ok"], 2)
            ch.inc(V.tensor_tensor(pmr, pmr, pmr2, mult))
            settle()
            ch.inc(V.tensor_scalar(pmr, pmr, XS * XS, 1e-30, mult, amax))
            settle()
            ch.inc(V.reciprocal(pmx, pmr))
            settle()
            ch.inc(V.tensor_scalar(tab[:, :, 16], pmx, 2.0 ** -12, None, mult))
            ch.inc(V.tensor_scalar(pmr, pmr, 2.0 ** 12, None, mult))
            settle()
            for o in range(FQ):
                ch.inc(V.tensor_tensor(dtab[:, :, o], dtab[:, :, o], pmr, mult))
            settle()

            dve.sem_inc(s["acc_ok"], 2)
            cho = ch.value()

            def dve_oproj(ot, m0, b):
                for s2 in range(2):
                    dve.wait_ge(s["yo_ok"], m0 + s2 + 3)
                    dve.wait_ge(s["acc_ok"], m0 + s2 + 2)
                    ch.inc(guard(yo2[:, s2, :], ro, fino))
                    settle()
                    dve.nop(nofuse=True)
                    V.tensor_copy(acc[b][:, bass.ds(ot, 1), s2 * 512:(s2 + 1) * 512].rearrange("p a c -> p (a c)"), ro
                                  ).then_inc(s["acc_ok"], 1)

            for b in range(2):
                with dve.Fori(0, FQ) as ot:
                    ch.enter(cho + 48 * b, ot, 6)
                    dve_oproj(ot, ot * 2 + 16 * b, b)
                    assert ch.n == 6
            ch.leave(cho + 96)

            dve.sem_inc(s["dve_ok"], 4)

            def dve_ffn(kind, k, before):
                n0, a0, b0, g0 = before
                seen, every = -1, BODY[kind][0]
                for i, q in enumerate(every):
                    r, c, t = q["r"], q["c"], q["t"]
                    if r != seen and r in (0, 8, 16):
                        wait_scales(dve, r, k)
                    seen = r
                    if c == 0:
                        for own in every[i:i + NC]:
                            if own["kind"] == "b":
                                to = target(t, own["c"])
                                dve.wait_ge(s["dve_ok"], n0 + own["n"] + 1)
                                dve.wait_ge(s["even_pe"], n0 + own["n"] + 1)
                                V.scalar_tensor_tensor(to, ps[:, own["c"], :], scale_col(t, 0), to, mult, add
                                                       ).then_inc(s["evb_ok"], 1)
                    rest = to = target(t, c)
                    if q["kind"] == "b":
                        dve.wait_ge(s["evb_ok"], b0 + q["b"] + 1)
                    else:
                        rest = tmp[:, q["slot"], :]
                        dve.wait_ge(s["act_ok"], a0 + q["a"] + 5)
                        if q["pool"]:
                            to = rest
                    dve.wait_ge(s["odd_pe"], n0 + q["n"] + 1)
                    V.scalar_tensor_tensor(to, ps[:, 4 + c, :], scale_col(t, 1), rest, mult, add
                                           ).then_inc(s["dve_ok"], 1)
                    for j, w, hc in h_steps(kind, q, (1, 3)):
                        dve_h(w, j, k, hc, n0, g0)

            def dve_h(w, step, k, c, n0, g0):
                u = 1 - w
                g, up = (gu[:, u, m, c * 512:(c + 1) * 512] for m in range(2))
                n = 8 * k - 4 + 4 * w + c + 1
                if step == 1:
                    wait_products(dve, w, 1, c, n0, g0)
                    dve.wait_ge(s["sil_ok"], n)
                    V.scalar_tensor_tensor(g, g, scl[:, u, 16:17], up, mult, mult).then_inc(s["hp_ok"], 1)
                else:
                    dve.wait_ge(s["hh_ok"], n)
                    V.tensor_tensor(hT[u][:, c, 1, :], g, hT[u][:, c, 0, :], sub).then_inc(s["hl_ok"], 1)

            dve_ffn("first", 0, ZERO)
            with dve.Fori(1, PAIRS) as k:
                dve_ffn("full", k, counts_before(k))
            n_end, _, _, g_end = counts_before(PAIRS)
            for step in (1, 3):
                for c in range(NC):
                    dve_h(0, step, PAIRS, c, n_end, g_end)
            dve_ffn("last", PAIRS, counts_before(PAIRS))

            for i in range(NX):
                dve.wait_ge(s["t_pe"], i + 1)
                dve.wait_ge(s[f"xr_in{i % 4}"], 16 * (i // 4 + 1))
                if i >= 4:
                    dve.wait_ge(s[f"out_ok{i % 4}"], 16 * (i // 4))
                V.scalar_tensor_tensor(fo[:, i % 4, :].rearrange("p (a c) -> p a c", a=2),
                                       ps[:, 2 * (i % 4):2 * (i % 4) + 2, :], mark[:, i:i + 1],
                                       xin[:, i % 4, :].rearrange("p (a c) -> p a c", a=2), add, add
                                       ).then_inc(s["f_ok"], 1)

        @block.tensor
        def _(pe):
            MM = nc.tensor.matmul
            TR = nc.tensor.transpose
            pe.wait_ge(s["ident"], 4)
            for bt in range(4):
                for k in range(3 * bt, 3 * bt + 3):
                    pe.wait_ge(s["sgn_done"], k + 1)
                    if k >= 2:
                        pe.wait_ge(s["wT_out"], k - 1)
                    for t in range(KT):
                        last = TR(bank16(k % 2)[:, t * P:(t + 1) * P], wsg[:, t * P:(t + 1) * P], id16[:])
                    last.then_inc(s["wT_pe"], 1)
                for i in range(4 * bt, 4 * bt + 4):
                    for part, st_, ok, done, free in ((0, hst, "h_ok", "xh_pe", "xh_out"),
                                                      (1, lst, "l_ok", "xl_pe", "xl_out")):
                        pe.wait_ge(s[ok], i + 1)
                        if i >= 2:
                            pe.wait_ge(s[free], i - 1)
                        for t in range(KT):
                            last = TR(bank16(2 + 2 * (i % 2) + part)[:, t * P:(t + 1) * P],
                                      st_[:, i % 2, t * P:(t + 1) * P], id16[:])
                        last.then_inc(s[done], 1)
            pe.wait_ge(s["wT_out"], NW)
            pe.wait_ge(s["xh_out"], NX)
            pe.wait_ge(s["xl_out"], NX)

            def pe_qkv(c):
                for p in range(12):
                    f = QKV[p]
                    pe.wait_ge(s["y_ok"], 12 * c + p + 1)
                    for kt in range(KT):
                        for part in range(2):
                            last = MM(ps[:, p % 6, :], wT[:, kt, f * P:(f + 1) * P],
                                      xT[:, part, kt, bass.ds(c * 512, 512)],
                                      start=(kt == 0 and part == 0), stop=(kt == KT - 1 and part == 1))
                    last.then_inc(s["qkv_pe"], 1)
                    if p == 5:
                        for fv in range(2):
                            pe.wait_ge(s["vr_ok"], 2 * c + fv + 1)
                            for t in range(4):
                                last = TR(ps[:, 6 + fv, t * P:(t + 1) * P], rv2[:, fv, t * P:(t + 1) * P], id32[:])
                            last.then_inc(s["v_pe"], 1)

            with pe.Fori(0, NC) as c:
                pe_qkv(c)

            pe.sem_inc(s["pv_pe"], 2)

            def row_scores(i0, i, qbuf, kbuf, qt):
                if not (isinstance(i0, int) and i0 + i == 0):
                    pe.wait_ge(s["max_ok"], i0 + i)
                for h2 in range(2):
                    last = MM(ps[:, h2, :], qst[0:96, qbuf, qt * P:(qt + 1) * P],
                              kst[0:96, kbuf, h2 * 512:(h2 + 1) * 512], start=True, stop=True)
                last.then_inc(s["s_pe"], 1)

            def maxima_rows(count, bank):
                pe.wait_ge(s["mhl_ok"], count)
                TR(ps[0:16, bank, 0:64].bitcast(f16), mhl[:, 0:16], id16[:]).then_inc(s["m_pe"], 1)

            def key_scores(n0, e, qbuf, kbuf):
                kt = e % 8
                pe.wait_ge(s["exp_ok"], n0 + e + 1)
                for a in range(2):
                    last = MM(ps[:, 2 + 2 * (e % 2) + a, :], kst[0:98, kbuf, kt * P:(kt + 1) * P],
                              qst[0:98, qbuf, a * 512:(a + 1) * 512], start=True, stop=True)
                last.then_inc(s["st_pe"], 1)

            pe.wait_ge(s["y_ok"], 12 * NC + 6)
            pe.wait_ge(s["v_out"], 2 * NC)
            pe.wait_ge(s["k_in0"], 48)
            for hd in range(2):
                pe.wait_ge(s[f"q_in{hd}"], 48)
                for i in range(8):
                    row_scores(0, 8 * hd + i, hd, 0, i)
                maxima_rows(hd + 1, 6 + hd)
            pe.wait_ge(s["q_in2"], 48)
            for i in range(4):
                row_scores(0, 16 + i, 2, 0, i)
            pe.wait_ge(s["m_in0"], 32)
            for e in range(2):
                key_scores(0, e, 0, 0)

            def pe_attention(it, last_body):
                for e in range(STEPS_BODY):
                    n, k, gi = e // 8, e % 8, e // 32
                    if n % 4 == 0 and k == 0:
                        pe.wait_ge(s[f"v_in{gi % 2}"], 32 * it + 16 * (gi // 2) + 16)
                    if k == 0:
                        pe.wait_ge(s["ev_ok"], 64 * it + 4 * n + 4)
                        pe.wait_ge(s["mrow_ok"], 16 * it + n + 2 if not (last_body and n == 15) else 64)
                    pe.wait_ge(s["exp_ok"], 128 * it + e + 3)
                    for a in range(2):
                        last = MM(ps[64 * a:64 * a + 64, 6 + n % 2, :], vst[:, gi % 2, k, :],
                                  prob[:, e % 2, a * 512:(a + 1) * 512], start=(k == 0), stop=(k == 7))
                    last.then_inc(s["pv_pe"], 1)
                    e2 = e + 2
                    if e2 < STEPS_BODY or not last_body:
                        n2 = e2 // 8
                        if e2 % 8 == 0:
                            pe.wait_ge(s[f"m_in{n2 % 4}"], 128 * it + 32 * (n2 // 4) + 32)
                        key_scores(128 * it, e2, n2 % 4, (n2 // 4) % 2)
                    hd, qt = (n + 2, 4 + k) if k < 4 else (n + 3, k - 4)
                    if not (last_body and hd > 15):
                        if qt == 0:
                            pe.wait_ge(s[f"q_in{hd % 4}"], 192 * it + 48 * (hd // 4) + 48)
                            if hd % 4 == 0:
                                pe.wait_ge(s[f"k_in{(hd // 4) % 2}"], 96 * it + 48 * (hd // 8) + 48)
                        row_scores(128 * it, LEAD_S + e, hd % 4, (hd // 4) % 2, qt)
                    if k == 5 and not (last_body and n + 2 > 15):
                        pe.wait_ge(s["ev_ok"], 64 * it + 4 * n + 8)
                        maxima_rows(16 * it + n + 3, 6 + (n + 1) % 2)

            with pe.Fori(0, 3) as it:
                pe_attention(it, False)
            pe_attention(3, True)

            pe.wait_ge(s["ev_ok"], 64 * 4 + 8)
            pe.wait_ge(s["snat_in"], 48)
            for m, nat in enumerate((snat_g, snat_u)):
                for g in range(KT):
                    TR(ps[:, 6, m * 224 + g * IT:m * 224 + (g + 1) * IT], nat[:, g, :], id32[0:IT, 0:IT])
            for o in range(FQ):
                last = TR(ps[:, 7, o * IT:(o + 1) * IT], snat_d[:, o * P:(o + 1) * P], id32[0:IT, 0:IT])
            last.then_inc(s["snat_pe"], 1)

            for i in range(FQ):
                pe.wait_ge(s["wosgn_ok"], i + 1)
                if i >= 2:
                    pe.wait_ge(s["woT_out"], i - 1)
                for t in range(KT):
                    last = TR(bank16(2 + i % 2)[:, t * P:(t + 1) * P], wosg[:, i % 2, t * P:(t + 1) * P], id16[:])
                last.then_inc(s["woT_pe"], 1)
            pe.wait_ge(s["woT_out"], FQ)
            for j in range(2):
                pe.wait_ge(s[f"ost_out{j}"], 16 * 9)

            def pe_oproj(ot, m0, b):
                for s2 in range(2):
                    pe.wait_ge(s["yo_ok"], m0 + s2 + 1)
                    pe.nop(nofuse=True)
                    for kt in range(KT):
                        for part in range(2):
                            last = MM(ps[:, s2, :], woT[:, kt, bass.ts(ot, P)],
                                      qz[:, 8 * b + kt, part, s2 * 512:(s2 + 1) * 512],
                                      start=(kt == 0 and part == 0), stop=(kt == KT - 1 and part == 1))
                    last.then_inc(s["o_pe"], 1)

            for b in range(2):
                with pe.Fori(0, FQ) as ot:
                    pe_oproj(ot, ot * 2 + 16 * b, b)

            def pe_ffn(kind, k, before):
                n0, a0, b0, _ = before
                every = BODY[kind][0]
                for i in range(0, len(every), NC):
                    r, t = every[i]["r"], every[i]["t"]
                    if r == 0:
                        pe.wait_ge(s["wgu_in0"], 16 * k + 16)
                    if r == 8:
                        pe.wait_ge(s["wd_in"], 16 * k)
                        pe.wait_ge(s["hl_ok"], 8 * k - 4)
                    if r == 16:
                        pe.wait_ge(s["wgu_in1"], 16 * k + 16)
                    for odd in range(2):
                        for c in range(NC):
                            q = every[i + c]
                            who, place = q["bank"]
                            if odd:
                                pe.wait_ge(s["dve_ok"], n0 + q["n"] + 1)
                                if r == 8:
                                    pe.wait_ge(s["hl_ok"], 8 * k - 3 + c)
                            elif who == "a":
                                pe.wait_ge(s["act_ok"], a0 + place + 5)
                            else:
                                pe.wait_ge(s["evb_ok"], b0 + place + 1)
                            for part in range(2):
                                if t[0] == "gu":
                                    g = 2 * t[3] + odd
                                    lhsT = wf[:, t[1], t[2], g * P:(g + 1) * P]
                                    rhs = xT[:, part, g, c * 512:(c + 1) * 512]
                                else:
                                    lhsT = wf[:, odd, 2, t[1] * P:(t[1] + 1) * P]
                                    rhs = hT[odd][:, c, part, :]
                                last = MM(ps[:, 4 * odd + c, :], lhsT, rhs, start=(part == 0), stop=(part == 1))
                            last.then_inc(s["odd_pe" if odd else "even_pe"], 1)

            pe.wait_ge(s["yo_ok"], 2 + 32)
            pe_ffn("first", 0, ZERO)
            with pe.Fori(1, PAIRS) as k:
                pe_ffn("full", k, counts_before(k))
            pe_ffn("last", PAIRS, counts_before(PAIRS))

            pe.wait_ge(s["dve_ok"], counts_before(PAIRS)[0] + BODY["last"][1][0] + 4)
            pe.wait_ge(s["pool_ok"], counts_before(PAIRS)[3] + BODY["last"][1][3])
            for i in range(NX):
                b, c0 = i // 8, (i % 8) * P
                if i >= 4:
                    pe.wait_ge(s["f_ok"], i - 3)
                for o in range(FQ):
                    last = TR(ps[:, 2 * (i % 4) + o // 4, (o % 4) * P:(o % 4 + 1) * P], acc[b][:, o, c0:c0 + P], id32[:])
                last.then_inc(s["t_pe"], 1)


_INS = ['L0_attn_hidden_states', 'L0_attn_q_weight', 'L0_attn_q_scale', 'L0_attn_k_weight', 'L0_attn_k_scale',
        'L0_attn_v_weight', 'L0_attn_v_scale', 'L0_attn_o_weight', 'L0_attn_o_scale',
        'L0_ffn_gate_w', 'L0_ffn_gate_z', 'L0_ffn_gate_s', 'L0_ffn_up_w', 'L0_ffn_up_z', 'L0_ffn_up_s',
        'L0_ffn_down_w', 'L0_ffn_down_z', 'L0_ffn_down_s']


def kernel(**inputs):
    import numpy as _np
    import concourse.bacc as _bacc
    from concourse import mybir as _mybir
    from concourse.bass_utils import run_bass_kernel_spmd as _run

    nc = _bacc.Bacc("TRN2", target_bir_lowering=False, num_devices=1)
    arrays, args = {}, []
    for name in _INS:
        a = _np.ascontiguousarray(inputs[name])
        arrays[f"in_{name}_dram"] = a
        args.append(nc.dram_tensor(f"in_{name}_dram", a.shape, _mybir.dt.from_np(a.dtype), kind="ExternalInput").ap())
    args.append(nc.dram_tensor("out_0_dram", (2, 1024, 1024), _mybir.dt.float32, kind="ExternalOutput").ap())
    args.append(nc.dram_tensor("zero_points", (28, 3, 1024), _mybir.dt.float16, kind="Internal").ap())
    args.append(nc.dram_tensor("dequantised", (28, 3, 128, 1024), _mybir.dt.float16, kind="Internal").ap())
    layer_kernel(nc, *args)
    r = _run(nc, [arrays], core_ids=[0])
    return r.results[0]["out_0_dram"]
```

```python
import concourse.bass as bass
from concourse import mybir
from contextlib import ExitStack


P = 128
T, H = 2048, 1024
S = 1024
KT = H // P
I = 3584
IT = I // P
PAIRS = IT // 2
D = 32
FQ, FK = 8, 2
NC = T // 512
NX = T // P
EPS = 1e-5
FMAX = 3.4028234663852886e38
XS = 256.0
QB = 4096.0
MU = 16384.0
HEADS_BODY, STEPS_BODY = 16, 128
LEAD_S = 20


RMAX = bass.bass_isa.ReduceOp.max


class Tally:

    def __init__(self, sem):
        self.sem, self.base, self.n = sem, 0, 0

    def inc(self, ins):
        self.n += 1
        return ins.then_inc(self.sem, 1)

    def value(self):
        return self.base + self.n

    def enter(self, start, i, per):
        self.base, self.n = start + i * per, 0

    def leave(self, total):
        self.base, self.n = 0, total


def layer_kernel(nc, x, wq, sq, wk, sk, wv, sv, wo, so, gw, gz, gs, uw, uz, us, dw, dz, ds, out, zscr, wscr):
    f32, f16, i32 = mybir.dt.float32, mybir.dt.float16, mybir.dt.int32
    ALU = mybir.AluOpType
    ACT = mybir.ActivationFunctionType
    AX = mybir.AxisListType.X
    add, sub, mult, amin, amax, iseq = ALU.add, ALU.subtract, ALU.mult, ALU.min, ALU.max, ALU.is_equal

    ctx = ExitStack()
    with ctx:
        def sb(name, shape, dt=f32):
            return ctx.enter_context(nc.sbuf_tensor(name, shape, dt))

        def sem(name):
            return ctx.enter_context(nc.semaphore(name))

        xT = sb("xT", [P, 2, KT, T], f16)
        zone_a = sb("zone_a", [P, 64 * 256])
        zone_b = sb("zone_b", [P, 75 * 256])

        def view(zone, kb, words, dt=f32):
            v = zone[:, kb * 256:kb * 256 + words]
            return v if dt == f32 else v.bitcast(dt)

        xs = view(zone_a, 0, 16384).rearrange("p (n c) -> p n c", n=NX)
        znat = view(zone_b, 12, 3072, i32)[0:IT, :]
        zf16 = view(zone_b, 24, 1536, f16)[0:IT, :]
        bn = view(zone_b, 30, NX * 12).rearrange("p (n c) -> p n c", n=NX)
        wT = view(zone_b, 32, 6144, f16).rearrange("p (k c) -> p k c", k=KT)
        hst = view(zone_b, 56, 1024, f16).rearrange("p (n c) -> p n c", n=2)
        lst = view(zone_b, 60, 1024, f16).rearrange("p (n c) -> p n c", n=2)
        wraw = view(zone_b, 64, 2048).rearrange("p (n c) -> p n c", n=2)
        wsg = view(zone_b, 72, 512, f16)
        y2 = view(zone_b, 56, 1024).rearrange("p (n c) -> p n c", n=2)
        r2 = view(zone_b, 60, 1024).rearrange("p (n c) -> p n c", n=2)
        rv2 = view(zone_b, 64, 1024).rearrange("p (n c) -> p n c", n=2)
        fin = view(zone_b, 68, 512, i32)
        qz = view(zone_a, 0, 16384, f16).rearrange("p (g h c) -> p g h c", g=16, h=2)
        vz = view(zone_b, 0, 4096).rearrange("p (g k d) -> p g k d", g=16, k=8)
        kz = view(zone_b, 16, 4096, f16).rearrange("p (n h c) -> p n h c", n=4, h=2)
        qst = view(zone_b, 32, 2048, f16).rearrange("p (n c) -> p n c", n=4)
        kst = view(zone_b, 40, 1024, f16).rearrange("p (n c) -> p n c", n=2)
        vst = view(zone_b, 44, 1024).rearrange("p (n k d) -> p n k d", n=2, k=8)
        prob = view(zone_b, 48, 2048).rearrange("p (n c) -> p n c", n=2)
        num = view(zone_b, 56, 2048).rearrange("p (n c) -> p n c", n=2)
        den = view(zone_b, 64, 2048).rearrange("p (n c) -> p n c", n=2)
        ost = view(zone_b, 64, 2048, f16).rearrange("p (n h c) -> p n h c", n=2, h=2)
        wst = view(zone_b, 72, 512, i32)
        acc = [view(zone_b, 0, 8192).rearrange("p (o c) -> p o c", o=FQ),
               view(zone_a, 0, 8192).rearrange("p (o c) -> p o c", o=FQ)]
        woT = view(zone_b, 32, 4096, f16).rearrange("p (k c) -> p k c", k=KT)
        yo2 = view(zone_b, 48, 1024).rearrange("p (n c) -> p n c", n=2)
        ro = view(zone_b, 52, 512)
        fino = view(zone_b, 54, 512, i32)
        woraw = view(zone_b, 48, 2048).rearrange("p (n c) -> p n c", n=2)
        wosg = view(zone_b, 64, 1024, f16).rearrange("p (n c) -> p n c", n=2)
        snat_g = view(zone_b, 0, 1024)[0:IT, :].rearrange("t (g c) -> t g c", g=KT)
        snat_u = view(zone_b, 4, 1024)[0:IT, :].rearrange("t (g c) -> t g c", g=KT)
        snat_d = view(zone_b, 8, 1024)[0:IT, :]
        gu = view(zone_a, 32, 8192).rearrange("p (u m c) -> p u m c", u=2, m=2)
        tmp = view(zone_b, 32, 4096).rearrange("p (n c) -> p n c", n=8)
        hT = [view(zone_b, 48, 2048, f16).rearrange("p (c h n) -> p c h n", c=NC, h=2),
              view(zone_a, 32 + 24, 2048, f16).rearrange("p (c h n) -> p c h n", c=NC, h=2)]
        wf = view(zone_b, 56, 3072, f16).rearrange("p (u m c) -> p u m c", u=2, m=3)
        xin = xT[:].rearrange("p h k t -> p (h k t)").bitcast(f32).rearrange("p (n c) -> p n c", n=NX)
        fo = view(zone_a, 48, 4096).rearrange("p (n c) -> p n c", n=4)
        id32 = sb("id32", [P, P])
        id16 = sb("id16", [P, P], f16)
        zone_c = sb("zone_c", [P, 750])
        zst = zone_c[:, 0:512].bitcast(f16).rearrange("p (n c) -> p n c", n=2)
        mrow = zone_c[:, 512:640].bitcast(f16).rearrange("p (n c) -> p n c", n=2)
        tab = zone_c[:, 0:IT * 17].rearrange("p (t c) -> p t c", t=IT)
        dtab = zone_c[:, IT * 17:IT * 25].rearrange("p (t c) -> p t c", t=IT)
        sm = sb("sm", [P, 274])

        def cols(a, n):
            return sm[:, a:a + n]

        ssum, spar, cc = cols(0, 20), cols(20, 20), cols(40, 20)
        mv = cols(60, 32).rearrange("p (n c) -> p n c", n=NX)
        ve, sd_, rs, t4 = cols(92, 4), cols(96, 4), cols(100, 4), cols(104, 4)
        fl, mark = cols(108, NX), cols(124, NX)
        cm, cmr, fac, gam = cols(140, 3), cols(143, 3), cols(146, 3), cols(149, 1)
        mxs = cols(150, 32).rearrange("p (n h c) -> p n h c", n=2, h=2)
        mhl = cols(182, 8).bitcast(f16)
        pmx, pmx2, pmr = (cols(190 + 28 * j, 28) for j in range(3))
        pmr2 = cols(60, 28)
        scl = zone_c[:, 700:734].rearrange("p (u c) -> p u c", u=2)
        dscl = zone_c[:, 734:750].rearrange("p (u c) -> p u c", u=2)

        ps = ctx.enter_context(nc.psum_tensor("ps", [P, 8, 512], f32))

        def bank16(b):
            return ps[:, b, :].bitcast(f16)

        names = """x_in0 x_in1 x_in2 x_in3 w_in0 w_in1 par_in snat_in znat_in z_out ident sgn_done abs_done wT_pe wT_out
            stat_ok std_ok norm_ok xc_ok xp_ok h_ok l_ok xh_pe xl_pe xh_out xl_out snat_pe z_ok pmx_ok pmr_ok
            cm_ok cmr_ok fac_ok chain
            qkv_pe y_ok r_ok h2_ok lq_ok vr_ok v_pe v_out
            q_in0 q_in1 q_in2 q_in3 m_in0 m_in1 m_in2 m_in3 k_in0 k_in1 v_in0 v_in1 const_ok
            s_pe max_ok mhl_ok m_pe mrow_ok st_pe exp_ok pv_pe ev_ok rc_ok mu_ok oh_ok ol_ok ost_out0 ost_out1
            piece_in sub_ok wz_out0 wz_out1 wgu_in0 wgu_in1 wd_in evb_ok
            wo_in0 wo_in1 wosgn_ok woabs_ok woT_pe woT_out co_ok o_pe yo_ok ro_ok acc_ok
            even_pe odd_pe act_ok pool_ok dve_ok sil_ok hp_ok hh_ok hl_ok scl0_in scl1_in dscl_in
            t_pe f_ok xr_in0 xr_in1 xr_in2 xr_in3 out_ok0 out_ok1 out_ok2 out_ok3""".split()
        s = {n: sem(n) for n in names}

        WSRC = [(wq, i * P) for i in range(FQ)] + [(wk, i * P) for i in range(FK)] + [(wv, i * P) for i in range(FK)]
        NW = len(WSRC)
        QKV = [10, 11] + list(range(10))
        GATE_UP = [(u, m, gp) for u in range(2) for m in range(2) for gp in range(4)]
        ROUNDS = [("gu",) + t for t in GATE_UP[:8]] + [("dn", ot, 0, 0) for ot in range(FQ)] \
            + [("gu",) + t for t in GATE_UP[8:]]

        def rounds(down, gateup):
            return [(r, t) for r, t in enumerate(ROUNDS) if (t[0] == "gu" and gateup) or (t[0] == "dn" and down)]

        def first_of(t):
            return t[0] == "gu" and t[3] == 0

        def by_vector(t, c):
            return not first_of(t) and c == 3 and t[:3] != ("gu", 0, 1)

        def chunks(down, gateup):
            out, n, a, b, g = [], 0, 0, 0, 0
            bank = {0: ("a", -3), 1: ("a", -2), 2: ("a", -1), 3: ("b", -1)}
            slots = {0: ("g", -6), 1: ("g", -5), 2: ("g", -4), 3: ("n", -13),
                     4: ("g", -3), 5: ("g", -2), 6: ("g", -1), 7: ("g", -19)}
            if gateup and not down:
                bank = {c: ("a", c - 4) for c in range(NC)}
                slots = {}
            for r, t in rounds(down, gateup):
                for c in range(NC):
                    kind, slot = "b" if by_vector(t, c) else "a", 4 * (r % 2) + c
                    pool = kind == "a" and not first_of(t)
                    out.append(dict(r=r, t=t, c=c, n=n, a=a, b=b, g=g, kind=kind, pool=pool, bank=bank[c],
                                    slot=slot, freed=slots.get(slot)))
                    bank[c] = (kind, a if kind == "a" else b)
                    if kind == "a":
                        slots[slot] = ("g", g) if pool else ("n", n)
                    n, a, b, g = n + 1, a + (kind == "a"), b + (kind == "b"), g + pool
            return out, (n, a, b, g)

        BODY = {"first": chunks(False, True), "full": chunks(True, True), "last": chunks(True, False)}

        def counts_before(k):
            return tuple(f + (k - 1) * g for f, g in zip(BODY["first"][1], BODY["full"][1]))

        ZERO = (0, 0, 0, 0)
        H_FULL = (((0, 1, 2, 3), (1, 3, 4, 5), (2, 4, 5, 6), (4, 6, 6, 7)),
                  ((8, 9, 10, 11), (10, 12, 14, 16), (16, 17, 18, 19), (17, 18, 20, 22)))
        H_STEPS = {"first": {(1, c, j): 16 + c + j for c in range(NC) for j in range(4)},
                   "full": {(w, c, j): H_FULL[w][j][c] for w in range(2) for j in range(4) for c in range(NC)},
                   "last": {}}

        def h_steps(kind, ch, mine):
            if ch["c"] != 1:
                return []
            return sorted((j, w, c) for (w, c, j), r in H_STEPS[kind].items() if r == ch["r"] and j in mine)

        def width(every, i):
            c = i % 2
            if every[i - c]["kind"] == every[i - c + 1]["kind"] == "a":
                return 0 if c else 2
            return 1

        def wait_products(eng, w, m, c, n0, g0):
            if by_vector(("gu", 1 - w, m, 1), c):
                eng.wait_ge(s["dve_ok"], n0 + (-16, 0, 16, 32)[2 * w + m] + 4)
            else:
                eng.wait_ge(s["pool_ok"], g0 + (-9, 0, 9, 21)[2 * w + m])

        def target(t, c, w=1):
            if t[0] == "gu":
                return gu[:, t[1], t[2], c * 512:(c + w) * 512]
            return acc[c // 2][:, t[1], (c % 2) * 512:(c % 2 + w) * 512]

        def scale_col(t, odd):
            if t[0] == "gu":
                k = t[2] * KT + 2 * t[3] + odd
                return scl[:, t[1], k:k + 1]
            return dscl[:, odd, t[1]:t[1] + 1]

        def wait_scales(eng, r, k):
            name, n = {0: ("scl0_in", 16 * k + 16), 8: ("dscl_in", 16 * k), 16: ("scl1_in", 16 * k + 16)}[r]
            eng.wait_ge(s[name], n)

        block = ctx.enter_context(nc.Block())

        @block.sync
        def _(sp):
            w_sem = [s["w_in0"], s["w_in1"]]
            def load_x(bt):
                for i in range(4 * bt, 4 * bt + 4):
                    b, r0 = i // 8, (i % 8) * P
                    sp.dma_start(xs[:, i, :], x[b, r0:r0 + P, :]).then_inc(s[f"x_in{bt}"], 16)

            def load_w(k):
                if k >= 2:
                    sp.wait_ge(s["sgn_done"], k - 1)
                    sp.wait_ge(s["abs_done"], k - 1)
                src, w0 = WSRC[k]
                sp.dma_start(wraw[:, k % 2, :], src[w0:w0 + P, :]).then_inc(w_sem[k % 2], 16)

            load_x(0)
            load_w(0)
            load_w(1)
            load_x(1)
            for k, (v, n, c0) in enumerate(((sq, FQ, 0), (sk, FK, 8), (sv, FK, 10), (so, FQ, 12))):
                sp.dma_start(spar[:, c0:c0 + n], v.rearrange("(t p) -> p t", p=P),
                             allow_slow_non_contiguous=True).then_inc(s["par_in"], 16)
            for k in range(2, 6):
                load_w(k)
            load_x(2)
            for m, zsrc in enumerate((gz, uz)):
                sp.dma_start(znat[:, m * 1024:(m + 1) * 1024].rearrange("t (g c) -> t g c", g=KT),
                             zsrc.rearrange("g (t c) -> t g c", c=P)).then_inc(s["znat_in"], 16)
            sp.dma_start(znat[:, 2048:3072], dz).then_inc(s["znat_in"], 16)
            for k in range(6, 9):
                load_w(k)
            load_x(3)
            for k in range(9, NW):
                load_w(k)
            sp.wait_ge(s["z_ok"], 1)
            sp.dma_start(zscr.rearrange("t m c -> t (m c)"), zf16).then_inc(s["z_out"], 16)

            def load_q(hd, g, buf):
                rows = slice(32 * (hd % 4), 32 * (hd % 4) + 32)
                for part, to in ((0, 0), (1, 32), (0, 64)):
                    sp.dma_start(qst[to:to + 32, buf, :], qz[rows, g, part, :]).then_inc(s[f"q_in{buf}"], 16)

            def load_kv(gi, it, g, buf):
                rows = slice(32 * gi, 32 * gi + 32)
                for part, to in ((0, 0), (0, 32), (1, 64)):
                    sp.dma_start(kst[to:to + 32, buf, :], kz[rows, it, part, :]).then_inc(s[f"k_in{buf}"], 16)
                sp.dma_start(vst[:, buf, :, 0:32], vz[:, g, :, :]).then_inc(s[f"v_in{buf}"], 16)

            def load_m(buf, par):
                for part in range(2):
                    sp.dma_start(qst[96 + part:97 + part, buf, :].rearrange("a (q c) -> a q c", q=8),
                                 mrow[8 * part:8 * part + 8, par, :]).then_inc(s[f"m_in{buf}"], 16)

            sp.wait_ge(s["lq_ok"], 20 + 1)
            sp.wait_ge(s["h2_ok"], 20)
            sp.wait_ge(s["v_out"], 4)
            sp.wait_ge(s["qkv_pe"], 12 * NC)
            load_kv(0, 0, 0, 0)
            for hd in range(4):
                load_q(hd, 0, hd)
            for hd in range(2):
                sp.wait_ge(s["mrow_ok"], hd + 1)
                load_m(hd, hd)

            def load_piece(t, p):
                t, m, j = t + p // 6, p % 6 // 2, p % 2
                if m < 2:
                    src = (gw, uw)[m].rearrange("(g p) i -> p g i", p=P)[:, 4 * j:4 * j + 4, bass.ts(t, P)]
                    dst = wst.rearrange("p (g c) -> p g c", g=4)
                else:
                    src, dst = dw[bass.ts(t, P), j * 512:(j + 1) * 512], wst
                sp.dma_start(dst, src).then_inc(s["piece_in"], 16)
                z = zscr[bass.ds(t, 1), m, j * 512:(j + 1) * 512]
                sp.dma_start(zst[:, p % 2, :], z.rearrange("a c -> (a c)").partition_broadcast(P)
                             ).then_inc(s["piece_in"], 16)

            def store_piece(t, p):
                t, m, j = t + p // 6, p % 6 // 2, p % 2
                dst = wscr[bass.ds(t, 1), m, :, j * 512:(j + 1) * 512].rearrange("a p c -> p (a c)")
                sp.dma_start(dst, zst[:, p % 2, :]).then_inc(s[f"wz_out{p % 2}"], 16)

            def next_piece(it, p, last):
                sp.wait_ge(s["sub_ok"], 42 * it + p + 1)
                sp.nop(nofuse=True)
                if p + 1 < 42 or not last:
                    sp.wait_ge(s[f"wz_out{(p + 1) % 2}"], 16 * 21 * it + 16 * ((p + 1) // 2) + 16)
                    sp.nop(nofuse=True)
                    load_piece(7 * it, p + 1)
                store_piece(7 * it, p)

            def store_output(it, go):
                sp.wait_ge(s["ol_ok"], 4 * it + go + 1)
                sp.nop(nofuse=True)
                sp.dma_start(qz[:, bass.ds(4 * it + go, 1), :, :].rearrange("p a h c -> p (a h) c"), ost[:, go % 2, :, :]).then_inc(s[f"ost_out{go % 2}"], 16)

            def sp_attention(it, first, last):
                for e in range(STEPS_BODY):
                    n, k, gi = e // 8, e % 8, e // 32
                    if e % 3 == 0 and e // 3 < 42:
                        next_piece(it, e // 3, last)
                    if e % 32 == 2 and not (last and gi == 3):
                        sp.wait_ge(s["pv_pe"], 128 * it + 32 * gi + 2)
                        ng = gi + 1
                        sp.nop(nofuse=True)
                        load_kv(ng % 4, it + ng // 4, 4 * it + ng, ng % 2)
                    if k == 6 and (n + 2 < 16 or not last):
                        sp.wait_ge(s["mrow_ok"], 16 * it + n + 3)
                        load_m((n + 2) % 4, n % 2)
                    if k == 7 and (n + 4 < 16 or not last):
                        sp.wait_ge(s["st_pe"], 128 * it + 8 * n + 8)
                        nx = n + 4
                        sp.nop(nofuse=True)
                        load_q(nx, (4 * it + nx // 4), nx % 4)
                    if e % 32 == 31 and not (first and gi == 0):
                        store_output(it, gi - 1)

            for j in range(2):
                sp.sem_inc(s[f"wz_out{j}"], 16)
            sp.wait_ge(s["z_out"], 16)
            load_piece(0, 0)
            sp_attention(0, True, False)
            with sp.Fori(1, 3) as it:
                sp_attention(it, False, False)
            sp_attention(3, False, True)

            sp.dma_start(snat_g, gs.rearrange("g (t c) -> t g c", c=P)).then_inc(s["snat_in"], 16)
            sp.dma_start(snat_u, us.rearrange("g (t c) -> t g c", c=P)).then_inc(s["snat_in"], 16)
            sp.dma_start(snat_d, ds).then_inc(s["snat_in"], 16)
            sp.wait_ge(s["pv_pe"], 512 + 2)
            wo_sem = [s["wo_in0"], s["wo_in1"]]
            for i in range(FQ):
                if i == 6:
                    store_output(3, 3)
                if i >= 2:
                    sp.wait_ge(s["wosgn_ok"], i - 1)
                    sp.wait_ge(s["woabs_ok"], i - 1)
                sp.dma_start(woraw[:, i % 2, :], wo[i * P:(i + 1) * P, :]).then_inc(wo_sem[i % 2], 16)

            def load_gate_up(u, t):
                sp.dma_start(wf[:, u, 0:2, :], wscr[bass.ds(t, 1), 0:2, :, :].rearrange("a m p c -> p (a m) c")
                             ).then_inc(s[f"wgu_in{u}"], 16)

            def load_down(t):
                sp.dma_start(wf[:, :, 2, :], wscr[bass.ds(t, 2), 2, :, :].rearrange("u p c -> p u c")
                             ).then_inc(s["wd_in"], 16)

            def scales(u, t):
                sp.dma_start(scl[:, u, :], tab[:, bass.ds(t, 1), :].rearrange("p a c -> p (a c)")
                             ).then_inc(s[f"scl{u}_in"], 16)

            def sp_ffn(k, n0, first, last):
                if not first:
                    sp.wait_ge(s["odd_pe"], n0)
                load_gate_up(1, 2 * k + 1)
                if not first:
                    sp.wait_ge(s["dve_ok"], n0 - 32 + 4)
                    sp.dma_start(dscl[:, :, :], dtab[:, bass.ds(2 * k - 2, 2), :]).then_inc(s["dscl_in"], 16)
                    sp.wait_ge(s["hp_ok"], 8 * k)
                scales(1, 2 * k + 1)
                if not last:
                    sp.wait_ge(s["odd_pe"], n0 + 32)
                    load_gate_up(0, 2 * k + 2)
                if not first:
                    sp.wait_ge(s["odd_pe"], n0 + 64)
                load_down(2 * k)
                if not last:
                    sp.wait_ge(s["hp_ok"], 8 * k + 4)
                    scales(0, 2 * k + 2)

            for j in range(2):
                sp.wait_ge(s[f"ost_out{j}"], 16 * 9)
            sp.wait_ge(s["woT_pe"], FQ)
            for j in range(2):
                sp.wait_ge(s[f"wz_out{j}"], 16 * 84 + 16)
            load_gate_up(0, 0)
            sp.wait_ge(s["acc_ok"], 2)
            scales(0, 0)
            sp_ffn(0, 0, True, False)
            with sp.Fori(1, PAIRS - 1) as k:
                sp_ffn(k, counts_before(k)[0], False, False)
            sp_ffn(PAIRS - 1, counts_before(PAIRS - 1)[0], False, True)
            sp.wait_ge(s["dve_ok"], counts_before(PAIRS)[0] - 32 + 4)
            sp.dma_start(dscl[:, :, :], dtab[:, IT - 2:IT, :]).then_inc(s["dscl_in"], 16)

            def rows_out(j):
                sp.wait_ge(s["f_ok"], j + 1)
                sp.dma_start(out[j // 8, (j % 8) * P:(j % 8) * P + P, :], fo[:, j % 4, :]).then_inc(s[f"out_ok{j % 4}"], 16)

            sp.wait_ge(s["odd_pe"], counts_before(PAIRS)[0])
            for i in range(NX):
                sp.dma_start(xin[:, i, :], x[i // 8, (i % 8) * P:(i % 8) * P + P, :]).then_inc(s[f"xr_in{i // 4}"], 16)
            for j in range(NX):
                rows_out(j)
            for j in range(4):
                sp.wait_ge(s[f"out_ok{j}"], 16 * NX // 4)

        @block.gpsimd
        def _(pool):
            nc.gpsimd.memset(id32[:], 0.0).then_inc(s["ident"], 1)
            nc.gpsimd.memset(id16[:], 0.0).then_inc(s["ident"], 1)
            pool.wait_ge(s["ident"], 2)
            for m in (id32, id16):
                nc.gpsimd.affine_select(out=m[:], in_=m[:], compare_op=ALU.not_equal, fill=1.0, base=0,
                                        pattern=[[-1, P]], channel_multiplier=1).then_inc(s["ident"], 1)
            for bt in range(4):
                for j in range(2):
                    i = 4 * bt + 2 + j
                    pool.wait_ge(s["norm_ok"], 4 * bt + j + 1)
                    nc.gpsimd.tensor_scalar(xs[:, i, :], xs[:, i, :], 64.0, -64.0, amin, amax).then_inc(s["xp_ok"], 1)
            pool.wait_ge(s["cm_ok"], 1)
            nc.gpsimd.partition_all_reduce(cmr, cm, P, RMAX).then_inc(s["cmr_ok"], 1)
            pool.wait_ge(s["qkv_pe"], 12 * NC)
            pool.wait_ge(s["lq_ok"], 10 * NC + 1)
            nc.gpsimd.memset(kst[96:98, :, :], MU).then_inc(s["const_ok"], 1)
            pool.wait_ge(s["const_ok"], 1)
            nc.gpsimd.memset(vst[:, :, :, 32:64], 1.0).then_inc(s["const_ok"], 1)

            def divide(it, gi):
                pool.wait_ge(s["rc_ok"], 64 * it + 16 * gi + 16)
                nc.gpsimd.tensor_tensor(num[:, gi % 2, :], num[:, gi % 2, :], den[:, gi % 2, :], mult
                                        ).then_inc(s["mu_ok"], 1)

            def tail_of(it, gi):
                pool.wait_ge(s["oh_ok"], 4 * it + gi + 1)
                nc.gpsimd.tensor_tensor(ost[:, gi % 2, 1, :], num[:, gi % 2, :], ost[:, gi % 2, 0, :], sub
                                        ).then_inc(s["ol_ok"], 1)

            with pool.Fori(0, 4) as it:
                for gi in range(4):
                    divide(it, gi)
                    tail_of(it, gi)

            pool.wait_ge(s["pmx_ok"], 1)
            nc.gpsimd.partition_all_reduce(pmr, pmx, P, RMAX).then_inc(s["pmr_ok"], 1)
            pool.wait_ge(s["pmx_ok"], 2)
            nc.gpsimd.partition_all_reduce(pmr2, pmx2, P, RMAX).then_inc(s["pmr_ok"], 1)

            def pool_ffn(kind, before):
                n0, _, _, g0 = before
                every = BODY[kind][0]
                for i, q in enumerate(every):
                    w = width(every, i)
                    if q["pool"] and w:
                        if not (kind == "first" and q["g"] < 3):
                            pool.wait_ge(s["pool_ok"], g0 + q["g"] - 2)
                        pool.wait_ge(s["dve_ok"], n0 + q["n"] + w + 4)
                        to = target(q["t"], q["c"], w)
                        nc.gpsimd.tensor_tensor(to, to, tmp[:, q["slot"]:q["slot"] + w, :].rearrange("p a c -> p (a c)"),
                                                add).then_inc(s["pool_ok"], w)

            pool_ffn("first", ZERO)
            with pool.Fori(1, PAIRS) as k:
                pool_ffn("full", counts_before(k))
            pool_ffn("last", counts_before(PAIRS))

        @block.scalar
        def _(act):
            A = nc.scalar.activation
            w_sem = [s["w_in0"], s["w_in1"]]

            def evac_x(i):
                act.wait_ge(s["xh_pe"], i + 1)
                A(xT[:, 0, :, i * P:(i + 1) * P], bank16(2 + 2 * (i % 2)).rearrange("p (k c) -> p k c", k=KT),
                  ACT.Copy).then_inc(s["xh_out"], 1)
                act.wait_ge(s["xl_pe"], i + 1)
                A(xT[:, 1, :, i * P:(i + 1) * P], bank16(3 + 2 * (i % 2)).rearrange("p (k c) -> p k c", k=KT),
                  ACT.Copy).then_inc(s["xl_out"], 1)

            def signs(bt):
                for k in range(3 * bt, 3 * bt + 3):
                    act.wait_ge(w_sem[k % 2], 16 * (k // 2 + 1))
                    if k >= 1:
                        act.wait_ge(s["wT_pe"], k)
                    A(wsg, wraw[:, k % 2, :], ACT.Sign).then_inc(s["sgn_done"], 1)

            def deviation(bt):
                act.wait_ge(s["stat_ok"], bt + 1)
                A(sd_, ve, ACT.Sqrt).then_inc(s["std_ok"], 1)

            signs(0)
            deviation(0)
            for bt in range(4):
                if bt + 1 < 4:
                    signs(bt + 1)
                for i in range(4 * bt, 4 * bt + 4):
                    if i % 4 == 2 and bt + 1 < 4:
                        deviation(bt + 1)
                    act.wait_ge(s["xc_ok" if i % 4 < 2 else "xp_ok"], 2 * bt + i % 2 + 1)
                    if i >= 2:
                        act.wait_ge(s["xh_pe"], i - 1)
                        act.wait_ge(s["l_ok"], i - 1)
                    A(hst[:, i % 2, :], xs[:, i, :], ACT.Copy, scale=fl[:, i:i + 1]).then_inc(s["h_ok"], 1)
                    if i > 4 * bt:
                        evac_x(i - 1)
                evac_x(4 * bt + 3)

            act.sem_inc(s["y_ok"], 6)
            act.wait_ge(s["fac_ok"], 1)
            act.wait_ge(s["z_out"], 16)

            def act_qkv(b2, s2):
                c = 2 * b2 + s2
                for p in range(12):
                    f = QKV[p]
                    act.wait_ge(s["qkv_pe"], 12 * c + p + 1)
                    act.wait_ge(s["r_ok"], 12 * c + p + 1)
                    A(y2[:, p % 2, :], ps[:, p % 6, :], ACT.Copy, scale=cc[:, f:f + 1]).then_inc(s["y_ok"], 1)
                    if p >= 3:
                        head(c, b2, s2, p - 1)
                head(c, b2, s2, 11)

            def head(c, b2, s2, p):
                f = QKV[p]
                act.wait_ge(s["r_ok"], 12 * c + p + 3)
                src, k = (r2[:, p % 2, :], 0 if f < 8 else 1)
                if f < 8:
                    dst = qz[:, bass.ds(b2 * 8 + f, 1), 0, s2 * 512:(s2 + 1) * 512].rearrange("p a c -> p (a c)")
                else:
                    dst = kz[:, bass.ds(b2 * 2 + (f - 8), 1), 0, s2 * 512:(s2 + 1) * 512].rearrange("p a c -> p (a c)")
                act.nop(nofuse=True)
                A(dst, src, ACT.Copy, scale=fac[:, k:k + 1]).then_inc(s["h2_ok"], 1)

            with act.Fori(0, 2) as b2:
                act_qkv(b2, 0)
                act_qkv(b2, 1)

            act.sem_inc(s["exp_ok"], 2)
            act.sem_inc(s["ev_ok"], 8)
            for j in range(2):
                act.sem_inc(s[f"ost_out{j}"], 16)

            def exp_step(n0, e):
                act.wait_ge(s["st_pe"], n0 + e + 1)
                act.wait_ge(s["pv_pe"], n0 + e + 1)
                A(prob[:, e % 2, :].rearrange("p (a c) -> p a c", a=2), ps[:, 2 + 2 * (e % 2):4 + 2 * (e % 2), :],
                  ACT.Exp, scale=gam[:, 0:1]).then_inc(s["exp_ok"], 1)

            exp_step(0, 0)
            exp_step(0, 1)

            def evacuate(it, n, j):
                half, gi = j // 2, n // 4
                rows = slice(32 * (n % 4), 32 * (n % 4) + 32)
                if j == 0:
                    act.wait_ge(s["pv_pe"], 128 * it + 8 * n + 10)
                    if n % 4 == 0:
                        act.wait_ge(s[f"ost_out{gi % 2}"], 32 * it + 16 * (gi // 2) + 16)
                dst = (den if j % 2 else num)[rows, gi % 2, half * 512:(half + 1) * 512]
                r0 = 64 * half + 32 * (j % 2)
                A(dst, ps[r0:r0 + 32, 6 + n % 2, :], ACT.Copy).then_inc(s["ev_ok"], 1)

            def head_of(it, gi):
                act.wait_ge(s["mu_ok"], 4 * it + gi + 1)
                A(ost[:, gi % 2, 0, :], num[:, gi % 2, :], ACT.Copy).then_inc(s["oh_ok"], 1)

            def act_attention(it, first, last):
                for e in range(STEPS_BODY):
                    n, k = e // 8, e % 8
                    if e + 2 < STEPS_BODY or not last:
                        exp_step(128 * it, e + 2)
                    if k < 4 and not (first and n == 0):
                        evacuate(it, n - 1, k)
                    if e % 32 == 30 and not (first and e < 32):
                        head_of(it, e // 32 - 1)
                if last:
                    for j in range(4):
                        evacuate(it, 15, j)

            act_attention(0, True, False)
            with act.Fori(1, 3) as it:
                act_attention(it, False, False)
            act_attention(3, False, True)

            wo_sem = [s["wo_in0"], s["wo_in1"]]
            for i in range(FQ):
                if i == 3:
                    head_of(3, 3)
                act.wait_ge(wo_sem[i % 2], 16 * (i // 2 + 1))
                if i >= 2:
                    act.wait_ge(s["woT_pe"], i - 1)
                A(wosg[:, i % 2, :], woraw[:, i % 2, :], ACT.Sign).then_inc(s["wosgn_ok"], 1)
            act.wait_ge(s["co_ok"], 1)
            act.sem_inc(s["yo_ok"], 2)

            def act_oproj(ot, m0):
                for s2 in range(2):
                    act.wait_ge(s["o_pe"], m0 + s2 + 1)
                    act.wait_ge(s["acc_ok"], m0 + s2 + 1)
                    act.nop(nofuse=True)
                    A(yo2[:, s2, :], ps[:, s2, :], ACT.Copy,
                      scale=cc[:, bass.ds(ot + 12, 1)]).then_inc(s["yo_ok"], 1)

            for b in range(2):
                with act.Fori(0, FQ) as ot:
                    act_oproj(ot, ot * 2 + 16 * b)

            act.sem_inc(s["act_ok"], 4)

            def act_ffn(kind, k, before):
                n0, a0, _, g0 = before
                seen = -1
                for ch in BODY[kind][0]:
                    r, c = ch["r"], ch["c"]
                    if r != seen and r in (0, 8, 16):
                        wait_scales(act, r, k)
                    seen = r
                    if ch["kind"] == "a":
                        act.wait_ge(s["even_pe"], n0 + ch["n"] + 1)
                        if ch["freed"]:
                            who, place = ch["freed"]
                            if who == "g":
                                act.wait_ge(s["pool_ok"], g0 + place + 1)
                            else:
                                act.wait_ge(s["dve_ok"], n0 + place + 5)
                        A(tmp[:, ch["slot"], :], ps[:, c, :], ACT.Copy, scale=scale_col(ch["t"], 0)
                          ).then_inc(s["act_ok"], 1)
                    for j, w, hc in h_steps(kind, ch, (0, 2)):
                        act_h(w, j, k, hc, n0, g0)

            def act_h(w, step, k, c, n0, g0):
                u = 1 - w
                g = gu[:, u, 0, c * 512:(c + 1) * 512]
                if step == 0:
                    wait_products(act, w, 0, c, n0, g0)
                    A(g, g, ACT.Silu).then_inc(s["sil_ok"], 1)
                else:
                    act.wait_ge(s["hp_ok"], 8 * k - 4 + 4 * w + c + 1)
                    A(hT[u][:, c, 0, :], g, ACT.Copy).then_inc(s["hh_ok"], 1)

            act_ffn("first", 0, ZERO)
            with act.Fori(1, PAIRS) as k:
                act_ffn("full", k, counts_before(k))
            n_end, _, _, g_end = counts_before(PAIRS)
            for step in (0, 2):
                for c in range(NC):
                    act_h(0, step, PAIRS, c, n_end, g_end)
            act_ffn("last", PAIRS, counts_before(PAIRS))

        @block.vector
        def _(dve):
            V = nc.vector
            ch = Tally(s["chain"])

            def settle():
                dve.wait_ge(s["chain"], ch.value())

            w_sem = [s["w_in0"], s["w_in1"]]
            def weights(bt):
                for k in range(3 * bt, 3 * bt + 3):
                    dve.wait_ge(w_sem[k % 2], 16 * (k // 2 + 1))
                    V.tensor_reduce(ssum[:, k:k + 1], wraw[:, k % 2, :], AX, add,
                                    apply_absolute_value=True).then_inc(s["abs_done"], 1)
                    dve.wait_ge(s["wT_pe"], k + 1)
                    V.tensor_copy(wT[:, :, k * P:(k + 1) * P],
                                  bank16(k % 2).rearrange("p (k c) -> p k c", k=KT)).then_inc(s["wT_out"], 1)

            def statistics(bt):
                dve.wait_ge(s[f"x_in{bt}"], 64)
                for i in range(4 * bt, 4 * bt + 4):
                    ch.inc(V.bn_stats(bn[:, i, 0:6], xs[:, i, 0:512]))
                    ch.inc(V.bn_stats(bn[:, i, 6:12], xs[:, i, 512:1024]))
                settle()
                for i in range(4 * bt, 4 * bt + 4):
                    ch.inc(V.bn_aggr(mv[:, i, :], bn[:, i, :]))
                settle()
                b4 = slice(4 * bt, 4 * bt + 4)
                V.tensor_scalar(ve, mv[:, b4, 1], EPS, None, add).then_inc(s["stat_ok"], 1)
                ch.inc(V.tensor_scalar(fl[:, b4], mv[:, b4, 1], 0.0, 0.0, mult, iseq))
                ch.inc(V.tensor_scalar(mark[:, b4], mv[:, b4, 0], 0.0, None, mult))
                settle()
                ch.inc(V.tensor_scalar(fl[:, b4], fl[:, b4], XS, None, mult))

            def normalise(bt):
                dve.wait_ge(s["std_ok"], bt + 1)
                if bt > 0:
                    dve.wait_ge(s["norm_ok"], 4 * bt)
                ch.inc(V.reciprocal(rs, sd_))
                settle()
                ch.inc(V.tensor_tensor(t4, rs, rs, mult))
                settle()
                ch.inc(V.tensor_tensor(t4, t4, ve, mult))
                settle()
                ch.inc(V.tensor_scalar(t4, t4, -0.5, 1.5, mult, add))
                settle()
                ch.inc(V.tensor_tensor(rs, rs, t4, mult))
                settle()
                for j in (2, 3, 0, 1):
                    i = 4 * bt + j
                    V.tensor_scalar(xs[:, i, :], xs[:, i, :], mv[:, i, 0:1], rs[:, j:j + 1], sub, mult
                                    ).then_inc(s["norm_ok"], 1)
                for j in range(2):
                    i = 4 * bt + j
                    dve.wait_ge(s["norm_ok"], 4 * bt + j + 3)
                    V.tensor_scalar(xs[:, i, :], xs[:, i, :], 64.0, -64.0, amin, amax).then_inc(s["xc_ok"], 1)

            def row_tails(tiles):
                for i in tiles:
                    dve.wait_ge(s["h_ok"], i + 1)
                    if i >= 2:
                        dve.wait_ge(s["xl_pe"], i - 1)
                    V.scalar_tensor_tensor(lst[:, i % 2, :], xs[:, i, :], fl[:, i:i + 1], hst[:, i % 2, :],
                                           mult, sub).then_inc(s["l_ok"], 1)

            weights(0)
            statistics(0)
            normalise(0)
            for bt in range(4):
                if bt + 1 < 4:
                    weights(bt + 1)
                    statistics(bt + 1)
                row_tails(range(4 * bt, 4 * bt + 2))
                if bt + 1 < 4:
                    normalise(bt + 1)
                row_tails(range(4 * bt + 2, 4 * bt + 4))

            dve.wait_ge(s["znat_in"], 48)
            V.tensor_copy(zf16, znat).then_inc(s["z_ok"], 1)
            dve.wait_ge(s["par_in"], 64)
            dve.wait_ge(s["abs_done"], NW)

            def channel_scales(a, b):
                ch.inc(V.tensor_scalar(cc[:, a:b], ssum[:, a:b], 1.0 / H, 1e-8, mult, amax))
                settle()
                ch.inc(V.tensor_tensor(cc[:, a:b], cc[:, a:b], spar[:, a:b], mult))
                settle()
                ch.inc(V.tensor_scalar(cc[:, a:b], cc[:, a:b], FMAX, -FMAX, amin, amax))
                settle()

            channel_scales(0, 12)
            ch.inc(V.tensor_scalar(cc[:, 0:12], cc[:, 0:12], 1.0 / XS, None, mult))
            settle()
            for j, (a, b) in enumerate(((0, 8), (8, 10), (10, 12))):
                ins = V.tensor_reduce(cm[:, j:j + 1], cc[:, a:b], AX, amax, apply_absolute_value=True)
                if j < 2:
                    ch.inc(ins)
                else:
                    ins.then_inc(s["cm_ok"], 1)
            dve.wait_ge(s["cmr_ok"], 1)
            ch.inc(V.tensor_scalar(cmr, cmr, 1e-30, None, amax))
            settle()
            ch.inc(V.reciprocal(fac, cmr))
            ch.inc(V.tensor_tensor(gam, cmr[:, 0:1], cmr[:, 1:2], mult))
            settle()
            ch.inc(V.tensor_scalar(gam, gam, (256.0 * 1024.0 / QB) ** 2 / float(D) ** 0.5, None, mult))
            V.tensor_scalar(fac, fac, QB / (256.0 * 1024.0), None, mult).then_inc(s["fac_ok"], 1)

            def guard(y, r, f):
                ch.inc(V.tensor_scalar(r, y, 1e6, -1e6, amin, amax))
                ch.inc(V.tensor_scalar(f, y, 0.0, 0.0, mult, iseq))
                settle()
                dve.nop(nofuse=True)
                return V.copy_predicated(r, f, y)

            dve.sem_inc(s["lq_ok"], 1)
            dve.sem_inc(s["r_ok"], 2)
            ch0 = ch.value()

            def dve_qkv(b2, s2):
                c = 2 * b2 + s2
                for p in range(12):
                    dve.wait_ge(s["y_ok"], 12 * c + p + 7)
                    dve.wait_ge(s["r_ok"], 12 * c + p + 2)
                    if p >= 2:
                        dve.wait_ge(s["lq_ok"], 10 * c + max(p - 3, 0) + 1)
                    dst = rv2[:, p, :] if p < 2 else r2[:, p % 2, :]
                    guard(y2[:, p % 2, :], dst, fin).then_inc(s["r_ok"], 1)
                    if p < 2:
                        dve.wait_ge(s["r_ok"], 12 * c + p + 3)
                        V.tensor_scalar(dst, dst, fac[:, 2:3], None, mult).then_inc(s["vr_ok"], 1)
                    if p >= 3:
                        tail(c, b2, s2, p - 1)
                    if p == 7:
                        for fv in range(2):
                            dve.wait_ge(s["v_pe"], 2 * c + fv + 1)
                            src = ps[:, 6 + fv, :].rearrange("p (t g d) -> p g t d", t=4, g=4)
                            to = vz[:, bass.ds(b2 * 8 + fv * 4, 4), 4 * s2:4 * s2 + 4, :]
                            dve.nop(nofuse=True)
                            V.tensor_copy(to, src).then_inc(s["v_out"], 1)
                tail(c, b2, s2, 11)

            def tail(c, b2, s2, p):
                f = QKV[p]
                dve.wait_ge(s["h2_ok"], 10 * c + p - 1)
                k = 0 if f < 8 else 1
                z, f0 = (qz, b2 * 8 + f) if f < 8 else (kz, b2 * 2 + (f - 8))
                hd = z[:, bass.ds(f0, 1), 0, s2 * 512:(s2 + 1) * 512].rearrange("p a c -> p (a c)")
                to = z[:, bass.ds(f0, 1), 1, s2 * 512:(s2 + 1) * 512].rearrange("p a c -> p (a c)")
                V.scalar_tensor_tensor(to, r2[:, p % 2, :], fac[:, k:k + 1], hd, mult, sub).then_inc(s["lq_ok"], 1)

            with dve.Fori(0, 2) as b2:
                ch.enter(ch0, b2, 48)
                dve_qkv(b2, 0)
                dve_qkv(b2, 1)
                assert ch.n == 48
            ch.leave(ch0 + 24 * NC)


            def row_max(i0, i, par, qt):
                for h2 in range(2):
                    dve.wait_ge(s["s_pe"], 2 * (i0 + i) + h2 + 1)
                    V.tensor_reduce(mxs[:, par, h2, qt:qt + 1], ps[:, h2, :], AX, amax).then_inc(s["max_ok"], 1)

            def split_max(i0, i, par):
                dve.wait_ge(s["max_ok"], 2 * (i0 + i) + 4)
                ch.inc(V.tensor_tensor(mxs[:, par, 0, :], mxs[:, par, 0, :], mxs[:, par, 1, :], amax))
                settle()
                ch.inc(V.tensor_scalar(mhl[:, 0:8], mxs[:, par, 0, :], -1.0 / MU, None, mult))
                settle()
                V.scalar_tensor_tensor(mhl[:, 8:16], mxs[:, par, 0, :], -1.0 / MU, mhl[:, 0:8], mult, sub
                                       ).then_inc(s["mhl_ok"], 1)

            def copy_rows(count, par, bank):
                dve.wait_ge(s["m_pe"], count)
                V.tensor_copy(mrow[0:16, par, :], ps[0:16, bank, 0:64].bitcast(f16)).then_inc(s["mrow_ok"], 1)

            dve.sem_inc(s["max_ok"], 2)
            for hd in range(2):
                for i in range(8):
                    row_max(0, 8 * hd + i, hd, i)
                split_max(0, 8 * hd + 7, hd)
                copy_rows(hd + 1, hd, 6 + hd)
            for i in range(4):
                row_max(0, 16 + i, 0, i)
            cha = ch.value()

            def dequantise(it, p):
                dve.wait_ge(s["piece_in"], 32 * (42 * it + p + 1))
                V.tensor_tensor(zst[:, p % 2, :], wst, zst[:, p % 2, :], sub).then_inc(s["sub_ok"], 1)

            def invert(it, gi, i):
                if i == 0:
                    dve.wait_ge(s["ev_ok"], 64 * it + 16 * gi + 24)
                d = den[:, gi % 2, 64 * i:64 * i + 64]
                V.reciprocal(d, d).then_inc(s["rc_ok"], 1)

            def dve_attention(it, first, last):
                left = []
                for e in range(STEPS_BODY):
                    n, k = e // 8, e % 8
                    hd, qt = (n + 2, 4 + k) if k < 4 else (n + 3, k - 4)
                    if not (last and hd > 15):
                        row_max(128 * it, LEAD_S + e, hd % 2, qt)
                        if k == 3:
                            split_max(128 * it, LEAD_S + e, hd % 2)
                    if k == 5 and not (last and n + 2 > 15):
                        copy_rows(16 * it + n + 3, n % 2, 6 + (n + 1) % 2)
                    if e % 32 == 4 and not (first and e < 32):
                        left = [(e // 32 - 1, i) for i in range(16)]
                    if e % 3 == 0 and e // 3 < 42:
                        dequantise(it, e // 3)
                    elif left:
                        invert(it, *left.pop(0))
                assert not left

            CHA = 32
            dve_attention(0, True, False)
            assert ch.value() == cha + CHA
            with dve.Fori(1, 3) as it:
                ch.enter(cha, it, CHA)
                dve_attention(it, False, False)
                assert ch.n == CHA, ch.n
            ch.leave(cha + 3 * CHA)
            dve_attention(3, False, True)

            wo_sem = [s["wo_in0"], s["wo_in1"]]

            def output_magnitude(i):
                dve.wait_ge(wo_sem[i % 2], 16 * (i // 2 + 1))
                V.tensor_reduce(ssum[:, 12 + i:13 + i], woraw[:, i % 2, :], AX, add,
                                apply_absolute_value=True).then_inc(s["woabs_ok"], 1)

            for i in range(8):
                invert(3, 3, i)
            for i in range(2):
                output_magnitude(i)
            for i in range(8, 16):
                invert(3, 3, i)
            for i in range(FQ):
                if i >= 2:
                    output_magnitude(i)
                dve.wait_ge(s["woT_pe"], i + 1)
                V.tensor_copy(woT[:, :, i * P:(i + 1) * P],
                              bank16(2 + i % 2).rearrange("p (k c) -> p k c", k=KT)).then_inc(s["woT_out"], 1)
            dve.wait_ge(s["woabs_ok"], FQ)
            channel_scales(12, 20)
            ch.inc(V.tensor_scalar(fac[:, 2:3], cmr[:, 2:3], 256.0 * 1024.0 / QB, None, mult))
            settle()
            V.tensor_scalar(cc[:, 12:20], cc[:, 12:20], fac[:, 2:3], None, mult).then_inc(s["co_ok"], 1)
            dve.wait_ge(s["snat_pe"], 1)
            for j in range(2):
                dve.wait_ge(s[f"wz_out{j}"], 16 * 84 + 16)
            for m in range(2):
                ch.inc(V.tensor_scalar(tab[:, :, m * KT:(m + 1) * KT].rearrange("p t g -> p g t"),
                                       ps[:, 6, m * 224:(m + 1) * 224].rearrange("p (g t) -> p g t", g=KT),
                                       1.0 / XS, None, mult))
            ch.inc(V.tensor_copy(dtab[:, :, :].rearrange("p t o -> p o t"),
                                 ps[:, 7, 0:224].rearrange("p (o t) -> p o t", o=FQ)))
            settle()
            V.tensor_reduce(pmx, tab[:, :, 0:KT], AX, amax, apply_absolute_value=True).then_inc(s["pmx_ok"], 1)
            V.tensor_reduce(pmx2, tab[:, :, KT:2 * KT], AX, amax, apply_absolute_value=True).then_inc(s["pmx_ok"], 1)
            dve.wait_ge(s["pmr_ok"], 2)
            ch.inc(V.tensor_tensor(pmr, pmr, pmr2, mult))
            settle()
            ch.inc(V.tensor_scalar(pmr, pmr, XS * XS, 1e-30, mult, amax))
            settle()
            ch.inc(V.reciprocal(pmx, pmr))
            settle()
            ch.inc(V.tensor_scalar(tab[:, :, 16], pmx, 2.0 ** -12, None, mult))
            ch.inc(V.tensor_scalar(pmr, pmr, 2.0 ** 12, None, mult))
            settle()
            for o in range(FQ):
                ch.inc(V.tensor_tensor(dtab[:, :, o], dtab[:, :, o], pmr, mult))
            settle()

            dve.sem_inc(s["acc_ok"], 2)
            cho = ch.value()

            def dve_oproj(ot, m0, b):
                for s2 in range(2):
                    dve.wait_ge(s["yo_ok"], m0 + s2 + 3)
                    dve.wait_ge(s["acc_ok"], m0 + s2 + 2)
                    ch.inc(guard(yo2[:, s2, :], ro, fino))
                    settle()
                    dve.nop(nofuse=True)
                    V.tensor_copy(acc[b][:, bass.ds(ot, 1), s2 * 512:(s2 + 1) * 512].rearrange("p a c -> p (a c)"), ro
                                  ).then_inc(s["acc_ok"], 1)

            for b in range(2):
                with dve.Fori(0, FQ) as ot:
                    ch.enter(cho + 48 * b, ot, 6)
                    dve_oproj(ot, ot * 2 + 16 * b, b)
                    assert ch.n == 6
            ch.leave(cho + 96)

            dve.sem_inc(s["dve_ok"], 4)

            def dve_ffn(kind, k, before):
                n0, a0, b0, g0 = before
                seen, every = -1, BODY[kind][0]
                for i, q in enumerate(every):
                    r, c, t = q["r"], q["c"], q["t"]
                    if r != seen and r in (0, 8, 16):
                        wait_scales(dve, r, k)
                    seen = r
                    if c == 0:
                        for own in every[i:i + NC]:
                            if own["kind"] == "b":
                                to = target(t, own["c"])
                                dve.wait_ge(s["dve_ok"], n0 + own["n"] + 1)
                                dve.wait_ge(s["even_pe"], n0 + own["n"] + 1)
                                V.scalar_tensor_tensor(to, ps[:, own["c"], :], scale_col(t, 0), to, mult, add
                                                       ).then_inc(s["evb_ok"], 1)
                    w = width(every, i)
                    if not w:
                        continue
                    rest = to = target(t, c, w)
                    if q["kind"] == "b":
                        dve.wait_ge(s["evb_ok"], b0 + q["b"] + 1)
                    else:
                        rest = tmp[:, q["slot"]:q["slot"] + w, :].rearrange("p a c -> p (a c)")
                        dve.wait_ge(s["act_ok"], a0 + q["a"] + w + 4)
                        if q["pool"]:
                            to = rest
                    dve.wait_ge(s["odd_pe"], n0 + q["n"] + w)
                    V.scalar_tensor_tensor(to, ps[:, 4 + c:4 + c + w, :].rearrange("p a c -> p (a c)"), scale_col(t, 1),
                                           rest, mult, add).then_inc(s["dve_ok"], w)
                    for j, w, hc in h_steps(kind, every[i + 1 - c % 2], (1, 3)) if c < 2 else ():
                        dve_h(w, j, k, hc, n0, g0)

            def dve_h(w, step, k, c, n0, g0):
                u = 1 - w
                g, up = (gu[:, u, m, c * 512:(c + 1) * 512] for m in range(2))
                n = 8 * k - 4 + 4 * w + c + 1
                if step == 1:
                    wait_products(dve, w, 1, c, n0, g0)
                    dve.wait_ge(s["sil_ok"], n)
                    V.scalar_tensor_tensor(g, g, scl[:, u, 16:17], up, mult, mult).then_inc(s["hp_ok"], 1)
                else:
                    dve.wait_ge(s["hh_ok"], n)
                    V.tensor_tensor(hT[u][:, c, 1, :], g, hT[u][:, c, 0, :], sub).then_inc(s["hl_ok"], 1)

            dve_ffn("first", 0, ZERO)
            with dve.Fori(1, PAIRS) as k:
                dve_ffn("full", k, counts_before(k))
            n_end, _, _, g_end = counts_before(PAIRS)
            for step in (1, 3):
                for c in range(NC):
                    dve_h(0, step, PAIRS, c, n_end, g_end)
            dve_ffn("last", PAIRS, counts_before(PAIRS))

            for i in range(NX):
                dve.wait_ge(s["t_pe"], i + 1)
                dve.wait_ge(s[f"xr_in{i // 4}"], 64)
                if i >= 4:
                    dve.wait_ge(s[f"out_ok{i % 4}"], 16 * (i // 4))
                V.scalar_tensor_tensor(fo[:, i % 4, :].rearrange("p (a c) -> p a c", a=2),
                                       ps[:, 2 * (i % 4):2 * (i % 4) + 2, :], mark[:, i:i + 1],
                                       xin[:, i, :].rearrange("p (a c) -> p a c", a=2), add, add
                                       ).then_inc(s["f_ok"], 1)

        @block.tensor
        def _(pe):
            MM = nc.tensor.matmul
            TR = nc.tensor.transpose
            pe.wait_ge(s["ident"], 4)
            def weight_transposes(bt):
                for k in range(3 * bt, 3 * bt + 3):
                    pe.wait_ge(s["sgn_done"], k + 1)
                    if k >= 2:
                        pe.wait_ge(s["wT_out"], k - 1)
                    for t in range(KT):
                        last = TR(bank16(k % 2)[:, t * P:(t + 1) * P], wsg[:, t * P:(t + 1) * P], id16[:])
                    last.then_inc(s["wT_pe"], 1)

            weight_transposes(0)
            for bt in range(4):
                if bt + 1 < 4:
                    weight_transposes(bt + 1)
                for i in range(4 * bt, 4 * bt + 4):
                    for part, st_, ok, done, free in ((0, hst, "h_ok", "xh_pe", "xh_out"),
                                                      (1, lst, "l_ok", "xl_pe", "xl_out")):
                        pe.wait_ge(s[ok], i + 1)
                        if i >= 2:
                            pe.wait_ge(s[free], i - 1)
                        for t in range(KT):
                            last = TR(bank16(2 + 2 * (i % 2) + part)[:, t * P:(t + 1) * P],
                                      st_[:, i % 2, t * P:(t + 1) * P], id16[:])
                        last.then_inc(s[done], 1)
            pe.wait_ge(s["wT_out"], NW)
            pe.wait_ge(s["xh_out"], NX)
            pe.wait_ge(s["xl_out"], NX)

            def pe_qkv(c):
                for p in range(12):
                    f = QKV[p]
                    pe.wait_ge(s["y_ok"], 12 * c + p + 1)
                    for kt in range(KT):
                        for part in range(2):
                            last = MM(ps[:, p % 6, :], wT[:, kt, f * P:(f + 1) * P],
                                      xT[:, part, kt, bass.ds(c * 512, 512)],
                                      start=(kt == 0 and part == 0), stop=(kt == KT - 1 and part == 1))
                    last.then_inc(s["qkv_pe"], 1)
                    if p == 5:
                        for fv in range(2):
                            pe.wait_ge(s["vr_ok"], 2 * c + fv + 1)
                            for t in range(4):
                                last = TR(ps[:, 6 + fv, t * P:(t + 1) * P], rv2[:, fv, t * P:(t + 1) * P], id32[:])
                            last.then_inc(s["v_pe"], 1)

            with pe.Fori(0, NC) as c:
                pe_qkv(c)

            pe.sem_inc(s["pv_pe"], 2)

            def row_scores(i0, i, qbuf, kbuf, qt):
                for h2 in range(2):
                    pe.wait_ge(s["max_ok"], 2 * (i0 + i) + h2 + 1)
                    MM(ps[:, h2, :], qst[0:96, qbuf, qt * P:(qt + 1) * P],
                       kst[0:96, kbuf, h2 * 512:(h2 + 1) * 512], start=True, stop=True).then_inc(s["s_pe"], 1)

            def maxima_rows(count, bank):
                pe.wait_ge(s["mhl_ok"], count)
                TR(ps[0:16, bank, 0:64].bitcast(f16), mhl[:, 0:16], id16[:]).then_inc(s["m_pe"], 1)

            def key_scores(n0, e, qbuf, kbuf):
                kt = e % 8
                pe.wait_ge(s["exp_ok"], n0 + e + 1)
                for a in range(2):
                    last = MM(ps[:, 2 + 2 * (e % 2) + a, :], kst[0:98, kbuf, kt * P:(kt + 1) * P],
                              qst[0:98, qbuf, a * 512:(a + 1) * 512], start=True, stop=True)
                last.then_inc(s["st_pe"], 1)

            pe.wait_ge(s["y_ok"], 12 * NC + 6)
            pe.wait_ge(s["v_out"], 2 * NC)
            pe.wait_ge(s["k_in0"], 48)
            for hd in range(2):
                pe.wait_ge(s[f"q_in{hd}"], 48)
                for i in range(8):
                    row_scores(0, 8 * hd + i, hd, 0, i)
                maxima_rows(hd + 1, 6 + hd)
            pe.wait_ge(s["q_in2"], 48)
            for i in range(4):
                row_scores(0, 16 + i, 2, 0, i)
            pe.wait_ge(s["const_ok"], 2)
            pe.wait_ge(s["m_in0"], 32)
            for e in range(2):
                key_scores(0, e, 0, 0)

            def pe_attention(it, last_body):
                for e in range(STEPS_BODY):
                    n, k, gi = e // 8, e % 8, e // 32
                    if n % 4 == 0 and k == 0:
                        pe.wait_ge(s[f"v_in{gi % 2}"], 32 * it + 16 * (gi // 2) + 16)
                    if k == 0:
                        pe.wait_ge(s["ev_ok"], 64 * it + 4 * n + 4)
                        pe.wait_ge(s["mrow_ok"], 16 * it + n + 2 if not (last_body and n == 15) else 64)
                    pe.wait_ge(s["exp_ok"], 128 * it + e + 3)
                    for a in range(2):
                        last = MM(ps[64 * a:64 * a + 64, 6 + n % 2, :], vst[:, gi % 2, k, :],
                                  prob[:, e % 2, a * 512:(a + 1) * 512], start=(k == 0), stop=(k == 7))
                    last.then_inc(s["pv_pe"], 1)
                    e2 = e + 2
                    if e2 < STEPS_BODY or not last_body:
                        n2 = e2 // 8
                        if e2 % 8 == 0:
                            pe.wait_ge(s[f"m_in{n2 % 4}"], 128 * it + 32 * (n2 // 4) + 32)
                        key_scores(128 * it, e2, n2 % 4, (n2 // 4) % 2)
                    hd, qt = (n + 2, 4 + k) if k < 4 else (n + 3, k - 4)
                    if not (last_body and hd > 15):
                        if qt == 0:
                            pe.wait_ge(s[f"q_in{hd % 4}"], 192 * it + 48 * (hd // 4) + 48)
                            if hd % 4 == 0:
                                pe.wait_ge(s[f"k_in{(hd // 4) % 2}"], 96 * it + 48 * (hd // 8) + 48)
                        row_scores(128 * it, LEAD_S + e, hd % 4, (hd // 4) % 2, qt)
                    if k == 5 and not (last_body and n + 2 > 15):
                        pe.wait_ge(s["ev_ok"], 64 * it + 4 * n + 8)
                        maxima_rows(16 * it + n + 3, 6 + (n + 1) % 2)

            pe_attention(0, False)
            with pe.Fori(1, 3) as it:
                pe_attention(it, False)
            pe_attention(3, True)

            pe.wait_ge(s["ev_ok"], 64 * 4 + 8)
            pe.wait_ge(s["snat_in"], 48)
            for m, nat in enumerate((snat_g, snat_u)):
                for g in range(KT):
                    TR(ps[:, 6, m * 224 + g * IT:m * 224 + (g + 1) * IT], nat[:, g, :], id32[0:IT, 0:IT])
            for o in range(FQ):
                last = TR(ps[:, 7, o * IT:(o + 1) * IT], snat_d[:, o * P:(o + 1) * P], id32[0:IT, 0:IT])
            last.then_inc(s["snat_pe"], 1)

            for i in range(FQ):
                pe.wait_ge(s["wosgn_ok"], i + 1)
                if i >= 2:
                    pe.wait_ge(s["woT_out"], i - 1)
                for t in range(KT):
                    last = TR(bank16(2 + i % 2)[:, t * P:(t + 1) * P], wosg[:, i % 2, t * P:(t + 1) * P], id16[:])
                last.then_inc(s["woT_pe"], 1)
            pe.wait_ge(s["woT_out"], FQ)
            for j in range(2):
                pe.wait_ge(s[f"ost_out{j}"], 16 * 9)

            def pe_oproj(ot, m0, b):
                for s2 in range(2):
                    pe.wait_ge(s["yo_ok"], m0 + s2 + 1)
                    pe.nop(nofuse=True)
                    for kt in range(KT):
                        for part in range(2):
                            last = MM(ps[:, s2, :], woT[:, kt, bass.ts(ot, P)],
                                      qz[:, 8 * b + kt, part, s2 * 512:(s2 + 1) * 512],
                                      start=(kt == 0 and part == 0), stop=(kt == KT - 1 and part == 1))
                    last.then_inc(s["o_pe"], 1)

            for b in range(2):
                with pe.Fori(0, FQ) as ot:
                    pe_oproj(ot, ot * 2 + 16 * b, b)

            def pe_ffn(kind, k, before):
                n0, a0, b0, _ = before
                every = BODY[kind][0]
                for i in range(0, len(every), NC):
                    r, t = every[i]["r"], every[i]["t"]
                    if r == 0:
                        pe.wait_ge(s["wgu_in0"], 16 * k + 16)
                    if r == 8:
                        pe.wait_ge(s["wd_in"], 16 * k)
                        pe.wait_ge(s["hl_ok"], 8 * k - 4)
                    if r == 16:
                        pe.wait_ge(s["wgu_in1"], 16 * k + 16)
                    for odd in range(2):
                        for c in range(NC):
                            q = every[i + c]
                            who, place = q["bank"]
                            if odd:
                                pe.wait_ge(s["dve_ok"], n0 + q["n"] + 1)
                                if r == 8:
                                    pe.wait_ge(s["hl_ok"], 8 * k - 3 + c)
                            elif who == "a":
                                pe.wait_ge(s["act_ok"], a0 + place + 5)
                            else:
                                pe.wait_ge(s["evb_ok"], b0 + place + 1)
                            for part in range(2):
                                if t[0] == "gu":
                                    g = 2 * t[3] + odd
                                    lhsT = wf[:, t[1], t[2], g * P:(g + 1) * P]
                                    rhs = xT[:, part, g, c * 512:(c + 1) * 512]
                                else:
                                    lhsT = wf[:, odd, 2, t[1] * P:(t[1] + 1) * P]
                                    rhs = hT[odd][:, c, part, :]
                                last = MM(ps[:, 4 * odd + c, :], lhsT, rhs, start=(part == 0), stop=(part == 1))
                            last.then_inc(s["odd_pe" if odd else "even_pe"], 1)

            pe.wait_ge(s["yo_ok"], 2 + 32)
            pe_ffn("first", 0, ZERO)
            with pe.Fori(1, PAIRS) as k:
                pe_ffn("full", k, counts_before(k))
            pe_ffn("last", PAIRS, counts_before(PAIRS))

            pe.wait_ge(s["dve_ok"], counts_before(PAIRS)[0] + BODY["last"][1][0] + 4)
            pe.wait_ge(s["pool_ok"], counts_before(PAIRS)[3] + BODY["last"][1][3])
            for i in range(NX):
                b, c0 = i // 8, (i % 8) * P
                if i >= 4:
                    pe.wait_ge(s["f_ok"], i - 3)
                for o in range(FQ):
                    last = TR(ps[:, 2 * (i % 4) + o // 4, (o % 4) * P:(o % 4 + 1) * P], acc[b][:, o, c0:c0 + P], id32[:])
                last.then_inc(s["t_pe"], 1)


_INS = ['L0_attn_hidden_states', 'L0_attn_q_weight', 'L0_attn_q_scale', 'L0_attn_k_weight', 'L0_attn_k_scale',
        'L0_attn_v_weight', 'L0_attn_v_scale', 'L0_attn_o_weight', 'L0_attn_o_scale',
        'L0_ffn_gate_w', 'L0_ffn_gate_z', 'L0_ffn_gate_s', 'L0_ffn_up_w', 'L0_ffn_up_z', 'L0_ffn_up_s',
        'L0_ffn_down_w', 'L0_ffn_down_z', 'L0_ffn_down_s']


def kernel(**inputs):
    import numpy as _np
    import concourse.bacc as _bacc
    from concourse import mybir as _mybir
    from concourse.bass_utils import run_bass_kernel_spmd as _run

    nc = _bacc.Bacc("TRN2", target_bir_lowering=False, num_devices=1)
    arrays, args = {}, []
    for name in _INS:
        a = _np.ascontiguousarray(inputs[name])
        arrays[f"in_{name}_dram"] = a
        args.append(nc.dram_tensor(f"in_{name}_dram", a.shape, _mybir.dt.from_np(a.dtype), kind="ExternalInput").ap())
    args.append(nc.dram_tensor("out_0_dram", (2, 1024, 1024), _mybir.dt.float32, kind="ExternalOutput").ap())
    args.append(nc.dram_tensor("zero_points", (28, 3, 1024), _mybir.dt.float16, kind="Internal").ap())
    args.append(nc.dram_tensor("dequantised", (28, 3, 128, 1024), _mybir.dt.float16, kind="Internal").ap())
    layer_kernel(nc, *args)
    r = _run(nc, [arrays], core_ids=[0])
    return r.results[0]["out_0_dram"]
```
